# Optimizing a Trainium2 kernel written in Bass

```python
import numpy as np
import jax
import jax.numpy as jnp

def _softmax(x, axis=-1):
    return jax.nn.softmax(x, axis=axis)

def _gelu(x):
    return jax.nn.gelu(x, approximate=True)

def _silu(x):
    return jax.nn.silu(x)

def _sigmoid(x):
    return jax.nn.sigmoid(x)

def _layernorm(x, axis=-1, eps=1e-05):
    m = jnp.mean(x, axis=axis, keepdims=True)
    v = jnp.var(x, axis=axis, keepdims=True)
    return (x - m) / jnp.sqrt(v + eps)

def _scatter_add(tgt, idx, src, axis=0):
    return tgt.at[idx].add(src)

def _segment_sum(src, seg, n):
    return jax.ops.segment_sum(src, seg, n)
kernel_name = 'mk_gps_d1_gnn_r8_599abf'

def setup_inputs(seed: int=0):
    np.random.seed(seed)
    _w = jnp.asarray

    def _rec_inputs():
        import jax
        import jax.numpy as jnp
        _gk = jax.random.key(seed)
        x = -0.0002117 + 1 * jax.random.normal(jax.random.fold_in(_gk, 1), (6250, 512), jnp.float32)
        src = jax.random.randint(jax.random.fold_in(_gk, 2), (100000,), 0, 6250, jnp.int32)
        dst = jax.random.randint(jax.random.fold_in(_gk, 3), (100000,), 0, 6250, jnp.int32)
        _o = jnp.argsort(dst, stable=True)
        src = src[_o]
        dst = dst[_o]
        return (x, src, dst)
    x, src, dst = _rec_inputs()

    def _L0_gnn_setup():
        import jax, jax.numpy as jnp
        import numpy as np
        N = 6250
        E = 100000
        F_IN = 512
        F_OUT = 512
        key = jax.random.key(seed)
        k_feat, k_src, k_dst, k_w1, k_b1, k_w2, k_b2 = jax.random.split(key, 7)
        feat = jax.random.normal(k_feat, (N, F_IN), dtype=jnp.float32)
        src_idx = jax.random.randint(k_src, (E,), 0, N, dtype=jnp.int32)
        dst_idx = jax.random.randint(k_dst, (E,), 0, N, dtype=jnp.int32)
        deg = jax.ops.segment_sum(jnp.ones((E,), jnp.float32), dst_idx, num_segments=N)
        in_deg = jnp.maximum(deg, 1.0)
        stdv = 1.0 / np.sqrt(F_IN)
        W1 = jax.random.uniform(k_w1, (F_OUT, F_IN), jnp.float32, -stdv, stdv)
        b1 = jax.random.uniform(k_b1, (F_OUT,), jnp.float32, -stdv, stdv)
        W2 = jax.random.uniform(k_w2, (F_OUT, F_IN), jnp.float32, -stdv, stdv)
        b2 = jax.random.uniform(k_b2, (F_OUT,), jnp.float32, -stdv, stdv)
        return {'feat': feat, 'src_idx': src_idx, 'dst_idx': dst_idx, 'in_deg': in_deg, 'W1': W1, 'b1': b1, 'W2': W2, 'b2': b2}
    _L0_gnn_all = _L0_gnn_setup()
    _L0_gnn_in = {k: v for k, v in _L0_gnn_all.items() if k in ('W1', 'b1', 'W2', 'b2')}
    del _L0_gnn_all

    def _L0_mix_setup():
        import jax, jax.numpy as jnp
        import numpy as np
        NUM_HEADS = 16
        EPS = 1e-15
        key = jax.random.key(seed)
        k1, k2, k3, k4 = jax.random.split(key, 4)
        B, N, C = (4, 2048, 512)
        x = jax.random.normal(k1, (B, N, C), dtype=jnp.float32)
        qkv_weight = jax.random.normal(k2, (3 * C, C), dtype=jnp.float32) * 0.02
        proj_weight = jax.random.normal(k3, (C, C), dtype=jnp.float32) * 0.02
        proj_bias = jax.random.normal(k4, (C,), dtype=jnp.float32) * 0.02
        return {'x': x, 'qkv_weight': qkv_weight, 'proj_weight': proj_weight, 'proj_bias': proj_bias}
    _L0_mix_all = _L0_mix_setup()
    _L0_mix_in = {k: v for k, v in _L0_mix_all.items() if k in ('qkv_weight', 'proj_weight', 'proj_bias')}
    del _L0_mix_all

    def _L0_ffn_setup():
        import jax, jax.numpy as jnp
        import numpy as np
        B, S, D = (32, 512, 512)
        E, H, O, K = (8, 256, 512, 2)
        key = jax.random.key(seed)
        ks = jax.random.split(key, 5)
        sc = lambda k, shape, scale: jax.random.normal(k, shape, jnp.float32) * scale
        return {'x': sc(ks[0], (B, S, D), 1.0), 'attn_w': sc(ks[1], (D, 1), 0.05), 'attn_b': jnp.zeros((1,), jnp.float32), 'gate_w': sc(ks[2], (D, E), 0.05), 'gate_b': jnp.zeros((E,), jnp.float32), 'w1': sc(ks[3], (E, D, H), 0.02), 'b1': jnp.zeros((E, H), jnp.float32), 'w2': sc(ks[4], (E, H, O), 0.02), 'b2': jnp.zeros((E, O), jnp.float32)}
    _L0_ffn_all = _L0_ffn_setup()
    _L0_ffn_in = {k: v for k, v in _L0_ffn_all.items() if k in ('attn_w', 'attn_b', 'gate_w', 'gate_b', 'w1', 'b1', 'w2', 'b2')}
    del _L0_ffn_all
    return {'x': x, 'src': src, 'dst': dst, 'L0_gnn_W1': _L0_gnn_in['W1'], 'L0_gnn_b1': _L0_gnn_in['b1'], 'L0_gnn_W2': _L0_gnn_in['W2'], 'L0_gnn_b2': _L0_gnn_in['b2'], 'L0_mix_qkv_weight': _L0_mix_in['qkv_weight'], 'L0_mix_proj_weight': _L0_mix_in['proj_weight'], 'L0_mix_proj_bias': _L0_mix_in['proj_bias'], 'L0_ffn_attn_w': _L0_ffn_in['attn_w'], 'L0_ffn_attn_b': _L0_ffn_in['attn_b'], 'L0_ffn_gate_w': _L0_ffn_in['gate_w'], 'L0_ffn_gate_b': _L0_ffn_in['gate_b'], 'L0_ffn_w1': _L0_ffn_in['w1'], 'L0_ffn_b1': _L0_ffn_in['b1'], 'L0_ffn_w2': _L0_ffn_in['w2'], 'L0_ffn_b2': _L0_ffn_in['b2']}

def reference(x, src, dst, L0_gnn_W1, L0_gnn_b1, L0_gnn_W2, L0_gnn_b2, L0_mix_qkv_weight, L0_mix_proj_weight, L0_mix_proj_bias, L0_ffn_attn_w, L0_ffn_attn_b, L0_ffn_gate_w, L0_ffn_gate_b, L0_ffn_w1, L0_ffn_b1, L0_ffn_w2, L0_ffn_b2):
    import jax
    import jax.numpy as jnp

    def _L0_gnn_ref(feat, src_idx, dst_idx, in_deg, W1, b1, W2, b2):
        import jax, jax.numpy as jnp
        import numpy as np
        N = 6250
        E = 100000
        F_IN = 512
        F_OUT = 512
        num_dst = in_deg.shape[0]
        agg = jax.ops.segment_sum(feat[src_idx], dst_idx, num_segments=num_dst)
        ah = agg / in_deg[:, None]
        out = jnp.einsum('nf,of->no', feat[:num_dst], W1) + b1 + jnp.einsum('nf,of->no', ah, W2) + b2
        return out

    def _L0_mix_ref(x, qkv_weight, proj_weight, proj_bias):
        import jax, jax.numpy as jnp
        import numpy as np
        NUM_HEADS = 16
        EPS = 1e-15
        B, N, C = x.shape
        H = NUM_HEADS
        D = C // H
        qkv = (x @ qkv_weight.T).reshape(B, N, 3, C)
        q = jax.nn.relu(qkv[:, :, 0]).reshape(B, N, H, D)
        k = jax.nn.relu(qkv[:, :, 1]).reshape(B, N, H, D)
        v = qkv[:, :, 2].reshape(B, N, H, D)
        qf = q.astype(jnp.float32)
        kf = k.astype(jnp.float32)
        vf = v.astype(jnp.float32)
        v_pad = jnp.concatenate([vf, jnp.ones_like(vf[..., :1])], axis=-1)
        vk = jnp.einsum('bnhc,bnhd->bhcd', v_pad, kf)
        vk_q = jnp.einsum('bnhd,bhcd->bnhc', qf, vk)
        proj_input = (vk_q[..., :-1] / (vk_q[..., -1:] + EPS)).astype(x.dtype).reshape(B, N, C)
        return proj_input @ proj_weight.T + proj_bias

    def _L0_ffn_ref(x, attn_w, attn_b, gate_w, gate_b, w1, b1, w2, b2):
        import jax, jax.numpy as jnp
        import numpy as np
        B, S, D = (32, 512, 512)
        E, H, O, K = (8, 256, 512, 2)
        scores = x @ attn_w + attn_b
        aw = jax.nn.softmax(scores, axis=1)
        pooled = jnp.sum(x * aw, axis=1)
        gates = jax.nn.softmax(pooled @ gate_w + gate_b, axis=-1)
        _, idx = jax.lax.top_k(gates, K)
        mask = jnp.sum(jax.nn.one_hot(idx, E, dtype=gates.dtype), axis=-2)
        g = gates * mask
        g = g / (jnp.sum(g, axis=-1, keepdims=True) + 1e-09)
        h = jax.nn.gelu(jnp.einsum('bsd,edh->ebsh', x, w1) + b1[:, None, None, :], approximate=False)
        eo = jax.nn.gelu(jnp.einsum('ebsh,eho->ebso', h, w2) + b2[:, None, None, :], approximate=False)
        return jnp.einsum('ebso,be->bso', eo, g)
    deg = jnp.maximum(jax.ops.segment_sum(jnp.ones(dst.shape, jnp.float32), dst, num_segments=6250), 1.0)
    xn = _layernorm(x, axis=-1)
    x = x + _L0_gnn_ref(xn, src, dst, deg, L0_gnn_W1, L0_gnn_b1, L0_gnn_W2, L0_gnn_b2) + _L0_mix_ref(xn[None], L0_mix_qkv_weight, L0_mix_proj_weight, L0_mix_proj_bias)[0]
    x = x + _L0_ffn_ref(_layernorm(x, axis=-1)[None], L0_ffn_attn_w, L0_ffn_attn_b, L0_ffn_gate_w, L0_ffn_gate_b, L0_ffn_w1, L0_ffn_b1, L0_ffn_w2, L0_ffn_b2)[0]
    return x

_drawn_inputs = setup_inputs


def setup_inputs(seed=0):
    import zlib

    import numpy as np

    out = dict(_drawn_inputs(seed))
    spreads = {'L0_ffn_gate_b': (0.0, 2.0), 'L0_ffn_b1': (0.0, 0.8), 'L0_ffn_b2': (0.0, 0.1)}
    factors = {'L0_mix_qkv_weight': 8.0,
     'L0_mix_proj_weight': 8.0,
     'L0_mix_proj_bias': 3.514,
     'L0_gnn_b1': 2.777,
     'L0_gnn_b2': 2.707}
    for name, (base, spread) in spreads.items():
        noise = np.random.default_rng([zlib.crc32(name.encode()), seed]).standard_normal(out[name].shape)
        drawn = base * np.exp(spread * noise) if base else spread * noise
        out[name] = jnp.asarray(drawn.astype(out[name].dtype))
    for name, factor in factors.items():
        out[name] = (out[name] * factor).astype(out[name].dtype)
    return out
```

```python
from contextlib import ExitStack

import numpy as np

import concourse.bass as bass
from concourse import mybir

F32, F16, I32, U32 = mybir.dt.float32, mybir.dt.float16, mybir.dt.int32, mybir.dt.uint32
ALU = mybir.AluOpType
ACT = mybir.ActivationFunctionType
AX = mybir.AxisListType
RMAX = bass.bass_isa.ReduceOp.max

P = 128
N, D, E = 6250, 512, 100000
HEAD = 32
NE, H = 8, 256
C = D // P
HC = H // P
T = (N + P - 1) // P
TAIL = N - (T - 1) * P
ROWS = T * P
BLOCKS = (E + P - 1) // P
R = 16
COLS = (BLOCKS + 2 + R - 1) // R * R
ROUNDS = COLS // R
U = 4
RG = R // U
OG = 8
GROUPS = COLS // U
CH = (BLOCKS + P - 1) // P
FULL = BLOCKS // P
XN = 5
XI = 3
G4 = 4
NG = T // G4
EPS_LN = 1e-5
EPS_ATT = 1e-15
EPS_GATE = 1e-9
SX = 2.0 ** 10
SW = 2.0 ** 14
SK = 2.0 ** -19
SP_ = 2.0 ** 14
LOW = -1e30

K_, Q_, W_, M_, W1_, HB_, W2_ = range(7)


def real(t):
    return not isinstance(t, int) or 0 <= t < T


def after(eng, sem, count):
    if not isinstance(count, int) or count > 0:
        eng.wait_ge(sem, count)


def pipeline(eng, body, first, lo, hi, last):
    for i in range(first, lo):
        body(i)
    with eng.Fori(lo, hi) as i:
        body(i)
    for i in range(hi, last):
        body(i)


def program(nc, x, src, dst, gw1, gb1, gw2, gb2, qkv_w, proj_w, proj_b, attn_w, attn_b, gate_w, gate_b,
            w1, b1, w2, b2, out):
    ctx = ExitStack()
    with ctx:
        def sb(name, shape, dt):
            return ctx.enter_context(nc.sbuf_tensor(name, shape, dt))

        table = nc.dram_tensor("table", (N, 2 * D), F16, kind="Internal").ap()
        x2_dram = nc.dram_tensor("x2_rows", (ROWS, D), F32, kind="Internal").ap()

        xT = sb("xT", [P, 2 * C, ROWS], F16)
        flat = xT[:, :, :].rearrange("p a n -> p (a n)").bitcast(F32)
        raw_w = [flat[:, k * C * D:(k + 1) * C * D].rearrange("p (a f) -> p a f", a=C) for k in range(6)]
        o = 6 * C * D
        raw_src = flat[:, o:o + CH * P].bitcast(I32).rearrange("p (a f) -> p a f", a=CH)
        o += CH * P
        raw_dst = flat[:, o:o + CH * P].bitcast(I32).rearrange("p (a f) -> p a f", a=CH)
        o += CH * P
        f_src = flat[:, o:o + CH * P].rearrange("p (a f) -> p a f", a=CH)
        o += CH * P
        f_dst = flat[:, o:o + CH * P].rearrange("p (a f) -> p a f", a=CH)
        o += CH * P
        f_pad = flat[:, o:o + CH * P].rearrange("p (a f) -> p a f", a=CH)
        o += CH * P
        below = flat[:, o:o + CH * (T + 1)].rearrange("p (a f) -> p a f", a=CH)
        o += CH * (T + 1)
        viol = flat[:, o:o + CH * (T + 1)].rearrange("p (a f) -> p a f", a=CH)
        o += CH * (T + 1)
        viol2 = flat[:, o:o + CH * (T + 1)].rearrange("p (a f) -> p a f", a=CH)

        wts = sb("wts", [P, 4, 2, C, D], F16)
        wk, wq, wg1, wg2 = (wts[:, k] for k in range(4))
        wm = wk
        w1raw = wts[:, 0].rearrange("p a c f -> p (a c f)").bitcast(F32).rearrange("p (e c h) -> p e c h", e=2, c=C)
        w2raw = wts[:, 1].rearrange("p a c f -> p (a c f)").bitcast(F32).rearrange("p (e c o) -> p e c o", e=2, c=HC)
        w1s = wts[:, 2].rearrange("p a c f -> p a (c f)").rearrange("p a (e c h) -> p a e c h", e=2, c=C)
        w2s = wts[:, 3].rearrange("p a c f -> p a (c f)").rearrange("p a (e c o) -> p a e c o", e=2, c=HC)

        ring = sb("ring", [P, R, 2 * D], F16)
        ring32 = ring[:, :, :].rearrange("p a f -> p (a f)").bitcast(F32).rearrange("p (a f) -> p a f", f=D)
        xnhl = ring[:, 0:XN, :]
        xin = ring32[:, XN:XN + XI, :]
        xn32 = ring32[:, XN + XI:XN + XI + 2, :]
        k32 = ring32[:, XN + XI + 2, :]
        khl = ring[:, XN + XI + 3:XN + XI + 5, :]
        x2g = ring32[:, 0:2 * G4, :].rearrange("p (b j) f -> p b j f", b=2)
        hT = ring[:, 2 * G4:4 * G4, :].rearrange("p a f -> p (a f)").rearrange(
            "p (b a e c n) -> p b a e c n", b=2, a=2, e=2, c=HC)

        onehot = sb("onehot", [P, OG * U, P], F16)
        oh32 = onehot[:, :, :].rearrange("p a f -> p (a f)").bitcast(F32)
        gt32 = oh32.rearrange("p (a f) -> p a f", a=C)
        g32 = gt32
        plb = oh32[:, 0:C * P].rearrange("p (a f) -> p a f", a=C)

        work = sb("work", [P, 10, D], F32)
        wvT, m32, pT32 = work[:, 0:4], work[:, 0:4], work[:, 4:8]
        vtm = work[:, 8].rearrange("p (a f) -> p a f", a=C)
        kacc = work[:, 9]
        x_in, xb, x2, xn2, acc, accs, w32, ah32 = (work[:, k] for k in range(8))
        ahT, pT = (work[:, k].bitcast(F16).rearrange("p (a c n) -> p a c n", a=2, c=C) for k in (8, 9))
        pre = work[:, 0:4].rearrange("p (b e) f -> p b e f", b=2)
        act2 = work[:, 4:8].rearrange("p (b e) f -> p b e f", b=2)
        b2b = work[:, 8:10]

        src_col = sb("src_col", [P, COLS], I32)
        dst_col = sb("dst_col", [P, COLS], F32)
        biasb = sb("biasb", [P, D], F32)
        awb = sb("awb", [P, D], F32)
        bias3 = ring32[:, 15:16, :]
        bias2 = ring32[:, 14:15, :]

        ident = sb("ident", [P, P], F32)
        ident16 = sb("ident16", [P, P], F16)
        ones = sb("ones", [P, P], F32)
        hmask = sb("hmask", [P, P], F32)
        iota_t = hmask
        zero16 = sb("zero16", [P, P], F16)
        one16 = sb("one16", [P, 1], F16)
        iota16 = sb("iota16", [P, P], F16)
        tile_base = sb("tile_base", [P, T + 1], F32)
        firsts = sb("firsts", [P, T + 1], F32)
        uns = sb("uns", [P, T + 1], F32)
        first_i = sb("first_i", [P, T + 2], I32)
        upper = sb("upper", [P, T + 1], I32)
        lower = sb("lower", [P, T + 1], I32)
        colidx = sb("colidx", [P, CH], F32)
        colmax = sb("colmax", [P, CH], F32)
        colmin = sb("colmin", [P, CH], F32)
        colok = sb("colok", [P, CH], F32)
        vsum = sb("vsum", [P, 4], F32)
        rowi = sb("rowi", [P, 1], F32)
        rowmask = sb("rowmask", [P, 1], F32)
        rowlow = sb("rowlow", [P, 1], F32)
        idx_slots = sb("idx_slots", [P, R], I32)
        epsc = sb("epsc", [P, 1], F32)
        amax = sb("amax", [P, 8], F32)
        gmax = sb("gmax", [P, 8], F32)
        pow2 = sb("pow2", [P, 8], F32)
        scale = sb("scale", [P, 8], F32)
        undo = sb("undo", [P, 8], F32)
        mix = sb("mix", [P, 8], F32)
        st6 = sb("st6", [P, 6], F32)
        mv = sb("mv", [P, 2], F32)
        std = sb("std", [P, 1], F32)
        rs0 = sb("rs0", [P, 1], F32)
        rstd = sb("rstd", [P, 1], F32)
        kinv = sb("kinv", [P, C], F32)
        ksb = sb("ksb", [P, D], F32)
        den = sb("den", [P, D // HEAD], F32)
        den2 = sb("den2", [P, D // HEAD], F32)
        dg = sb("dg", [P, 1], F32)
        rd = sb("rd", [P, 1], F32)
        sraw = sb("sraw", [P, 1], F32)
        sm = sb("sm", [P, 2], F32)
        negm = sb("negm", [P, 1], F32)
        e2 = sb("e2", [P, 2], F32)
        lsum = sb("lsum", [P, 1], F32)
        wp = sb("wp", [P, 1], F32)
        lw = sb("lw", [P, 1], F32)
        gst = sb("gst", [P, 8], F32)
        abb = sb("abb", [P, 1], F32)
        gwt = sb("gwt", [P, C, NE], F32)
        gbb = sb("gbb", [P, NE], F32)
        pld = sb("pld", [P, 8], F32)
        lg = sb("lg", [P, NE], F32)
        gts = sb("gts", [P, NE], F32)
        top = sb("top", [P, 8], F32)
        topi = sb("topi", [P, 8], U32)
        gexp = sb("gexp", [P, 2], F32)
        b1t = sb("b1t", [P, 2, HC], F32)

        bank = [ctx.enter_context(nc.psum_tensor(f"bank{k}", [P, D], F32)) for k in range(8)]
        ps_q, ps_o, ps_b, ps_agg, ps_deg, ps_ta, ps_tp, ps_tx = bank
        ps_t = [bank[b][:, :].bitcast(F16).rearrange("p (q n) -> p q n", q=2 * C)[:, 0:C, :] for b in (4, 6)]
        ps_k = bank[5]

        names = """consts dve_chain act_chain pool_chain
            edges_loaded biases_loaded small_loaded floats_made turned_edges turned_taken below_made below_summed
            viol_made viol_summed firsts_made cols_made
            amax_made gmax_made scales_made w_turned w_hi_made w_lo_made
            x_loaded stats_made mv_made std_made rs_made rstd_made xn_made hi_made lo_made table_stored
            t_made t_hi_taken t_lo_taken k_made k32_made khi_made klo_made kacc_made g_made
            ksum_made gt_hi_copied gt_lo_copied vt_made vtm_made m_made m32_made mmax_made mgmax_made mscale_made
            mhi_made mlo_made p2_ready
            arrived released iota_made oh_made oh_used q_made w_made den_made den2_made rec_made p_made turned_ah turned_p
            turned_x2 agg_made dg_made rd_made ah_made ahT_hi ahT_lo pT_hi pT_lo lin_made xa_made x2_made x2_stored
            st2_made mv2_made std2_made rs2_made rstd2_made xn2_made sraw_made sc_made negm_made exp_made
            m_kept l_made accs_made acc_made x2T_hi x2T_lo xb_made x_loaded2
            best_made wp_made lw_made pooled_made plb_made logits_made lg_made gexp_made chosen
            e_amax_made e_gmax_made e_scales w1_hi w1_lo w2_hi w2_lo b_loaded
            z_made g32_made h_hi h_lo eo_made pre_made act_made y_made y_half x2g_loaded out_stored turn pool_turn""".split()
        s = {n: ctx.enter_context(nc.semaphore(n)) for n in names}
        w_loaded = [ctx.enter_context(nc.semaphore(f"w_loaded{k}")) for k in range(6)]
        e_loaded = [ctx.enter_context(nc.semaphore(f"e_loaded{k}")) for k in range(4)]
        slot_loaded = [ctx.enter_context(nc.semaphore(f"slot_loaded{k}")) for k in range(R)]
        block = ctx.enter_context(nc.Block())

        NCONST = 15
        SPLIT = 4 * C

        def cols(t, w=P):
            return bass.ds(t * P, w)

        def one(a, k):
            return a[:, bass.ds(k, 1), :].rearrange("p a f -> p (a f)")

        def bcast(v, n):
            return v.rearrange("(a n) -> a n", a=1).to_broadcast([P, n])

        @block.sync
        def _(sp):
            sp.wait_ge(s["consts"], NCONST)
            for raw, dr in ((raw_src, src), (raw_dst, dst)):
                sp.dma_start(raw[:, 0:FULL, :],
                             dr[0:FULL * P * P].rearrange("(k p e) -> p k e", p=P, e=P)).then_inc(s["edges_loaded"], 16)
                o, last = FULL * P * P, BLOCKS - FULL * P - 1
                sp.dma_start(raw[0:last, FULL, :],
                             dr[o:o + last * P].rearrange("(p e) -> p e", e=P)).then_inc(s["edges_loaded"], 16)
                o += last * P
                sp.dma_start(raw[last:last + 1, FULL, 0:E - o],
                             dr[o:E].rearrange("(p e) -> p e", p=1)).then_inc(s["edges_loaded"], 16)
            for k, w in enumerate((qkv_w[D:2 * D], qkv_w[0:D], gw1, gw2, qkv_w[2 * D:3 * D], proj_w)):
                sp.dma_start(raw_w[k], w.rearrange("(a p) f -> p a f", p=P)).then_inc(w_loaded[k], 16)

            def rows(i):
                if real(i):
                    after(sp, s["xn_made"], i - XI + 1)
                    sp.sem_inc(s["turn"], 1)
                    after(sp, s["x_loaded"], 16 * i)
                    n = TAIL if isinstance(i, int) and i == T - 1 else P
                    sp.dma_start(xin[0:n, bass.ds(i % XI, 1), :].rearrange("p a f -> p (a f)"),
                                 x[bass.ds(i * P, n), :]).then_inc(s["x_loaded"], 16)
                t = i - 5
                if real(t):
                    n = TAIL if isinstance(t, int) and t == T - 1 else P
                    after(sp, s["hi_made"], t + 1)
                    after(sp, s["lo_made"], t + 1)
                    after(sp, s["table_stored"], 16 * t)
                    sp.dma_start(table[bass.ds(t * P, n), :],
                                 xnhl[0:n, bass.ds(t % XN, 1), :].rearrange("p a f -> p (a f)")
                                 ).then_inc(s["table_stored"], 16)
            pipeline(sp, rows, 0, 6, T - 1, T + 5)

            sp.wait_ge(s["firsts_made"], 1)
            passes = sp.value_load(first_i[0:1, T + 1:T + 2], min_val=1, max_val=T)
            with sp.Fori(0, passes) as a:
                with sp.Fori(0, ROUNDS) as g:
                    for k in range(R):
                        sp.wait_ge(slot_loaded[k], (a * ROUNDS + g) * 16 + 16)
                        if k % U == U - 1:
                            sp.sem_inc(s["arrived"], 1)

            sp.wait_ge(s["chosen"], 1)
            for e in range(2):
                v = sp.value_load(topi[0:1, e:e + 1], min_val=0, max_val=NE - 1)
                sp.dma_start(w1raw[:, e], w1[bass.ds(v, 1), :, :].rearrange("a (c p) h -> p (a c) h", p=P)
                             ).then_inc(e_loaded[e], 16)
                sp.dma_start(w2raw[:, e], w2[bass.ds(v, 1), :, :].rearrange("a (c p) o -> p (a c) o", p=P)
                             ).then_inc(e_loaded[2 + e], 16)
                with nc.allow_non_contiguous_dma(reason="a bias per partition, 1 KB in all"):
                    sp.dma_start(b1t[:, e], b1[bass.ds(v, 1), :].rearrange("a (c p) -> p (a c)", p=P)
                                 ).then_inc(s["b_loaded"], 16)
                sp.dma_start(b2b[:, e], b2[bass.ds(v, 1), :].to_broadcast([P, D])).then_inc(s["b_loaded"], 16)

            def group(g):
                whole = not isinstance(g, int) or g < NG
                j = G4 if whole else 1
                after(sp, s["out_stored"], 16 * (g - 1))
                sp.sem_inc(s["turn"], 1)
                after(sp, s["x2g_loaded"], 16 * g)
                sp.dma_start(x2g[:, bass.ds(g % 2, 1), 0:j, :].rearrange("p a j f -> p (a j) f"),
                             x2_dram[bass.ds(g * G4 * P, j * P), :].rearrange("(j p) f -> p j f", p=P)
                             ).then_inc(s["x2g_loaded"], 16)

            def store(g):
                after(sp, s["y_made"], G4 * g + G4)
                sp.dma_start(out[bass.ds(g * G4 * P, G4 * P), :].rearrange("(j p) f -> p j f", p=P),
                             x2g[:, bass.ds(g % 2, 1), :, :].rearrange("p a j f -> p (a j) f")
                             ).then_inc(s["out_stored"], 16)
            sp.wait_ge(s["x2_stored"], 16 * T)
            group(0)
            group(1)
            store(0)
            with sp.Fori(2, NG) as g:
                group(g)
                store(g - 1)
            group(NG)
            store(NG - 1)
            sp.wait_ge(s["y_made"], T)
            body = TAIL // 16 * 16
            sp.dma_start(out[(T - 1) * P:(T - 1) * P + body, :], x2g[0:body, NG % 2, 0, :]).then_inc(s["out_stored"], 16)
            sp.dma_start(out[(T - 1) * P + body:N, :], x2g[body:TAIL, NG % 2, 0, :]).then_inc(s["out_stored"], 16)
            sp.wait_ge(s["out_stored"], 16 * (NG + 2))

        @block.gpsimd
        def _(pool):
            made = [0]

            def link(ins):
                made[0] += 1
                ins.then_inc(s["pool_chain"], 1)
                pool.wait_ge(s["pool_chain"], made[0])

            imp = dict(allow_small_or_imprecise_dtypes=True)
            link(pool.memset(raw_dst[:, FULL, :], -1))
            link(pool.memset(raw_src[:, FULL, :], 0))
            link(pool.memset(ident[:], 0.0))
            link(pool.affine_select(out=ident[:], in_=ident[:], compare_op=ALU.not_equal, fill=1.0, base=0,
                                    pattern=[[-1, P]], channel_multiplier=1))
            link(pool.tensor_copy(ident16[:], ident[:]))
            link(pool.memset(hmask[:], 1.0))
            hm = hmask[:, :].rearrange("p (a c) -> p a c", c=HEAD)
            link(pool.affine_select(out=hm, in_=hm, compare_op=ALU.is_ge, fill=0.0, base=0,
                                    pattern=[[-HEAD, P // HEAD], [0, HEAD]], channel_multiplier=1))
            link(pool.affine_select(out=hm, in_=hm, compare_op=ALU.is_ge, fill=0.0, base=HEAD - 1,
                                    pattern=[[HEAD, P // HEAD], [0, HEAD]], channel_multiplier=-1))
            pool.memset(ones[:], 1.0).then_inc(s["consts"], 1)
            pool.memset(zero16[:], 0.0).then_inc(s["consts"], 1)
            pool.memset(one16[:], 1.0).then_inc(s["consts"], 1)
            pool.memset(epsc[:], EPS_LN / (SX * SX)).then_inc(s["consts"], 1)
            pool.memset(kacc, 0.0).then_inc(s["consts"], 1)
            pool.iota(iota16[:], pattern=[[1, P]], base=0, channel_multiplier=0, **imp).then_inc(s["consts"], 1)
            pool.iota(tile_base[:], pattern=[[P, T + 1]], base=0, channel_multiplier=0, **imp).then_inc(s["consts"], 1)
            pool.iota(uns[:], pattern=[[COLS, T + 1]], base=0, channel_multiplier=0, **imp).then_inc(s["consts"], 1)
            pool.iota(colidx[:], pattern=[[P, CH]], base=1, channel_multiplier=1, **imp).then_inc(s["consts"], 1)
            pool.iota(rowi[:], pattern=[[0, 1]], base=0, channel_multiplier=1, **imp).then_inc(s["consts"], 1)
            pool.memset(src_col[:], 0).then_inc(s["consts"], 1)
            pool.memset(dst_col[:], -1.0).then_inc(s["consts"], 1)
            pool.memset(sm[:, :], LOW).then_inc(s["consts"], 1)
            pool.memset(lsum[:], 0.0).then_inc(s["consts"], 1)
            pool.memset(amax[:], 0.0).then_inc(s["consts"], 1)

            pool.wait_ge(s["amax_made"], 1)
            pool.partition_all_reduce(gmax[:, 0:3], amax[:, 0:3], P, RMAX).then_inc(s["gmax_made"], 1)

            def keys(i):
                if real(i):
                    pool.wait_ge(s["khi_made"], i + 1)
                    pool.tensor_tensor(out=one(khl, i % 2)[:, D:2 * D], in0=k32, in1=one(khl, i % 2)[:, 0:D],
                                       op=ALU.subtract).then_inc(s["klo_made"], 1)
                    after(pool, s["kacc_made"], i)
                    pool.tensor_tensor(out=kacc, in0=kacc, in1=k32, op=ALU.add).then_inc(s["kacc_made"], 1)
            pipeline(pool, keys, 0, 1, T, T)

            pool.wait_ge(s["mmax_made"], 1)
            pool.partition_all_reduce(gmax[:, 3:4], amax[:, 3:4], P, RMAX).then_inc(s["mgmax_made"], 1)

            pool.wait_ge(s["firsts_made"], 1)
            pool.wait_ge(s["cols_made"], 1)
            pool.wait_ge(s["table_stored"], 16 * T)
            pool.wait_ge(s["g_made"], T)
            passes = pool.value_load(first_i[0:1, T + 1:T + 2], min_val=1, max_val=T)
            with pool.Fori(0, passes) as a:
                with pool.Fori(0, ROUNDS) as g:
                    it = a * ROUNDS + g
                    for k in range(0, R, U):
                        pool.wait_ge(s["released"], it * RG + k // U + 1)
                        pool.tensor_copy(idx_slots[:, k:k + U], src_col[:, bass.ds(g * R + k, U)]
                                         ).then_inc(s["pool_turn"], 1)
                        pool.wait_ge(s["pool_turn"], it * RG + k // U + 1)
                        pool.sem_inc(s["turn"], 1)
                        for n in range(k, k + U):
                            pool.indirect_dma_start(
                                ring[:, n, :], None, table[:, :],
                                bass.IndirectOffsetOnAxis(ap=idx_slots[:, n:n + 1], axis=0)
                            ).then_inc(slot_loaded[n], 16)

            pool.wait_ge(s["acc_made"], T)
            pool.wait_ge(s["m_kept"], T)
            pool.partition_all_reduce(gst[:, 0:1], sm[:, 0:1], P, RMAX).then_inc(s["best_made"], 1)
            pool.wait_ge(s["e_amax_made"], 1)
            pool.partition_all_reduce(gmax[:, 4:7], amax[:, 4:7], P, RMAX).then_inc(s["e_gmax_made"], 1)

        @block.tensor
        def _(pe):
            mm = nc.tensor.matmul

            def three(out_, wh, wl, mh, ml, n, first=True, last=True):
                for c in range(n):
                    mm(out_, wh(c), mh(c), start=first and c == 0, stop=False)
                    mm(out_, wh(c), ml(c), start=False, stop=False)
                for c in range(n):
                    r = mm(out_, wl(c), mh(c), start=False, stop=last and c == n - 1)
                return r

            pe.wait_ge(s["consts"], NCONST)
            pe.wait_ge(s["floats_made"], 1)
            n = 0
            for f in (f_src, f_dst):
                for k in range(CH):
                    after(pe, s["turned_taken"], n - 1)
                    nc.tensor.transpose(bank[6 + n % 2][:, 0:P], f[:, k, :], ident[:]).then_inc(s["turned_edges"], 1)
                    n += 1
            pe.wait_ge(s["below_made"], 1)
            for k in range(CH):
                r = mm(bank[5][:, 0:T + 1], ones[:], below[:, k, :], start=(k == 0), stop=(k == CH - 1))
            r.then_inc(s["below_summed"], 1)
            pe.wait_ge(s["viol_made"], 1)
            mm(bank[4][:, 0:2], ones[:], vsum[:, 0:2], start=True, stop=True).then_inc(s["viol_summed"], 1)
            n = 0
            for k in range(6):
                pe.wait_ge(w_loaded[k], 16)
                for c in range(C):
                    after(pe, s["w_hi_made"], n - 3)
                    after(pe, s["w_lo_made"], min(n - 3, SPLIT))
                    for a in range(C):
                        r = nc.tensor.transpose(bank[n % 4][:, a * P:(a + 1) * P],
                                                raw_w[k][:, a, c * P:(c + 1) * P], ident[:])
                    r.then_inc(s["w_turned"], 1)
                    n += 1
            pe.wait_ge(s["w_hi_made"], 6 * C)
            pe.wait_ge(s["w_lo_made"], SPLIT)

            def keys(i):
                t = i + 1
                if real(t):
                    after(pe, s["lo_made"], t + 1)
                    after(pe, s["t_hi_taken"], t)
                    after(pe, s["t_lo_taken"], t)
                    for q in range(2 * C):
                        r = nc.tensor.transpose(ps_t[q // C][:, q % C, :], one(xnhl, t % XN)[:, q * P:(q + 1) * P], ident16[:])
                    r.then_inc(s["t_made"], 1)
                t = i
                if real(t):
                    after(pe, s["t_hi_taken"], t + 1)
                    after(pe, s["t_lo_taken"], t + 1)
                    after(pe, s["k32_made"], t)
                    three(ps_k[:, :], lambda c: xT[:, c, cols(t)], lambda c: xT[:, C + c, cols(t)],
                          lambda c: wk[:, 0, c, :], lambda c: wk[:, 1, c, :], C).then_inc(s["k_made"], 1)
                t = i - 1
                if real(t):
                    pe.wait_ge(s["klo_made"], t + 1)
                    kh, kl, xs = one(khl, t % 2)[:, 0:D], one(khl, t % 2)[:, D:2 * D], one(xnhl, t % XN)
                    st, en = (isinstance(t, int) and t == 0), (isinstance(t, int) and t == T - 1)
                    for c in range(C):
                        mm(bank[c][:, :], xs[:, c * P:(c + 1) * P], kh, start=st, stop=False)
                        mm(bank[c][:, :], xs[:, c * P:(c + 1) * P], kl, start=False, stop=False)
                        r = mm(bank[c][:, :], xs[:, D + c * P:D + (c + 1) * P], kh, start=False, stop=en)
                    r.then_inc(s["g_made"], 1)
            pipeline(pe, keys, -1, 2, T - 4, T + 1)

            pe.wait_ge(s["kacc_made"], T)
            for c in range(C):
                mm(bank[6][:, c:c + 1], kacc[:, c * P:(c + 1) * P], ones[:, 0:1], start=True, stop=True)
            mm(bank[7][:, :], ones[:], kacc, start=True, stop=True).then_inc(s["ksum_made"], 1)
            pe.wait_ge(s["gt_hi_copied"], 2)
            pe.wait_ge(s["gt_lo_copied"], 2)
            for j in range(C):
                for c in range(C):
                    r = mm(bank[4][:, j * P:(j + 1) * P], wvT[:, c, j * P:(j + 1) * P], gt32[:, c, j * P:(j + 1) * P],
                           start=(c == 0), stop=(c == C - 1))
            r.then_inc(s["vt_made"], 1)
            pe.wait_ge(s["vtm_made"], 1)
            for j in range(C):
                mm(bank[j][:, :], vtm[:, j, :], pT32[:, j, :], start=True, stop=True).then_inc(s["m_made"], 1)
            pe.sem_inc(s["released"], RG)
            pe.sem_inc(s["oh_used"], OG)

            agg3 = ps_agg[:, :].rearrange("p (c n) -> p c n", c=C)

            def consume(q, t, skip_lower=None, skip_upper=None):
                pe.wait_ge(s["arrived"], q + 1)
                pe.wait_ge(s["oh_made"], q + t + 1)
                w = onehot[:, bass.ds((q + t) % OG * U, U), :]
                rows = ring[:, bass.ds(q % RG * U, U), :]

                def half(k0):
                    for k in range(k0, k0 + U // 2):
                        mm(ps_agg[:, :], w[:, k, :], rows[:, k, 0:D], start=False, stop=False, skip_group_check=True)
                        r = mm(ps_agg[:, :], w[:, k, :], rows[:, k, D:2 * D], start=False, stop=False,
                               skip_group_check=True)
                        d = mm(ps_deg[:, 0:1], w[:, k, :], one16[:], start=False, stop=False, skip_group_check=True)
                    return r, d
                if skip_upper is not None:
                    with pe.If(skip_upper < 1):
                        half(U // 2)
                    half(0)[1].then_inc(s["oh_used"], 1)
                    return
                if skip_lower is None:
                    half(0)
                else:
                    with pe.If(skip_lower < 1):
                        half(0)
                r, d = half(U // 2)
                r.then_inc(s["released"], 1)
                d.then_inc(s["oh_used"], 1)

            def layer(i):
                t = i
                if real(t):
                    if isinstance(t, int) and t == 0:
                        pe.wait_ge(s["p2_ready"], 1)
                    after(pe, s["w_made"], t)
                    three(ps_q[:, :], lambda c: xT[:, c, cols(t)], lambda c: xT[:, C + c, cols(t)],
                          lambda c: wq[:, 0, c, :], lambda c: wq[:, 1, c, :], C).then_inc(s["q_made"], 1)
                t = i - 1
                if real(t):
                    after(pe, s["ah_made"], t + 1)
                    after(pe, s["ahT_lo"], t)
                    for c in range(C):
                        r = nc.tensor.transpose(ps_ta[:, c * P:(c + 1) * P], ah32[:, c * P:(c + 1) * P], ident[:])
                    r.then_inc(s["turned_ah"], 1)
                    after(pe, s["p_made"], t + 1)
                    after(pe, s["pT_lo"], t)
                    for c in range(C):
                        r = nc.tensor.transpose(ps_tp[:, c * P:(c + 1) * P], w32[:, c * P:(c + 1) * P], ident[:])
                    r.then_inc(s["turned_p"], 1)
                t = i
                if real(t):
                    a = pe.value_load(first_i[0:1, bass.ds(t, 1)], min_val=0, max_val=GROUPS * T)
                    b = pe.value_load(first_i[0:1, bass.ds(t + 1, 1)], min_val=0, max_val=GROUPS * T)
                    after(pe, s["ah_made"], t)
                    after(pe, s["dg_made"], t)
                    mm(agg3, zero16[:], zero16[:, None, :].to_broadcast([P, C, P]), start=True, stop=False, skip_group_check=True)
                    mm(ps_deg[:, 0:1], zero16[:], one16[:], start=True, stop=False, skip_group_check=True)
                    in_upper = pe.value_load(upper[0:1, bass.ds(t, 1)], min_val=0, max_val=1)
                    in_lower = pe.value_load(lower[0:1, bass.ds(t + 1, 1)], min_val=0, max_val=1)
                    with pe.If(a < b):
                        consume(a, t, skip_lower=in_upper)
                        with pe.If(a + 1 < b):
                            with pe.Fori(a + 1, b) as q:
                                consume(q, t)
                t = i - 1
                if real(t):
                    after(pe, s["x2_made"], t)
                    three(ps_o[:, :], lambda c: xT[:, c, cols(t)], lambda c: xT[:, C + c, cols(t)],
                          lambda c: wg1[:, 0, c, :], lambda c: wg1[:, 1, c, :], C, last=False)
                t = i
                if real(t):
                    consume(b, t, skip_upper=in_lower)
                    mm(agg3, zero16[:], zero16[:, None, :].to_broadcast([P, C, P]), start=False, stop=True, skip_group_check=True)
                    mm(ps_deg[:, 0:1], zero16[:], one16[:], start=False, stop=True, skip_group_check=True
                       ).then_inc(s["agg_made"], 1)
                t = i - 1
                if real(t):
                    after(pe, s["ahT_lo"], t + 1)
                    three(ps_o[:, :], lambda c: ahT[:, 0, c, :], lambda c: ahT[:, 1, c, :],
                          lambda c: wg2[:, 0, c, :], lambda c: wg2[:, 1, c, :], C, first=False)
                    after(pe, s["pT_lo"], t + 1)
                    three(ps_b[:, :], lambda c: pT[:, 0, c, :], lambda c: pT[:, 1, c, :],
                          lambda c: wm[:, 0, c, :], lambda c: wm[:, 1, c, :], C).then_inc(s["lin_made"], 1)
                t = i - 2
                if real(t):
                    after(pe, s["xn2_made"], t + 1)
                    after(pe, s["x2T_lo"], t)
                    for c in range(C):
                        r = nc.tensor.transpose(ps_tx[:, c * P:(c + 1) * P], xn2[:, c * P:(c + 1) * P], ident[:])
                    r.then_inc(s["turned_x2"], 1)
            pipeline(pe, layer, 0, 3, T, T + 2)

            pe.wait_ge(s["wp_made"], 1)
            pe.wait_ge(s["lw_made"], 1)
            for c in range(C):
                mm(bank[0][:, c:c + 1], acc[:, c * P:(c + 1) * P], wp[:], start=True, stop=True)
            mm(bank[0][:, C:C + 1], ones[:], lw[:], start=True, stop=True).then_inc(s["pooled_made"], 1)
            pe.wait_ge(s["plb_made"], 1)
            for c in range(C):
                r = mm(bank[1][:, 0:NE], plb[:, c, :], gwt[:, c, :], start=(c == 0), stop=(c == C - 1))
            r.then_inc(s["logits_made"], 1)

            pe.wait_ge(s["w1_hi"], 1)
            pe.wait_ge(s["w1_lo"], 1)
            pe.wait_ge(s["w2_hi"], 1)
            pe.wait_ge(s["w2_lo"], 1)
            pe.wait_ge(s["x2T_lo"], T)

            def hidden(g, n):
                for b in range(2 * HC):
                    e, hc = b // HC, b % HC
                    after(pe, s["g32_made"], 2 * HC * g - 2 * HC + b + 1)
                    three(bank[b][:, 0:n], lambda c: w1s[:, 0, e, c, hc * P:(hc + 1) * P],
                          lambda c: w1s[:, 1, e, c, hc * P:(hc + 1) * P],
                          lambda c: xT[:, c, bass.ds(g * G4 * P, n)],
                          lambda c: xT[:, C + c, bass.ds(g * G4 * P, n)], C).then_inc(s["z_made"], 1)

            def outs(g, tiles):
                after(pe, s["h_lo"], 2 * HC * g + 2 * HC)
                for j in range(tiles):
                    for e in range(2):
                        after(pe, s["pre_made"], 2 * (G4 * g + j) - 4 + e + 1)
                        hh = hT[:, bass.ds(g % 2, 1)].rearrange("p b a e c n -> p (b a) e c n")
                        three(bank[4 + 2 * (j % 2) + e][:, :],
                              lambda c: hh[:, 0, e, c, j * P:(j + 1) * P], lambda c: hh[:, 1, e, c, j * P:(j + 1) * P],
                              lambda c: w2s[:, 0, e, c, :], lambda c: w2s[:, 1, e, c, :], HC).then_inc(s["eo_made"], 1)
            hidden(0, G4 * P)
            hidden(1, G4 * P)
            outs(0, G4)
            with pe.Fori(2, NG) as g:
                hidden(g, G4 * P)
                outs(g - 1, G4)
            hidden(NG, P)
            outs(NG - 1, G4)
            outs(NG, 1)

        @block.scalar
        def _(act):
            F = nc.scalar.activation
            made = [0]

            def link(ins):
                made[0] += 1
                ins.then_inc(s["act_chain"], 1)
                act.wait_ge(s["act_chain"], made[0])

            act.dma_start(biasb[:], bcast(gb1, D)).then_inc(s["biases_loaded"], 16)
            act.dma_start(bias2[:, 0], bcast(gb2, D)).then_inc(s["biases_loaded"], 16)
            act.dma_start(bias3[:, 0], bcast(proj_b, D)).then_inc(s["biases_loaded"], 16)
            act.dma_start(awb[:], attn_w.rearrange("(a n) b -> a (n b)", a=1).to_broadcast([P, D])
                          ).then_inc(s["small_loaded"], 16)
            act.dma_start(abb[:], bcast(attn_b, 1)).then_inc(s["small_loaded"], 16)
            act.dma_start(gbb[:], bcast(gate_b, NE)).then_inc(s["small_loaded"], 16)
            act.dma_start(gwt[:], gate_w.rearrange("(c p) e -> p c e", p=P)).then_inc(s["small_loaded"], 16)

            n = 0
            act.wait_ge(s["scales_made"], 1)
            for k, (w, col) in enumerate(((wk, K_), (wq, Q_), (wg1, W_), (wg2, W_), (None, 0), (None, 0))):
                for c in range(C):
                    n += 1
                    act.wait_ge(s["w_turned"], n)
                    if w is None:
                        F((wvT if k == 4 else pT32)[:, c, :], bank[(n - 1) % 4][:, :], ACT.Copy).then_inc(s["w_hi_made"], 1)
                    else:
                        F(w[:, 0, c, :], bank[(n - 1) % 4][:, :], ACT.Copy, scale=scale[:, col:col + 1]
                          ).then_inc(s["w_hi_made"], 1)

            def keys(i):
                t = i + 1
                if real(t):
                    after(act, s["t_made"], t + 1)
                    F(xT[:, 0:C, cols(t)], ps_t[0], ACT.Copy).then_inc(s["t_hi_taken"], 1)
                t = i + 3
                if real(t):
                    after(act, s["xn_made"], t + 1)
                    after(act, s["g_made"], t - XN + 1)
                    after(act, s["table_stored"], 16 * (t - XN + 1))
                    F(one(xnhl, t % XN)[:, 0:D], one(xn32, t % 2), ACT.Copy).then_inc(s["hi_made"], 1)
                t = i + 4
                if real(t):
                    after(act, s["mv_made"], t + 1)
                    after(act, s["rs_made"], t)
                    F(std[:], mv[:, 1:2], ACT.Sqrt, bias=epsc[:], scale=1.0 / (SX * SX)).then_inc(s["std_made"], 1)
                t = i
                if real(t):
                    after(act, s["k32_made"], t + 1)
                    after(act, s["g_made"], t - 1)
                    F(one(khl, t % 2)[:, 0:D], k32, ACT.Copy).then_inc(s["khi_made"], 1)
            pipeline(act, keys, -4, 2, T - 4, T)

            act.wait_ge(s["g_made"], T)
            for c in range(2):
                F(gt32[:, c, :], bank[c][:, :], ACT.Copy).then_inc(s["gt_hi_copied"], 1)
            act.wait_ge(s["mscale_made"], 1)
            for c in range(C):
                r = F(wm[:, 0, c, :], m32[:, c, :], ACT.Copy, scale=scale[:, M_:M_ + 1])
            r.then_inc(s["mhi_made"], 1)

            def layer(i):
                t = i - 3
                if real(t):
                    after(act, s["turned_x2"], t + 1)
                    F(xT[:, 0:C, cols(t)], ps_tx[:, :].rearrange("p (c n) -> p c n", c=C), ACT.Copy).then_inc(s["x2T_hi"], 1)
                t = i - 2
                if real(t):
                    after(act, s["mv2_made"], t + 1)
                    after(act, s["rs2_made"], t)
                    F(std[:], mv[:, 1:2], ACT.Sqrt, bias=epsc[:], scale=1.0 / (SX * SX)).then_inc(s["std2_made"], 1)
                t = i - 1
                if real(t):
                    after(act, s["turned_ah"], t + 1)
                    F(ahT[:, 0], ps_ta[:, :].rearrange("p (c n) -> p c n", c=C), ACT.Copy).then_inc(s["ahT_hi"], 1)
                    after(act, s["turned_p"], t + 1)
                    F(pT[:, 0], ps_tp[:, :].rearrange("p (c n) -> p c n", c=C), ACT.Copy, scale=SP_).then_inc(s["pT_hi"], 1)
                t = i - 2
                if real(t):
                    after(act, s["negm_made"], t + 1)
                    F(e2[:], sm[:], ACT.Exp, bias=negm[:]).then_inc(s["exp_made"], 1)
                    after(act, s["exp_made"], t + 1)
                    after(act, s["acc_made"], t)
                    F(accs, acc, ACT.Copy, scale=e2[:, 0:1]).then_inc(s["accs_made"], 1)
                    after(act, s["x2_stored"], 16 * t)
                    after(act, s["x2_made"], t + 1)
                    act.dma_start(x2_dram[bass.ds(t * P, P), :], x2).then_inc(s["x2_stored"], 16)
                t = i
                if real(t):
                    n = TAIL if isinstance(t, int) and t == T - 1 else P
                    if isinstance(t, int) and t == 0:
                        act.wait_ge(s["p2_ready"], 1)
                    after(act, s["xb_made"], t)
                    after(act, s["x_loaded2"], 16 * t)
                    act.dma_start(x_in[0:n, :], x[bass.ds(t * P, n), :]).then_inc(s["x_loaded2"], 16)
                    after(act, s["rd_made"], t + 1)
                    F(ah32, ps_agg[:, :], ACT.Copy, scale=rd[:]).then_inc(s["ah_made"], 1)
            pipeline(act, layer, 0, 4, T - 1, T + 3)

            act.wait_ge(s["best_made"], 2)
            F(wp[:], sm[:, 0:1], ACT.Exp, bias=gst[:, 1:2]).then_inc(s["wp_made"], 1)
            act.wait_ge(s["lg_made"], 1)
            F(gts[:], lg[:], ACT.Exp, bias=gst[:, 2:3]).then_inc(s["gexp_made"], 1)

            act.wait_ge(s["e_scales"], 1)
            F(w1s[:, 0], w1raw, ACT.Copy, scale=scale[:, W1_:W1_ + 1]).then_inc(s["w1_hi"], 1)
            F(w2s[:, 0], w2raw, ACT.Copy, scale=scale[:, W2_:W2_ + 1]).then_inc(s["w2_hi"], 1)
            act.wait_ge(s["b_loaded"], 64)

            def hidden(g, n):
                for b in range(2 * HC):
                    e, hc = b // HC, b % HC
                    after(act, s["z_made"], 2 * HC * g + b + 1)
                    after(act, s["h_lo"], 2 * HC * g - 2 * HC + b + 1)
                    F(g32[:, b, 0:n], bank[b][:, 0:n], ACT.Gelu, bias=b1t[:, e, hc:hc + 1], scale=mix[:, 3:4]
                      ).then_inc(s["g32_made"], 1)
                    after(act, s["g32_made"], 2 * HC * g + b + 1)
                    after(act, s["eo_made"], 2 * G4 * g - 2 * G4)
                    hh = hT[:, bass.ds(g % 2, 1)].rearrange("p b a e c n -> p (b a) e c n")
                    F(hh[:, 0, e, hc, 0:n], g32[:, b, 0:n], ACT.Copy, scale=scale[:, HB_:HB_ + 1]).then_inc(s["h_hi"], 1)

            def outs(g, tiles):
                for j in range(tiles):
                    for e in range(2):
                        m = 2 * (G4 * g + j) + e
                        after(act, s["pre_made"], m + 1)
                        after(act, s["y_half"], m - 3)
                        F(act2[:, j % 2, e], pre[:, j % 2, e], ACT.Gelu).then_inc(s["act_made"], 1)
            hidden(0, G4 * P)
            hidden(1, G4 * P)
            outs(0, G4)
            with act.Fori(2, NG) as g:
                hidden(g, G4 * P)
                outs(g - 1, G4)
            hidden(NG, P)
            outs(NG - 1, G4)
            outs(NG, 1)

        @block.vector
        def _(dve):
            V = nc.vector
            made = [0]

            def link(ins):
                made[0] += 1
                ins.then_inc(s["dve_chain"], 1)
                dve.wait_ge(s["dve_chain"], made[0])

            def powers(a, b, sw=SW):
                link(V.tensor_scalar(gmax[:, a:b], gmax[:, a:b], 1e-30, None, ALU.max))
                link(V.tensor_scalar(pow2[:, a:b].bitcast(I32), gmax[:, a:b].bitcast(I32), 0x7F800000, None,
                                     ALU.bitwise_and))
                link(V.reciprocal(scale[:, a:b], pow2[:, a:b]))
                link(V.tensor_scalar(scale[:, a:b], scale[:, a:b], sw, None, ALU.mult))
                link(V.tensor_scalar(undo[:, a:b], pow2[:, a:b], 1.0 / sw, None, ALU.mult))

            dve.wait_ge(s["consts"], NCONST)
            dve.wait_ge(s["edges_loaded"], 96)
            V.tensor_copy(f_src, raw_src)
            link(V.tensor_copy(f_dst, raw_dst))
            dve.sem_inc(s["floats_made"], 1)
            n = 0
            for col in (src_col, dst_col):
                for k in range(CH):
                    n += 1
                    w = min(P, BLOCKS - k * P)
                    dve.wait_ge(s["turned_edges"], n)
                    r = V.tensor_copy(col[:, 1 + k * P:1 + k * P + w], bank[6 + (n - 1) % 2][:, 0:w])
                    r.then_inc(s["turned_taken"], 1)
            dve.wait_ge(s["turned_taken"], n)
            dve.sem_inc(s["cols_made"], 1)
            link(V.tensor_scalar(f_pad, f_dst, 0.0, float(1 << 20), ALU.is_lt, ALU.mult))
            link(V.tensor_tensor(f_pad, f_pad, f_dst, ALU.add))
            V.tensor_reduce(colmax[:], f_dst, AX.X, ALU.max)
            link(V.tensor_reduce(colmin[:], f_pad, AX.X, ALU.min))
            shape = [P, CH, T + 1]
            base3 = tile_base[:, None, :].to_broadcast(shape)
            link(V.tensor_scalar(colok[:], colidx[:], float(BLOCKS), None, ALU.is_le))
            ok3 = colok[:, :, None].to_broadcast(shape)
            link(V.tensor_tensor(below, colmax[:, :, None].to_broadcast(shape), base3, ALU.is_lt))
            link(V.tensor_tensor(below, below, ok3, ALU.mult))
            dve.sem_inc(s["below_made"], 1)
            dve.wait_ge(s["below_summed"], 1)
            link(V.tensor_copy(firsts[:], bank[5][:, 0:T + 1]))
            f3 = firsts[:, None, :].to_broadcast(shape)
            c3 = colidx[:, :, None].to_broadcast(shape)
            link(V.tensor_tensor(viol, c3, f3, ALU.is_le))
            link(V.tensor_tensor(viol, viol, ok3, ALU.mult))
            link(V.tensor_tensor(viol2, viol, below, ALU.mult))
            link(V.tensor_tensor(viol, viol, viol2, ALU.subtract))
            link(V.tensor_reduce(vsum[:, 0:1], viol, AX.XY, ALU.add))
            link(V.tensor_scalar(firsts[:, 1:T + 1], firsts[:, 1:T + 1], 1.0, None, ALU.add))
            link(V.tensor_tensor(viol, colmin[:, :, None].to_broadcast(shape), base3, ALU.is_lt))
            link(V.tensor_tensor(viol, viol, ok3, ALU.mult))
            link(V.tensor_tensor(viol2, c3, f3, ALU.is_gt))
            link(V.tensor_tensor(viol, viol, viol2, ALU.mult))
            link(V.tensor_reduce(vsum[:, 1:2], viol, AX.XY, ALU.add))
            dve.sem_inc(s["viol_made"], 1)
            dve.wait_ge(s["viol_summed"], 1)
            link(V.tensor_reduce(vsum[:, 2:3], bank[4][:, 0:2], AX.X, ALU.add))
            link(V.tensor_scalar(vsum[:, 3:4], vsum[:, 2:3], 0.0, None, ALU.is_gt))
            link(V.tensor_scalar(uns[:], uns[:], float(COLS * T - 1), None, ALU.min))
            link(V.tensor_tensor(uns[:], uns[:], firsts[:], ALU.subtract))
            link(V.scalar_tensor_tensor(out=first_i[:, 0:T + 1], in0=uns[:], scalar=vsum[:, 3:4], in1=firsts[:],
                                        op0=ALU.mult, op1=ALU.add))
            link(V.tensor_scalar(upper[:], first_i[:, 0:T + 1], U.bit_length() - 2, 1, ALU.arith_shift_right,
                                 ALU.bitwise_and))
            link(V.tensor_scalar(lower[:], upper[:], 1, None, ALU.bitwise_xor))
            link(V.tensor_scalar(first_i[:, 0:T + 1], first_i[:, 0:T + 1], U.bit_length() - 1, None,
                                 ALU.arith_shift_right))
            link(V.tensor_scalar(first_i[:, T + 1:T + 2], vsum[:, 3:4], float(T - 1), 1.0, ALU.mult, ALU.add))
            dve.sem_inc(s["firsts_made"], 1)
            link(V.tensor_scalar(rowmask[:], rowi[:], float(TAIL), None, ALU.is_lt))
            link(V.tensor_scalar(rowlow[:], rowmask[:], -LOW, LOW, ALU.mult, ALU.add))

            for k, col in ((0, K_), (1, Q_), (2, W_), (3, 7)):
                dve.wait_ge(w_loaded[k], 16)
                V.tensor_reduce(amax[:, col:col + 1], raw_w[k], AX.XY, ALU.max, apply_absolute_value=True
                                ).then_inc(s["dve_chain"], 1)
                made[0] += 1
            dve.wait_ge(s["dve_chain"], made[0])
            link(V.tensor_tensor(amax[:, W_:W_ + 1], amax[:, W_:W_ + 1], amax[:, 7:8], ALU.max))
            dve.sem_inc(s["amax_made"], 1)
            dve.wait_ge(s["gmax_made"], 1)
            powers(0, 3)
            dve.sem_inc(s["scales_made"], 1)
            dve.wait_ge(s["biases_loaded"], 48)
            link(V.tensor_tensor(bias2[:, 0], bias2[:, 0], bias3[:, 0], ALU.add))
            link(V.tensor_tensor(biasb[:], biasb[:], bias2[:, 0], ALU.add))
            n = 0
            for k, (w, col) in enumerate(((wk, K_), (wq, Q_), (wg1, W_), (wg2, W_), (None, 0), (None, 0))):
                for c in range(C):
                    n += 1
                    dve.wait_ge(s["w_hi_made"], n)
                    if w is not None:
                        V.scalar_tensor_tensor(out=w[:, 1, c, :], in0=bank[(n - 1) % 4][:, :],
                                               scalar=scale[:, col:col + 1], in1=w[:, 0, c, :],
                                               op0=ALU.mult, op1=ALU.subtract).then_inc(s["w_lo_made"], 1)

            def keys(i):
                t = i + 1
                if real(t):
                    after(dve, s["t_made"], t + 1)
                    V.tensor_copy(xT[:, C:2 * C, cols(t)], ps_t[1]).then_inc(s["t_lo_taken"], 1)
                t = i + 3
                if real(t):
                    after(dve, s["std_made"], t + 1)
                    V.reciprocal(rs0[:], std[:]).then_inc(s["rs_made"], 1)
                    after(dve, s["rs_made"], t + 1)
                    m = rowmask[:] if isinstance(t, int) and t == T - 1 else ones[:, 0:1]
                    V.tensor_scalar(rstd[:], rs0[:], m, None, ALU.mult).then_inc(s["rstd_made"], 1)
                    after(dve, s["rstd_made"], t + 1)
                    after(dve, s["hi_made"], t - 1)
                    V.tensor_scalar(one(xn32, t % 2), one(xin, t % XI), mv[:, 0:1], rstd[:],
                                    ALU.subtract, ALU.mult).then_inc(s["xn_made"], 1)
                t = i + 2
                if real(t):
                    after(dve, s["hi_made"], t + 1)
                    V.tensor_tensor(one(xnhl, t % XN)[:, D:2 * D], one(xn32, t % 2), one(xnhl, t % XN)[:, 0:D],
                                    ALU.subtract).then_inc(s["lo_made"], 1)
                t = i + 4
                if real(t):
                    after(dve, s["x_loaded"], 16 * t + 16)
                    V.bn_stats(st6[:], one(xin, t % XI)).then_inc(s["stats_made"], 1)
                    after(dve, s["stats_made"], t + 1)
                    after(dve, s["xn_made"], t)
                    dve.sem_inc(s["turn"], 1)
                    V.bn_aggr(mv[:], st6[:]).then_inc(s["mv_made"], 1)
                t = i
                if real(t):
                    after(dve, s["k_made"], t + 1)
                    after(dve, s["kacc_made"], t)
                    V.tensor_scalar(k32, ps_k[:, :], SK, 0.0, ALU.mult, ALU.max).then_inc(s["k32_made"], 1)
            pipeline(dve, keys, -4, 2, T - 4, T)

            dve.wait_ge(s["g_made"], T)
            for c in (2, 3):
                V.tensor_copy(gt32[:, c, :], bank[c][:, :]).then_inc(s["gt_lo_copied"], 1)
            dve.wait_ge(s["ksum_made"], 1)
            link(V.tensor_scalar(kinv[:], bank[6][:, 0:C], 1e-30, None, ALU.max))
            link(V.reciprocal(kinv[:], kinv[:]))
            link(V.tensor_scalar(kinv[:], kinv[:], 1.0 / SX, None, ALU.mult))
            link(V.tensor_tensor(mix[:, 0:1], undo[:, K_:K_ + 1], undo[:, Q_:Q_ + 1], ALU.mult))
            link(V.tensor_scalar(mix[:, 0:1], mix[:, 0:1], 1.0 / (SX * SX * SK), None, ALU.mult))
            link(V.tensor_scalar(ksb[:], bank[7][:, :], mix[:, 0:1], None, ALU.mult))
            link(V.tensor_scalar(mix[:, 1:2], undo[:, W_:W_ + 1], 1.0 / SX, None, ALU.mult))
            dve.wait_ge(s["vt_made"], 1)
            V.tensor_tensor(vtm, bank[4][:, :].rearrange("p (a f) -> p a f", a=C),
                            hmask[:, None, :].to_broadcast([P, C, P]), ALU.mult).then_inc(s["vtm_made"], 1)
            for j in range(C):
                dve.wait_ge(s["m_made"], j + 1)
                link(V.tensor_scalar(m32[:, j, :], bank[j][:, :], kinv[:, j:j + 1], None, ALU.mult))
            link(V.tensor_reduce(amax[:, M_:M_ + 1], m32, AX.XY, ALU.max, apply_absolute_value=True))
            dve.sem_inc(s["mmax_made"], 1)
            dve.wait_ge(s["mgmax_made"], 1)
            powers(M_, M_ + 1)
            link(V.tensor_scalar(mix[:, 2:3], undo[:, M_:M_ + 1], 1.0 / SP_, None, ALU.mult))
            dve.sem_inc(s["mscale_made"], 1)
            dve.wait_ge(s["mhi_made"], 1)
            for c in range(C):
                r = V.scalar_tensor_tensor(out=wm[:, 1, c, :], in0=m32[:, c, :], scalar=scale[:, M_:M_ + 1],
                                           in1=wm[:, 0, c, :], op0=ALU.mult, op1=ALU.subtract)
            link(r)
            link(V.memset(acc, 0.0))
            dve.sem_inc(s["p2_ready"], 1)

            def layer(i):
                t = i
                if real(t):
                    a = dve.value_load(first_i[0:1, bass.ds(t, 1)], min_val=0, max_val=GROUPS * T)
                    b = dve.value_load(first_i[0:1, bass.ds(t + 1, 1)], min_val=0, max_val=GROUPS * T)
                    V.tensor_scalar(iota_t[:], iota16[:], tile_base[:, bass.ds(t, 1)], None, ALU.add
                                    ).then_inc(s["iota_made"], 1)
                    after(dve, s["iota_made"], t + 1)
                    dve.sem_inc(s["turn"], 1)
                    with dve.Fori(a, b + 1) as q:
                        dve.wait_ge(s["oh_used"], q + t + 1)
                        V.tensor_tensor(onehot[:, bass.ds((q + t) % OG * U, U), :],
                                        iota_t[:, None, :].to_broadcast([P, U, P]),
                                        dst_col[:, bass.ds(q % GROUPS * U, U), None].to_broadcast([P, U, P]),
                                        ALU.is_equal).then_inc(s["oh_made"], 1)
                t = i - 3
                if real(t):
                    after(dve, s["x2T_hi"], t + 1)
                    V.tensor_tensor(xT[:, C:2 * C, cols(t)], ps_tx[:, :].rearrange("p (c n) -> p c n", c=C),
                                    xT[:, 0:C, cols(t)], ALU.subtract).then_inc(s["x2T_lo"], 1)
                t = i - 2
                if real(t):
                    after(dve, s["lin_made"], t + 1)
                    after(dve, s["x2_stored"], 16 * t)
                    after(dve, s["xb_made"], t + 1)
                    V.scalar_tensor_tensor(out=x2, in0=ps_o[:, :], scalar=mix[:, 1:2], in1=xb,
                                           op0=ALU.mult, op1=ALU.add).then_inc(s["xa_made"], 1)
                    after(dve, s["xa_made"], t + 1)
                    V.scalar_tensor_tensor(out=x2, in0=ps_b[:, :], scalar=mix[:, 2:3], in1=x2,
                                           op0=ALU.mult, op1=ALU.add).then_inc(s["x2_made"], 1)
                    after(dve, s["x2_made"], t + 1)
                    V.bn_stats(st6[:], x2).then_inc(s["st2_made"], 1)
                    after(dve, s["st2_made"], t + 1)
                    dve.sem_inc(s["turn"], 1)
                    V.bn_aggr(mv[:], st6[:]).then_inc(s["mv2_made"], 1)
                t = i - 1
                if real(t):
                    after(dve, s["ahT_hi"], t + 1)
                    V.tensor_tensor(ahT[:, 1], ps_ta[:, :].rearrange("p (c n) -> p c n", c=C), ahT[:, 0],
                                    ALU.subtract).then_inc(s["ahT_lo"], 1)
                    after(dve, s["pT_hi"], t + 1)
                    V.scalar_tensor_tensor(out=pT[:, 1], in0=ps_tp[:, :].rearrange("p (c n) -> p c n", c=C),
                                           scalar=SP_, in1=pT[:, 0], op0=ALU.mult, op1=ALU.subtract
                                           ).then_inc(s["pT_lo"], 1)
                t = i - 2
                if real(t):
                    after(dve, s["std2_made"], t + 1)
                    V.reciprocal(rstd[:], std[:]).then_inc(s["rs2_made"], 1)
                    after(dve, s["rs2_made"], t + 1)
                    after(dve, s["turned_x2"], t)
                    V.tensor_scalar(xn2, x2, mv[:, 0:1], rstd[:], ALU.subtract, ALU.mult).then_inc(s["xn2_made"], 1)
                    after(dve, s["xn2_made"], t + 1)
                    V.scalar_tensor_tensor(out=accs, in0=xn2, scalar=1.0 / SX, in1=awb[:], op0=ALU.mult, op1=ALU.mult,
                                           accum_out=sraw[:]).then_inc(s["sraw_made"], 1)
                    after(dve, s["sraw_made"], t + 1)
                    after(dve, s["m_kept"], t)
                    V.tensor_scalar(sm[:, 1:2], sraw[:], abb[:], None, ALU.add).then_inc(s["sc_made"], 1)
                    if isinstance(t, int) and t == T - 1:
                        dve.wait_ge(s["sc_made"], t + 1)
                        link(V.tensor_tensor(sm[:, 1:2], sm[:, 1:2], rowmask[:], ALU.mult))
                        link(V.tensor_tensor(sm[:, 1:2], sm[:, 1:2], rowlow[:], ALU.add))
                    after(dve, s["sc_made"], t + 1)
                    V.tensor_reduce(negm[:], sm[:], AX.X, ALU.max, negate=True).then_inc(s["negm_made"], 1)
                t = i
                if real(t):
                    after(dve, s["q_made"], t + 1)
                    after(dve, s["turned_p"], t)
                    V.scalar_tensor_tensor(out=w32, in0=ps_q[:, :], scalar=0.0, in1=ksb[:], op0=ALU.max,
                                           op1=ALU.mult).then_inc(s["w_made"], 1)
                    after(dve, s["w_made"], t + 1)
                    V.tensor_reduce(den[:], w32.rearrange("p (h c) -> p h c", c=HEAD), AX.X, ALU.add
                                    ).then_inc(s["den_made"], 1)
                    after(dve, s["den_made"], t + 1)
                    V.tensor_scalar(den2[:], den[:], EPS_ATT, None, ALU.add).then_inc(s["den2_made"], 1)
                    after(dve, s["den2_made"], t + 1)
                    V.reciprocal(den[:], den2[:]).then_inc(s["rec_made"], 1)
                    after(dve, s["rec_made"], t + 1)
                    w3 = w32.rearrange("p (h c) -> p h c", c=HEAD)
                    V.tensor_tensor(w3, w3, den[:, :, None].to_broadcast([P, D // HEAD, HEAD]), ALU.mult
                                    ).then_inc(s["p_made"], 1)
                t = i - 2
                if real(t):
                    after(dve, s["accs_made"], t + 1)
                    V.tensor_scalar(sm[:, 0:1], negm[:], -1.0, None, ALU.mult).then_inc(s["m_kept"], 1)
                    after(dve, s["l_made"], t)
                    V.scalar_tensor_tensor(out=lsum[:], in0=lsum[:], scalar=e2[:, 0:1], in1=e2[:, 1:2],
                                           op0=ALU.mult, op1=ALU.add).then_inc(s["l_made"], 1)
                    V.scalar_tensor_tensor(out=acc, in0=xn2, scalar=e2[:, 1:2], in1=accs,
                                           op0=ALU.mult, op1=ALU.add).then_inc(s["acc_made"], 1)
                t = i - 1
                if real(t):
                    after(dve, s["x_loaded2"], 16 * t + 16)
                    V.tensor_tensor(xb, x_in, biasb[:], ALU.add).then_inc(s["xb_made"], 1)
                t = i
                if real(t):
                    after(dve, s["agg_made"], t + 1)
                    V.tensor_scalar(dg[:], ps_deg[:, 0:1], 1.0, None, ALU.max).then_inc(s["dg_made"], 1)
                    after(dve, s["dg_made"], t + 1)
                    V.reciprocal(rd[:], dg[:]).then_inc(s["rd_made"], 1)
            pipeline(dve, layer, 0, 4, T, T + 3)

            dve.wait_ge(s["best_made"], 1)
            link(V.tensor_scalar(gst[:, 1:2], gst[:, 0:1], -1.0, None, ALU.mult))
            dve.sem_inc(s["best_made"], 1)
            dve.wait_ge(s["wp_made"], 1)
            dve.wait_ge(s["l_made"], T)
            V.tensor_tensor(lw[:], lsum[:], wp[:], ALU.mult).then_inc(s["lw_made"], 1)
            dve.wait_ge(s["pooled_made"], 1)
            link(V.tensor_copy(pld[:, 0:C + 1], bank[0][:, 0:C + 1]))
            link(V.reciprocal(pld[:, 5:6], pld[:, C:C + 1]))
            link(V.tensor_scalar(pld[:, 5:6], pld[:, 5:6], 1.0 / SX, None, ALU.mult))
            link(V.tensor_scalar(pld[:, 0:C], pld[:, 0:C], pld[:, 5:6], None, ALU.mult))
            link(V.tensor_copy(plb, pld[:, 0:C, None].to_broadcast([P, C, P])))
            dve.wait_ge(s["small_loaded"], 64)
            dve.sem_inc(s["plb_made"], 1)
            dve.wait_ge(s["logits_made"], 1)
            link(V.tensor_tensor(lg[:], bank[1][:, 0:NE], gbb[:], ALU.add))
            link(V.tensor_reduce(gst[:, 2:3], lg[:], AX.X, ALU.max, negate=True))
            dve.sem_inc(s["lg_made"], 1)
            dve.wait_ge(s["gexp_made"], 1)
            link(V.tensor_reduce(gst[:, 3:4], gts[:], AX.X, ALU.add))
            link(V.reciprocal(gst[:, 4:5], gst[:, 3:4]))
            link(V.tensor_scalar(gts[:], gts[:], gst[:, 4:5], None, ALU.mult))
            link(V.max(top[:], gts[:]))
            link(V.max_index(topi[:], top[:], gts[:]))
            dve.sem_inc(s["chosen"], 1)
            link(V.tensor_tensor(gst[:, 5:6], top[:, 0:1], top[:, 1:2], ALU.add))
            link(V.tensor_scalar(gst[:, 5:6], gst[:, 5:6], EPS_GATE, None, ALU.add))
            link(V.reciprocal(gst[:, 6:7], gst[:, 5:6]))
            link(V.tensor_scalar(gexp[:], top[:, 0:2], gst[:, 6:7], None, ALU.mult))

            dve.wait_ge(s["x2_stored"], 16 * T)
            for k in range(4):
                dve.wait_ge(e_loaded[k], 16)
            dve.wait_ge(s["b_loaded"], 64)
            V.tensor_reduce(amax[:, W1_:W1_ + 1], w1raw.rearrange("p e c h -> p (e c h)"), AX.X, ALU.max, apply_absolute_value=True)
            V.tensor_reduce(amax[:, HB_:HB_ + 1], b1t[:], AX.XY, ALU.max, apply_absolute_value=True)
            link(V.tensor_reduce(amax[:, W2_:W2_ + 1], w2raw.rearrange("p e c o -> p (e c o)"), AX.X, ALU.max, apply_absolute_value=True))
            dve.sem_inc(s["e_amax_made"], 1)
            dve.wait_ge(s["e_gmax_made"], 1)
            link(V.scalar_tensor_tensor(out=gmax[:, HB_:HB_ + 1], in0=gmax[:, W1_:W1_ + 1], scalar=float(D),
                                        in1=gmax[:, HB_:HB_ + 1], op0=ALU.mult, op1=ALU.add))
            powers(4, 7)
            link(V.tensor_scalar(mix[:, 3:4], undo[:, W1_:W1_ + 1], 1.0 / SX, None, ALU.mult))
            link(V.tensor_tensor(mix[:, 4:5], undo[:, HB_:HB_ + 1], undo[:, W2_:W2_ + 1], ALU.mult))
            dve.sem_inc(s["e_scales"], 1)
            dve.wait_ge(s["w1_hi"], 1)
            flat1, flat2 = "p e c h -> p (e c h)", "p e c o -> p (e c o)"
            V.scalar_tensor_tensor(out=w1s[:, 1].rearrange(flat1), in0=w1raw.rearrange(flat1),
                                   scalar=scale[:, W1_:W1_ + 1], in1=w1s[:, 0].rearrange(flat1),
                                   op0=ALU.mult, op1=ALU.subtract).then_inc(s["w1_lo"], 1)
            dve.wait_ge(s["w2_hi"], 1)
            V.scalar_tensor_tensor(out=w2s[:, 1].rearrange(flat2), in0=w2raw.rearrange(flat2),
                                   scalar=scale[:, W2_:W2_ + 1], in1=w2s[:, 0].rearrange(flat2),
                                   op0=ALU.mult, op1=ALU.subtract).then_inc(s["w2_lo"], 1)

            def hidden(g, n):
                for b in range(2 * HC):
                    e, hc = b // HC, b % HC
                    after(dve, s["h_hi"], 2 * HC * g + b + 1)
                    hh = hT[:, bass.ds(g % 2, 1)].rearrange("p b a e c n -> p (b a) e c n")
                    V.scalar_tensor_tensor(out=hh[:, 1, e, hc, 0:n], in0=g32[:, b, 0:n], scalar=scale[:, HB_:HB_ + 1],
                                           in1=hh[:, 0, e, hc, 0:n], op0=ALU.mult, op1=ALU.subtract
                                           ).then_inc(s["h_lo"], 1)

            def outs(g, tiles):
                def add(j):
                    y = x2g[:, bass.ds(g % 2, 1), j, :].rearrange("p a f -> p (a f)")
                    if j == 0:
                        after(dve, s["x2g_loaded"], 16 * g + 16)
                    for e in range(2):
                        m = 2 * (G4 * g + j) + e
                        after(dve, s["act_made"], m + 1)
                        after(dve, s["y_half"], m)
                        r = V.scalar_tensor_tensor(out=y, in0=act2[:, j % 2, e], scalar=gexp[:, e:e + 1], in1=y,
                                                   op0=ALU.mult, op1=ALU.add)
                        r.then_inc(s["y_half"], 1)
                    after(dve, s["y_half"], m + 1)
                    dve.sem_inc(s["y_made"], 1)
                for j in range(tiles):
                    for e in range(2):
                        m = 2 * (G4 * g + j) + e
                        after(dve, s["eo_made"], m + 1)
                        after(dve, s["act_made"], m - 3)
                        V.scalar_tensor_tensor(out=pre[:, j % 2, e], in0=bank[4 + 2 * (j % 2) + e][:, :],
                                               scalar=mix[:, 4:5], in1=b2b[:, e], op0=ALU.mult, op1=ALU.add
                                               ).then_inc(s["pre_made"], 1)
                    if j:
                        add(j - 1)
                add(tiles - 1)
            hidden(0, G4 * P)
            hidden(1, G4 * P)
            outs(0, G4)
            with dve.Fori(2, NG) as g:
                hidden(g, G4 * P)
                outs(g - 1, G4)
            hidden(NG, P)
            outs(NG - 1, G4)
            outs(NG, 1)


_INS = ['x', 'src', 'dst', 'L0_gnn_W1', 'L0_gnn_b1', 'L0_gnn_W2', 'L0_gnn_b2', 'L0_mix_qkv_weight',
        'L0_mix_proj_weight', 'L0_mix_proj_bias', 'L0_ffn_attn_w', 'L0_ffn_attn_b', 'L0_ffn_gate_w',
        'L0_ffn_gate_b', 'L0_ffn_w1', 'L0_ffn_b1', 'L0_ffn_w2', 'L0_ffn_b2']


def kernel(**inputs):
    import concourse.bacc as _bacc
    from concourse.bass_utils import run_bass_kernel_spmd as _run

    nc = _bacc.Bacc("TRN2", target_bir_lowering=False, num_devices=1)
    arrays, args = {}, []
    for name in _INS:
        a = np.ascontiguousarray(inputs[name])
        arrays[f"in_{name}"] = a
        args.append(nc.dram_tensor(f"in_{name}", a.shape, mybir.dt.from_np(a.dtype), kind="ExternalInput").ap())
    args.append(nc.dram_tensor("out_x", (N, D), F32, kind="ExternalOutput").ap())
    program(nc, *args)
    r = _run(nc, [arrays], core_ids=[0])
    return r.results[0]["out_x"]
```

```python
from contextlib import ExitStack

import numpy as np

import concourse.bass as bass
from concourse import mybir

F32, F16, I32, U32 = mybir.dt.float32, mybir.dt.float16, mybir.dt.int32, mybir.dt.uint32
ALU = mybir.AluOpType
ACT = mybir.ActivationFunctionType
AX = mybir.AxisListType
RMAX = bass.bass_isa.ReduceOp.max

P = 128
N, D, E = 6250, 512, 100000
HEAD = 32
NE, H = 8, 256
C = D // P
HC = H // P
T = (N + P - 1) // P
TAIL = N - (T - 1) * P
ROWS = T * P
BLOCKS = (E + P - 1) // P
R = 16
COLS = (BLOCKS + 2 + R - 1) // R * R
ROUNDS = COLS // R
U = 4
RG = R // U
OG = 8
GROUPS = COLS // U
CH = (BLOCKS + P - 1) // P
FULL = BLOCKS // P
XN = 5
XI = 3
G4 = 4
NG = T // G4
EPS_LN = 1e-5
EPS_ATT = 1e-15
EPS_GATE = 1e-9
SX = 2.0 ** 10
SW = 2.0 ** 14
SK = 2.0 ** -19
SP_ = 2.0 ** 14
LOW = -1e30
FAR = 1 << 20

K_, Q_, W_, M_, W1_, HB_, W2_ = range(7)


def real(t):
    return not isinstance(t, int) or 0 <= t < T


def after(eng, sem, count):
    if not isinstance(count, int) or count > 0:
        eng.wait_ge(sem, count)


def pipeline(eng, body, first, lo, hi, last):
    for i in range(first, lo):
        body(i)
    with eng.Fori(lo, hi) as i:
        body(i)
    for i in range(hi, last):
        body(i)


def program(nc, x, src, dst, gw1, gb1, gw2, gb2, qkv_w, proj_w, proj_b, attn_w, attn_b, gate_w, gate_b,
            w1, b1, w2, b2, out):
    ctx = ExitStack()
    with ctx:
        def sb(name, shape, dt):
            return ctx.enter_context(nc.sbuf_tensor(name, shape, dt))

        table = nc.dram_tensor("table", (N, 2 * D), F16, kind="Internal").ap()
        x2_dram = nc.dram_tensor("x2_rows", (ROWS, D), F32, kind="Internal").ap()

        xT = sb("xT", [P, 2 * C, ROWS], F16)
        flat = xT[:, :, :].rearrange("p a n -> p (a n)").bitcast(F32)
        raw_w = [flat[:, k * C * D:(k + 1) * C * D].rearrange("p (a f) -> p a f", a=C) for k in range(6)]
        o = 6 * C * D
        raw_src = flat[:, o:o + CH * P].bitcast(I32).rearrange("p (a f) -> p a f", a=CH)
        o += CH * P
        raw_dst = flat[:, o:o + CH * P].bitcast(I32).rearrange("p (a f) -> p a f", a=CH)
        o += CH * P
        f_src = flat[:, o:o + CH * P].rearrange("p (a f) -> p a f", a=CH)
        o += CH * P
        f_dst = flat[:, o:o + CH * P].rearrange("p (a f) -> p a f", a=CH)
        o += CH * P
        steps = flat[:, o:o + CH * P].rearrange("p (a f) -> p a f", a=CH)
        o += CH * P
        below = flat[:, o:o + CH * (T + 1)].bitcast(F16)[:, 0:CH * (T + 1)].rearrange("p (a f) -> p a f", a=CH)

        wts = sb("wts", [P, 4, 2, C, D], F16)
        wk, wq, wg1, wg2 = (wts[:, k] for k in range(4))
        wm = wk
        w1raw = wts[:, 0].rearrange("p a c f -> p (a c f)").bitcast(F32).rearrange("p (e c h) -> p e c h", e=2, c=C)
        w2raw = wts[:, 1].rearrange("p a c f -> p (a c f)").bitcast(F32).rearrange("p (e c o) -> p e c o", e=2, c=HC)
        w1s = wts[:, 2].rearrange("p a c f -> p a (c f)").rearrange("p a (e c h) -> p a e c h", e=2, c=C)
        w2s = wts[:, 3].rearrange("p a c f -> p a (c f)").rearrange("p a (e c o) -> p a e c o", e=2, c=HC)

        ring = sb("ring", [P, R, 2 * D], F16)
        ring32 = ring[:, :, :].rearrange("p a f -> p (a f)").bitcast(F32).rearrange("p (a f) -> p a f", f=D)
        xnhl = ring[:, 0:XN, :]
        xin = ring32[:, XN:XN + XI, :]
        xn32 = ring32[:, XN + XI:XN + XI + 2, :]
        k32 = ring32[:, XN + XI + 2, :]
        khl = ring[:, XN + XI + 3:XN + XI + 5, :]
        x2g = ring32[:, 0:2 * G4, :].rearrange("p (b j) f -> p b j f", b=2)
        hT = ring[:, 2 * G4:4 * G4, :].rearrange("p a f -> p (a f)").rearrange(
            "p (b a e c n) -> p b a e c n", b=2, a=2, e=2, c=HC)

        onehot = sb("onehot", [P, OG * U, P], F16)
        oh32 = onehot[:, :, :].rearrange("p a f -> p (a f)").bitcast(F32)
        gt32 = oh32.rearrange("p (a f) -> p a f", a=C)
        g32 = gt32
        plb = oh32[:, 0:C * P].rearrange("p (a f) -> p a f", a=C)

        work = sb("work", [P, 10, D], F32)
        wvT, m32, pT32 = work[:, 0:4], work[:, 0:4], work[:, 4:8]
        vtm = work[:, 8].rearrange("p (a f) -> p a f", a=C)
        kacc = work[:, 9]
        x_in, xb, x2, xn2, acc, accs, w32, ah32 = (work[:, k] for k in range(8))
        ahT, pT = (work[:, k].bitcast(F16).rearrange("p (a c n) -> p a c n", a=2, c=C) for k in (8, 9))
        pre = work[:, 0:4].rearrange("p (b e) f -> p b e f", b=2)
        act2 = work[:, 4:8].rearrange("p (b e) f -> p b e f", b=2)
        b2b = work[:, 8:10]

        src_col = sb("src_col", [P, COLS], I32)
        dst_col = sb("dst_col", [P, COLS], F32)
        biasb = sb("biasb", [P, D], F32)
        awb = sb("awb", [P, D], F32)
        bias3 = ring32[:, 15:16, :]
        bias2 = ring32[:, 14:15, :]

        ident = sb("ident", [P, P], F32)
        ident16 = sb("ident16", [P, P], F16)
        ones = sb("ones", [P, P], F32)
        hmask = sb("hmask", [P, P], F32)
        iota_t = hmask
        zero16 = sb("zero16", [P, P], F16)
        ones16 = sb("ones16", [P, P], F16)
        iota16 = sb("iota16", [P, P], F16)
        tile_base = sb("tile_base", [P, T + 1], F32)
        firsts = sb("firsts", [P, T + 1], F32)
        uns = sb("uns", [P, T + 1], F32)
        first_i = sb("first_i", [P, T + 2], I32)
        upper = sb("upper", [P, T + 1], I32)
        lower = sb("lower", [P, T + 1], I32)
        before = sb("before", [P, CH], I32)
        least = sb("least", [P, 4], F32)
        back16 = sb("back16", [P, 1], F16)
        unsorted = sb("unsorted", [P, 1], F32)
        rowi = sb("rowi", [P, 1], F32)
        rowmask = sb("rowmask", [P, 1], F32)
        rowlow = sb("rowlow", [P, 1], F32)
        idx_slots = sb("idx_slots", [P, R], I32)
        epsc = sb("epsc", [P, 1], F32)
        amax = sb("amax", [P, 8], F32)
        gmax = sb("gmax", [P, 8], F32)
        pow2 = sb("pow2", [P, 8], F32)
        scale = sb("scale", [P, 8], F32)
        undo = sb("undo", [P, 8], F32)
        mix = sb("mix", [P, 8], F32)
        st6 = sb("st6", [P, 6], F32)
        mv = sb("mv", [P, 2], F32)
        std = sb("std", [P, 1], F32)
        rs0 = sb("rs0", [P, 1], F32)
        rstd = sb("rstd", [P, 1], F32)
        kinv = sb("kinv", [P, C], F32)
        ksb = sb("ksb", [P, D], F32)
        den = sb("den", [P, D // HEAD], F32)
        den2 = sb("den2", [P, D // HEAD], F32)
        dg = sb("dg", [P, 1], F32)
        rd = sb("rd", [P, 1], F32)
        sraw = sb("sraw", [P, 1], F32)
        sm = sb("sm", [P, 2], F32)
        negm = sb("negm", [P, 1], F32)
        e2 = sb("e2", [P, 2], F32)
        lsum = sb("lsum", [P, 1], F32)
        wp = sb("wp", [P, 1], F32)
        lw = sb("lw", [P, 1], F32)
        gst = sb("gst", [P, 8], F32)
        abb = sb("abb", [P, 1], F32)
        gwt = sb("gwt", [P, C, NE], F32)
        gbb = sb("gbb", [P, NE], F32)
        pld = sb("pld", [P, 8], F32)
        lg = sb("lg", [P, NE], F32)
        gts = sb("gts", [P, NE], F32)
        top = sb("top", [P, 8], F32)
        topi = sb("topi", [P, 8], U32)
        gexp = sb("gexp", [P, 2], F32)
        b1t = sb("b1t", [P, 2, HC], F32)

        bank = [ctx.enter_context(nc.psum_tensor(f"bank{k}", [P, D], F32)) for k in range(8)]
        ps_q, ps_o, ps_b, ps_agg, ps_deg, ps_ta, ps_tp, ps_tx = bank
        ps_t = [bank[b][:, :].bitcast(F16).rearrange("p (q n) -> p q n", q=2 * C)[:, 0:C, :] for b in (4, 6)]
        ps_k = bank[5]

        names = """consts pads_made ident_made dve_chain act_chain pool_chain
            edges_loaded biases_loaded small_loaded floats_made turned_edges below_made below_summed counts_read
            firsts_made cols_made
            amax_made gmax_made scales_made w_turned w_hi_made w_lo_made
            x_loaded stats_made mv_made std_made rs_made rstd_made xn_made hi_made lo_made table_stored
            t_made t_hi_taken t_lo_taken k_made k32_made khi_made klo_made kacc_made g_made
            ksum_made gt_hi_copied gt_lo_copied vt_made vtm_made m_made m32_made mmax_made mgmax_made banks_read mscale_made
            mhi_made matrix_split
            arrived released iota_made oh_made oh_used q_made w_made den_made den2_made rec_made p_made turned_ah turned_p
            turned_x2 agg_made dg_made rd_made ah_made ahT_hi ahT_lo pT_hi pT_lo lin_made xa_made x2_made x2_stored
            st2_made mv2_made std2_made rs2_made rstd2_made xn2_made sraw_made sc_made negm_made exp_made
            m_kept l_made accs_made acc_made x2T_hi x2T_lo xb_made x_loaded2
            best_made wp_made lw_made pooled_made plb_made logits_made lg_made gexp_made chosen
            e_amax_made e_gmax_made e_scales w1_hi w1_lo w2_hi w2_lo b_loaded
            z_made g32_made h_hi h_lo eo_made pre_made act_made y_made y_half x2g_loaded out_stored turn pool_turn""".split()
        s = {n: ctx.enter_context(nc.semaphore(n)) for n in names}
        w_loaded = [ctx.enter_context(nc.semaphore(f"w_loaded{k}")) for k in range(6)]
        e_loaded = [ctx.enter_context(nc.semaphore(f"e_loaded{k}")) for k in range(4)]
        slot_loaded = [ctx.enter_context(nc.semaphore(f"slot_loaded{k}")) for k in range(R)]
        block = ctx.enter_context(nc.Block())

        NCONST = 14

        def lo_parts(n):
            return min(n, 2 * C) + max(0, n - 4 * C)

        def cols(t, w=P):
            return bass.ds(t * P, w)

        def one(a, k):
            return a[:, bass.ds(k, 1), :].rearrange("p a f -> p (a f)")

        def bcast(v, n):
            return v.rearrange("(a n) -> a n", a=1).to_broadcast([P, n])

        @block.sync
        def _(sp):
            def weight(k, w):
                sp.dma_start(raw_w[k], w.rearrange("(a p) f -> p a f", p=P)).then_inc(w_loaded[k], 16)
            weight(0, qkv_w[D:2 * D])
            sp.wait_ge(s["pads_made"], 1)
            for raw, dr in ((raw_dst, dst), (raw_src, src)):
                sp.dma_start(raw[:, 0:FULL, :],
                             dr[0:FULL * P * P].rearrange("(k p e) -> p k e", p=P, e=P)).then_inc(s["edges_loaded"], 16)
                o, last = FULL * P * P, BLOCKS - FULL * P - 1
                sp.dma_start(raw[0:last, FULL, :],
                             dr[o:o + last * P].rearrange("(p e) -> p e", e=P)).then_inc(s["edges_loaded"], 16)
                o += last * P
                sp.dma_start(raw[last:last + 1, FULL, 0:E - o],
                             dr[o:E].rearrange("(p e) -> p e", p=1)).then_inc(s["edges_loaded"], 16)
            with nc.allow_non_contiguous_dma(reason="an edge in 128, 3 KB in all"):
                ends = dst[0:(BLOCKS - 1) * P].rearrange("(r e) -> r e", e=P)[:, P - 1:P]
                sp.dma_start(before[1:P, 0:1], ends[0:P - 1, :]).then_inc(s["edges_loaded"], 16)
                sp.dma_start(before[:, 1:FULL], ends[P - 1:FULL * P - 1, :].rearrange("(k p) e -> p (k e)", p=P)
                             ).then_inc(s["edges_loaded"], 16)
                sp.dma_start(before[0:BLOCKS - FULL * P, FULL:FULL + 1], ends[FULL * P - 1:BLOCKS - 1, :]
                             ).then_inc(s["edges_loaded"], 16)
            for k, w in ((1, qkv_w[0:D]), (4, gw1), (5, gw2), (2, qkv_w[2 * D:3 * D]), (3, proj_w)):
                weight(k, w)

            def rows(i):
                if real(i):
                    after(sp, s["xn_made"], i - XI + 1)
                    sp.sem_inc(s["turn"], 1)
                    after(sp, s["x_loaded"], 16 * i)
                    n = TAIL if isinstance(i, int) and i == T - 1 else P
                    sp.dma_start(xin[0:n, bass.ds(i % XI, 1), :].rearrange("p a f -> p (a f)"),
                                 x[bass.ds(i * P, n), :]).then_inc(s["x_loaded"], 16)
                t = i - 5
                if real(t):
                    n = TAIL if isinstance(t, int) and t == T - 1 else P
                    after(sp, s["hi_made"], t + 1)
                    after(sp, s["lo_made"], t + 1)
                    after(sp, s["table_stored"], 16 * t)
                    sp.dma_start(table[bass.ds(t * P, n), :],
                                 xnhl[0:n, bass.ds(t % XN, 1), :].rearrange("p a f -> p (a f)")
                                 ).then_inc(s["table_stored"], 16)
            for i in range(XI):
                rows(i)
            pipeline(sp, rows, XI, 6, T - 1, T + 5)

            sp.wait_ge(s["firsts_made"], 1)
            passes = sp.value_load(first_i[0:1, T + 1:T + 2], min_val=1, max_val=T)
            with sp.Fori(0, passes) as a:
                with sp.Fori(0, ROUNDS) as g:
                    for k in range(R):
                        sp.wait_ge(slot_loaded[k], (a * ROUNDS + g) * 16 + 16)
                        if k % U == U - 1:
                            sp.sem_inc(s["arrived"], 1)

            sp.wait_ge(s["chosen"], 1)
            for e in range(2):
                v = sp.value_load(topi[0:1, e:e + 1], min_val=0, max_val=NE - 1)
                sp.dma_start(w1raw[:, e], w1[bass.ds(v, 1), :, :].rearrange("a (c p) h -> p (a c) h", p=P)
                             ).then_inc(e_loaded[e], 16)
                sp.dma_start(w2raw[:, e], w2[bass.ds(v, 1), :, :].rearrange("a (c p) o -> p (a c) o", p=P)
                             ).then_inc(e_loaded[2 + e], 16)
                with nc.allow_non_contiguous_dma(reason="a bias per partition, 1 KB in all"):
                    sp.dma_start(b1t[:, e], b1[bass.ds(v, 1), :].rearrange("a (c p) -> p (a c)", p=P)
                                 ).then_inc(s["b_loaded"], 16)
                sp.dma_start(b2b[:, e], b2[bass.ds(v, 1), :].to_broadcast([P, D])).then_inc(s["b_loaded"], 16)

            def group(g):
                whole = not isinstance(g, int) or g < NG
                j = G4 if whole else 1
                after(sp, s["out_stored"], 16 * (g - 1))
                sp.sem_inc(s["turn"], 1)
                after(sp, s["x2g_loaded"], 16 * g)
                sp.dma_start(x2g[:, bass.ds(g % 2, 1), 0:j, :].rearrange("p a j f -> p (a j) f"),
                             x2_dram[bass.ds(g * G4 * P, j * P), :].rearrange("(j p) f -> p j f", p=P)
                             ).then_inc(s["x2g_loaded"], 16)

            def store(g):
                after(sp, s["y_made"], G4 * g + G4)
                sp.dma_start(out[bass.ds(g * G4 * P, G4 * P), :].rearrange("(j p) f -> p j f", p=P),
                             x2g[:, bass.ds(g % 2, 1), :, :].rearrange("p a j f -> p (a j) f")
                             ).then_inc(s["out_stored"], 16)
            sp.wait_ge(s["x2_stored"], 16 * T)
            group(0)
            group(1)
            store(0)
            with sp.Fori(2, NG) as g:
                group(g)
                store(g - 1)
            group(NG)
            store(NG - 1)
            sp.wait_ge(s["y_made"], T)
            body = TAIL // 16 * 16
            sp.dma_start(out[(T - 1) * P:(T - 1) * P + body, :], x2g[0:body, NG % 2, 0, :]).then_inc(s["out_stored"], 16)
            sp.dma_start(out[(T - 1) * P + body:N, :], x2g[body:TAIL, NG % 2, 0, :]).then_inc(s["out_stored"], 16)
            sp.wait_ge(s["out_stored"], 16 * (NG + 2))

        @block.gpsimd
        def _(pool):
            made = [0]

            def link(ins):
                made[0] += 1
                ins.then_inc(s["pool_chain"], 1)
                pool.wait_ge(s["pool_chain"], made[0])

            imp = dict(allow_small_or_imprecise_dtypes=True)
            link(pool.memset(raw_dst[:, FULL, :], FAR))
            link(pool.memset(raw_src[:, FULL, :], 0))
            link(pool.memset(before[:], 0))
            pool.sem_inc(s["pads_made"], 1)
            link(pool.memset(ident[:], 0.0))
            link(pool.affine_select(out=ident[:], in_=ident[:], compare_op=ALU.not_equal, fill=1.0, base=0,
                                    pattern=[[-1, P]], channel_multiplier=1))
            pool.sem_inc(s["ident_made"], 1)
            pool.memset(amax[:], 0.0).then_inc(s["consts"], 1)
            pool.iota(tile_base[:], pattern=[[P, T + 1]], base=0, channel_multiplier=0, **imp).then_inc(s["consts"], 1)
            pool.iota(rowi[:], pattern=[[0, 1]], base=0, channel_multiplier=1, **imp).then_inc(s["consts"], 1)
            link(pool.tensor_copy(ident16[:], ident[:]))
            link(pool.memset(hmask[:], 1.0))
            hm = hmask[:, :].rearrange("p (a c) -> p a c", c=HEAD)
            link(pool.affine_select(out=hm, in_=hm, compare_op=ALU.is_ge, fill=0.0, base=0,
                                    pattern=[[-HEAD, P // HEAD], [0, HEAD]], channel_multiplier=1))
            link(pool.affine_select(out=hm, in_=hm, compare_op=ALU.is_ge, fill=0.0, base=HEAD - 1,
                                    pattern=[[HEAD, P // HEAD], [0, HEAD]], channel_multiplier=-1))
            pool.memset(ones[:], 1.0).then_inc(s["consts"], 1)
            pool.memset(zero16[:], 0.0).then_inc(s["consts"], 1)
            pool.memset(ones16[:], 1.0).then_inc(s["consts"], 1)
            pool.memset(epsc[:], EPS_LN / (SX * SX)).then_inc(s["consts"], 1)
            pool.memset(kacc, 0.0).then_inc(s["consts"], 1)
            pool.iota(iota16[:], pattern=[[1, P]], base=0, channel_multiplier=0, **imp).then_inc(s["consts"], 1)
            pool.iota(uns[:], pattern=[[COLS, T + 1]], base=0, channel_multiplier=0, **imp).then_inc(s["consts"], 1)
            pool.memset(src_col[:], 0).then_inc(s["consts"], 1)
            pool.memset(dst_col[:], -1.0).then_inc(s["consts"], 1)
            pool.memset(sm[:, :], LOW).then_inc(s["consts"], 1)
            pool.memset(lsum[:], 0.0).then_inc(s["consts"], 1)

            for k in range(3):
                pool.wait_ge(s["amax_made"], k + 1)
                pool.partition_all_reduce(gmax[:, k:k + 1], amax[:, k:k + 1], P, RMAX).then_inc(s["gmax_made"], 1)

            def keys(i):
                if real(i):
                    pool.wait_ge(s["khi_made"], i + 1)
                    pool.tensor_tensor(out=one(khl, i % 2)[:, D:2 * D], in0=k32, in1=one(khl, i % 2)[:, 0:D],
                                       op=ALU.subtract).then_inc(s["klo_made"], 1)
                    after(pool, s["kacc_made"], i)
                    pool.tensor_tensor(out=kacc, in0=kacc, in1=k32, op=ALU.add).then_inc(s["kacc_made"], 1)
            pipeline(pool, keys, 0, 1, T, T)

            pool.wait_ge(s["firsts_made"], 1)
            pool.wait_ge(s["cols_made"], 4)
            pool.wait_ge(s["table_stored"], 16 * T)
            pool.wait_ge(s["g_made"], T)
            passes = pool.value_load(first_i[0:1, T + 1:T + 2], min_val=1, max_val=T)

            def gather(it, g, k):
                pool.wait_ge(s["released"], it * RG + k // U + 1)
                pool.tensor_copy(idx_slots[:, k:k + U], src_col[:, bass.ds(g * R + k, U)]
                                 ).then_inc(s["pool_turn"], 1)
                pool.wait_ge(s["pool_turn"], it * RG + k // U + 1)
                pool.sem_inc(s["turn"], 1)
                for n in range(k, k + U):
                    pool.indirect_dma_start(
                        ring[:, n, :], None, table[:, :],
                        bass.IndirectOffsetOnAxis(ap=idx_slots[:, n:n + 1], axis=0)
                    ).then_inc(slot_loaded[n], 16)
            for k in range(0, R, U):
                gather(0, 0, k)
            pool.wait_ge(s["mmax_made"], 1)
            pool.partition_all_reduce(gmax[:, 3:4], amax[:, 3:4], P, RMAX).then_inc(s["mgmax_made"], 1)
            with pool.Fori(1, ROUNDS) as g:
                for k in range(0, R, U):
                    gather(g, g, k)
            with pool.If(passes > 1):
                with pool.Fori(1, passes) as a:
                    with pool.Fori(0, ROUNDS) as g:
                        for k in range(0, R, U):
                            gather(a * ROUNDS + g, g, k)

            pool.wait_ge(s["acc_made"], T)
            pool.wait_ge(s["m_kept"], T)
            pool.partition_all_reduce(gst[:, 0:1], sm[:, 0:1], P, RMAX).then_inc(s["best_made"], 1)
            pool.wait_ge(s["e_amax_made"], 1)
            pool.partition_all_reduce(gmax[:, 4:7], amax[:, 4:7], P, RMAX).then_inc(s["e_gmax_made"], 1)

        @block.tensor
        def _(pe):
            mm = nc.tensor.matmul

            def three(out_, wh, wl, mh, ml, n, first=True, last=True):
                for c in range(n):
                    mm(out_, wh(c), mh(c), start=first and c == 0, stop=False)
                    mm(out_, wh(c), ml(c), start=False, stop=False)
                for c in range(n):
                    r = mm(out_, wl(c), mh(c), start=False, stop=last and c == n - 1)
                return r

            def turn_weight(k):
                pe.wait_ge(w_loaded[k], 16)
                for c in range(C):
                    n = k * C + c
                    after(pe, s["w_hi_made"], n - 3)
                    after(pe, s["w_lo_made"], lo_parts(n - 3))
                    for a in range(C):
                        r = nc.tensor.transpose(bank[n % 4][:, a * P:(a + 1) * P],
                                                raw_w[k][:, a, c * P:(c + 1) * P], ident[:])
                    r.then_inc(s["w_turned"], 1)
            pe.wait_ge(s["ident_made"], 1)
            turn_weight(0)
            pe.wait_ge(s["floats_made"], 2)
            for j, f in enumerate((f_dst, f_src)):
                for k in range(CH):
                    r = nc.tensor.transpose(bank[4 + 2 * j + k // C][:, k % C * P:(k % C + 1) * P], f[:, k, :], ident[:])
                    if k == C - 1 or k == CH - 1:
                        r.then_inc(s["turned_edges"], 1)
            turn_weight(1)
            pe.wait_ge(s["consts"], NCONST)
            pe.wait_ge(s["below_made"], 1)
            pe.wait_ge(s["cols_made"], 1)
            for k in range(CH):
                mm(bank[4][:, 0:T + 1], ones16[:], below[:, k, :], start=(k == 0), stop=(k == CH - 1))
            mm(bank[4][:, T + 1:T + 2], ones16[:], back16[:], start=True, stop=True).then_inc(s["below_summed"], 1)
            for k in range(2, 6):
                turn_weight(k)
            pe.wait_ge(s["w_hi_made"], 6 * C)
            pe.wait_ge(s["w_lo_made"], lo_parts(6 * C))
            pe.wait_ge(s["counts_read"], 1)

            def keys(i):
                t = i + 1
                if real(t):
                    after(pe, s["lo_made"], t + 1)
                    after(pe, s["t_hi_taken"], t)
                    after(pe, s["t_lo_taken"], t)
                    for q in range(2 * C):
                        r = nc.tensor.transpose(ps_t[q // C][:, q % C, :], one(xnhl, t % XN)[:, q * P:(q + 1) * P], ident16[:])
                    r.then_inc(s["t_made"], 1)
                t = i
                if real(t):
                    after(pe, s["t_hi_taken"], t + 1)
                    after(pe, s["t_lo_taken"], t + 1)
                    after(pe, s["k32_made"], t)
                    three(ps_k[:, :], lambda c: xT[:, c, cols(t)], lambda c: xT[:, C + c, cols(t)],
                          lambda c: wk[:, 0, c, :], lambda c: wk[:, 1, c, :], C).then_inc(s["k_made"], 1)
                t = i - 1
                if real(t):
                    pe.wait_ge(s["klo_made"], t + 1)
                    kh, kl, xs = one(khl, t % 2)[:, 0:D], one(khl, t % 2)[:, D:2 * D], one(xnhl, t % XN)
                    st, en = (isinstance(t, int) and t == 0), (isinstance(t, int) and t == T - 1)
                    for c in range(C):
                        mm(bank[c][:, :], xs[:, c * P:(c + 1) * P], kh, start=st, stop=False)
                        mm(bank[c][:, :], xs[:, c * P:(c + 1) * P], kl, start=False, stop=False)
                        r = mm(bank[c][:, :], xs[:, D + c * P:D + (c + 1) * P], kh, start=False, stop=en)
                    r.then_inc(s["g_made"], 1)
            pipeline(pe, keys, -1, 2, T - 4, T + 1)

            pe.sem_inc(s["released"], RG)
            pe.sem_inc(s["oh_used"], OG)

            pe.wait_ge(s["kacc_made"], T)
            for c in range(C):
                mm(bank[6][:, c:c + 1], kacc[:, c * P:(c + 1) * P], ones[:, 0:1], start=True, stop=True)
            mm(bank[7][:, :], ones[:], kacc, start=True, stop=True).then_inc(s["ksum_made"], 1)
            pe.wait_ge(s["gt_hi_copied"], 2)
            pe.wait_ge(s["gt_lo_copied"], 2)
            for j in range(C):
                for c in range(C):
                    r = mm(bank[4][:, j * P:(j + 1) * P], wvT[:, c, j * P:(j + 1) * P], gt32[:, c, j * P:(j + 1) * P],
                           start=(c == 0), stop=(c == C - 1))
            r.then_inc(s["vt_made"], 1)
            pe.wait_ge(s["vtm_made"], 1)
            for j in range(C):
                mm(bank[j][:, :], vtm[:, j, :], pT32[:, j, :], start=True, stop=True).then_inc(s["m_made"], 1)

            agg3 = ps_agg[:, :].rearrange("p (c n) -> p c n", c=C)

            def consume(q, t, skip_lower=None, skip_upper=None):
                pe.wait_ge(s["arrived"], q + 1)
                pe.wait_ge(s["oh_made"], q + t + 1)
                w = onehot[:, bass.ds((q + t) % OG * U, U), :]
                rows = ring[:, bass.ds(q % RG * U, U), :]

                def half(k0, last=False):
                    for k in range(k0, k0 + U // 2):
                        mm(ps_agg[:, :], w[:, k, :], rows[:, k, 0:D], start=False, stop=False, skip_group_check=True)
                        r = mm(ps_agg[:, :], w[:, k, :], rows[:, k, D:2 * D], start=False,
                               stop=last and k == k0 + U // 2 - 1, skip_group_check=True)
                        d = mm(ps_deg[:, 0:1], w[:, k, :], ones16[:, 0:1], start=False, stop=False, skip_group_check=True)
                    return r, d
                if skip_upper is not None:
                    with pe.If(skip_upper < 1):
                        half(U // 2)
                    half(0, last=True)[1].then_inc(s["oh_used"], 1)
                    return
                if skip_lower is None:
                    half(0)
                else:
                    with pe.If(skip_lower < 1):
                        half(0)
                r, d = half(U // 2)
                r.then_inc(s["released"], 1)
                d.then_inc(s["oh_used"], 1)

            def layer(i):
                t = i
                if real(t):
                    if isinstance(t, int) and t == 0:
                        pe.wait_ge(s["banks_read"], 1)
                    a = pe.value_load(first_i[0:1, bass.ds(t, 1)], min_val=0, max_val=GROUPS * T)
                    b = pe.value_load(first_i[0:1, bass.ds(t + 1, 1)], min_val=0, max_val=GROUPS * T)
                    in_upper = pe.value_load(upper[0:1, bass.ds(t, 1)], min_val=0, max_val=1)
                    in_lower = pe.value_load(lower[0:1, bass.ds(t + 1, 1)], min_val=0, max_val=1)
                    after(pe, s["w_made"], t)
                    three(ps_q[:, :], lambda c: xT[:, c, cols(t)], lambda c: xT[:, C + c, cols(t)],
                          lambda c: wq[:, 0, c, :], lambda c: wq[:, 1, c, :], C).then_inc(s["q_made"], 1)
                t = i - 1
                if real(t):
                    after(pe, s["ah_made"], t + 1)
                    after(pe, s["ahT_lo"], t)
                    for c in range(C):
                        r = nc.tensor.transpose(ps_ta[:, c * P:(c + 1) * P], ah32[:, c * P:(c + 1) * P], ident[:])
                    r.then_inc(s["turned_ah"], 1)
                    after(pe, s["p_made"], t + 1)
                    after(pe, s["pT_lo"], t)
                    for c in range(C):
                        r = nc.tensor.transpose(ps_tp[:, c * P:(c + 1) * P], w32[:, c * P:(c + 1) * P], ident[:])
                    r.then_inc(s["turned_p"], 1)
                t = i
                if real(t):
                    after(pe, s["ah_made"], t)
                    after(pe, s["dg_made"], t)
                    mm(agg3, zero16[:], zero16[:, None, :].to_broadcast([P, C, P]), start=True, stop=False, skip_group_check=True)
                    mm(ps_deg[:, 0:1], zero16[:], ones16[:, 0:1], start=True, stop=False, skip_group_check=True)
                    with pe.If(a < b):
                        consume(a, t, skip_lower=in_upper)
                        with pe.If(a + 1 < b):
                            with pe.Fori(a + 1, b) as q:
                                consume(q, t)
                t = i - 1
                if real(t):
                    after(pe, s["x2_made"], t)
                    three(ps_o[:, :], lambda c: xT[:, c, cols(t)], lambda c: xT[:, C + c, cols(t)],
                          lambda c: wg1[:, 0, c, :], lambda c: wg1[:, 1, c, :], C, last=False)
                t = i
                if real(t):
                    consume(b, t, skip_upper=in_lower)
                    mm(ps_deg[:, 0:1], zero16[:], ones16[:, 0:1], start=False, stop=True, skip_group_check=True
                       ).then_inc(s["agg_made"], 1)
                t = i - 1
                if real(t):
                    after(pe, s["ahT_lo"], t + 1)
                    three(ps_o[:, :], lambda c: ahT[:, 0, c, :], lambda c: ahT[:, 1, c, :],
                          lambda c: wg2[:, 0, c, :], lambda c: wg2[:, 1, c, :], C, first=False)
                    after(pe, s["pT_lo"], t + 1)
                    if isinstance(t, int) and t == 0:
                        pe.wait_ge(s["matrix_split"], 1)
                    three(ps_b[:, :], lambda c: pT[:, 0, c, :], lambda c: pT[:, 1, c, :],
                          lambda c: wm[:, 0, c, :], lambda c: wm[:, 1, c, :], C).then_inc(s["lin_made"], 1)
                t = i - 2
                if real(t):
                    after(pe, s["xn2_made"], t + 1)
                    after(pe, s["x2T_lo"], t)
                    for c in range(C):
                        r = nc.tensor.transpose(ps_tx[:, c * P:(c + 1) * P], xn2[:, c * P:(c + 1) * P], ident[:])
                    r.then_inc(s["turned_x2"], 1)
            pipeline(pe, layer, 0, 3, T, T + 2)

            pe.wait_ge(s["wp_made"], 1)
            pe.wait_ge(s["lw_made"], 1)
            for c in range(C):
                mm(bank[0][:, c:c + 1], acc[:, c * P:(c + 1) * P], wp[:], start=True, stop=True)
            mm(bank[0][:, C:C + 1], ones[:], lw[:], start=True, stop=True).then_inc(s["pooled_made"], 1)
            pe.wait_ge(s["plb_made"], 1)
            for c in range(C):
                r = mm(bank[1][:, 0:NE], plb[:, c, :], gwt[:, c, :], start=(c == 0), stop=(c == C - 1))
            r.then_inc(s["logits_made"], 1)

            pe.wait_ge(s["w1_hi"], 1)
            pe.wait_ge(s["w1_lo"], 1)
            pe.wait_ge(s["w2_hi"], 1)
            pe.wait_ge(s["w2_lo"], 1)
            pe.wait_ge(s["x2T_lo"], T)

            def hidden(g, n):
                for b in range(2 * HC):
                    e, hc = b // HC, b % HC
                    after(pe, s["g32_made"], 2 * HC * g - 2 * HC + b + 1)
                    three(bank[b][:, 0:n], lambda c: w1s[:, 0, e, c, hc * P:(hc + 1) * P],
                          lambda c: w1s[:, 1, e, c, hc * P:(hc + 1) * P],
                          lambda c: xT[:, c, bass.ds(g * G4 * P, n)],
                          lambda c: xT[:, C + c, bass.ds(g * G4 * P, n)], C).then_inc(s["z_made"], 1)

            def outs(g, tiles):
                after(pe, s["h_lo"], 2 * HC * g + 2 * HC)
                for j in range(tiles):
                    for e in range(2):
                        after(pe, s["pre_made"], 2 * (G4 * g + j) - 4 + e + 1)
                        hh = hT[:, bass.ds(g % 2, 1)].rearrange("p b a e c n -> p (b a) e c n")
                        three(bank[4 + 2 * (j % 2) + e][:, :],
                              lambda c: hh[:, 0, e, c, j * P:(j + 1) * P], lambda c: hh[:, 1, e, c, j * P:(j + 1) * P],
                              lambda c: w2s[:, 0, e, c, :], lambda c: w2s[:, 1, e, c, :], HC).then_inc(s["eo_made"], 1)
            hidden(0, G4 * P)
            hidden(1, G4 * P)
            outs(0, G4)
            with pe.Fori(2, NG) as g:
                hidden(g, G4 * P)
                outs(g - 1, G4)
            hidden(NG, P)
            outs(NG - 1, G4)
            outs(NG, 1)

        @block.scalar
        def _(act):
            F = nc.scalar.activation
            made = [0]

            def link(ins):
                made[0] += 1
                ins.then_inc(s["act_chain"], 1)
                act.wait_ge(s["act_chain"], made[0])

            act.dma_start(biasb[:], bcast(gb1, D)).then_inc(s["biases_loaded"], 16)
            act.dma_start(bias2[:, 0], bcast(gb2, D)).then_inc(s["biases_loaded"], 16)
            act.dma_start(bias3[:, 0], bcast(proj_b, D)).then_inc(s["biases_loaded"], 16)
            act.dma_start(awb[:], attn_w.rearrange("(a n) b -> a (n b)", a=1).to_broadcast([P, D])
                          ).then_inc(s["small_loaded"], 16)
            act.dma_start(abb[:], bcast(attn_b, 1)).then_inc(s["small_loaded"], 16)
            act.dma_start(gbb[:], bcast(gate_b, NE)).then_inc(s["small_loaded"], 16)
            act.dma_start(gwt[:], gate_w.rearrange("(c p) e -> p c e", p=P)).then_inc(s["small_loaded"], 16)

            def split_weight(k, out_, scales, col):
                after(act, s["scales_made"], scales)
                for c in range(C):
                    n = k * C + c
                    act.wait_ge(s["w_turned"], n + 1)
                    if col is None:
                        F(out_[:, c, :], bank[n % 4][:, :], ACT.Copy).then_inc(s["w_hi_made"], 1)
                    else:
                        F(out_[:, 0, c, :], bank[n % 4][:, :], ACT.Copy, scale=scale[:, col:col + 1]
                          ).then_inc(s["w_hi_made"], 1)
            split_weight(0, wk, 1, K_)
            act.wait_ge(s["edges_loaded"], 144)
            F(f_dst, raw_dst, ACT.Copy).then_inc(s["floats_made"], 1)
            F(f_src, raw_src, ACT.Copy).then_inc(s["floats_made"], 1)
            act.wait_ge(s["consts"], NCONST)
            for j, col in enumerate((dst_col, src_col)):
                for h in range(2):
                    w = min(C * P, BLOCKS - h * C * P)
                    act.wait_ge(s["turned_edges"], 2 * j + h + 1)
                    F(col[:, 1 + h * C * P:1 + h * C * P + w], bank[4 + 2 * j + h][:, 0:w], ACT.Copy
                      ).then_inc(s["cols_made"], 1)
            split_weight(1, wq, 2, Q_)
            split_weight(2, wvT, 0, None)
            split_weight(3, pT32, 0, None)
            def keys(i):
                t = i + 1
                if real(t):
                    after(act, s["t_made"], t + 1)
                    F(xT[:, 0:C, cols(t)], ps_t[0], ACT.Copy).then_inc(s["t_hi_taken"], 1)
                t = i + 3
                if real(t):
                    after(act, s["xn_made"], t + 1)
                    after(act, s["g_made"], t - XN + 1)
                    after(act, s["table_stored"], 16 * (t - XN + 1))
                    F(one(xnhl, t % XN)[:, 0:D], one(xn32, t % 2), ACT.Copy).then_inc(s["hi_made"], 1)
                t = i + 4
                if real(t):
                    after(act, s["mv_made"], t + 1)
                    after(act, s["rs_made"], t)
                    F(std[:], mv[:, 1:2], ACT.Sqrt, bias=epsc[:], scale=1.0 / (SX * SX)).then_inc(s["std_made"], 1)
                t = i
                if real(t):
                    after(act, s["k32_made"], t + 1)
                    after(act, s["g_made"], t - 1)
                    F(one(khl, t % 2)[:, 0:D], k32, ACT.Copy).then_inc(s["khi_made"], 1)
            keys(-4)
            split_weight(4, wg1, 3, W_)
            keys(-3)
            split_weight(5, wg2, 3, W_)
            keys(-2)
            pipeline(act, keys, -1, 2, T - 4, T)

            act.wait_ge(s["g_made"], T)
            for c in range(2):
                F(gt32[:, c, :], bank[c][:, :], ACT.Copy).then_inc(s["gt_hi_copied"], 1)
            def layer(i):
                t = i - 3
                if real(t):
                    after(act, s["turned_x2"], t + 1)
                    F(xT[:, 0:C, cols(t)], ps_tx[:, :].rearrange("p (c n) -> p c n", c=C), ACT.Copy).then_inc(s["x2T_hi"], 1)
                t = i - 2
                if real(t):
                    after(act, s["mv2_made"], t + 1)
                    after(act, s["rs2_made"], t)
                    F(std[:], mv[:, 1:2], ACT.Sqrt, bias=epsc[:], scale=1.0 / (SX * SX)).then_inc(s["std2_made"], 1)
                t = i - 1
                if real(t):
                    after(act, s["turned_ah"], t + 1)
                    F(ahT[:, 0], ps_ta[:, :].rearrange("p (c n) -> p c n", c=C), ACT.Copy).then_inc(s["ahT_hi"], 1)
                    after(act, s["turned_p"], t + 1)
                    F(pT[:, 0], ps_tp[:, :].rearrange("p (c n) -> p c n", c=C), ACT.Copy, scale=SP_).then_inc(s["pT_hi"], 1)
                t = i - 2
                if real(t):
                    after(act, s["negm_made"], t + 1)
                    F(e2[:], sm[:], ACT.Exp, bias=negm[:]).then_inc(s["exp_made"], 1)
                    after(act, s["exp_made"], t + 1)
                    after(act, s["acc_made"], t)
                    F(accs, acc, ACT.Copy, scale=e2[:, 0:1]).then_inc(s["accs_made"], 1)
                    after(act, s["x2_stored"], 16 * t)
                    after(act, s["x2_made"], t + 1)
                    act.dma_start(x2_dram[bass.ds(t * P, P), :], x2).then_inc(s["x2_stored"], 16)
                t = i
                if real(t):
                    n = TAIL if isinstance(t, int) and t == T - 1 else P
                    if not isinstance(t, int) or t > 0:
                        after(act, s["xb_made"], t)
                        after(act, s["x_loaded2"], 16 * t)
                        act.dma_start(x_in[0:n, :], x[bass.ds(t * P, n), :]).then_inc(s["x_loaded2"], 16)
                    after(act, s["rd_made"], t + 1)
                    F(ah32, ps_agg[:, :], ACT.Copy, scale=rd[:]).then_inc(s["ah_made"], 1)
            layer(0)
            act.wait_ge(s["mscale_made"], 1)
            for c in range(C):
                r = F(wm[:, 0, c, :], m32[:, c, :], ACT.Copy, scale=scale[:, M_:M_ + 1])
            r.then_inc(s["mhi_made"], 1)
            act.wait_ge(s["matrix_split"], 1)
            act.dma_start(x_in, x[0:P, :]).then_inc(s["x_loaded2"], 16)
            pipeline(act, layer, 1, 4, T - 1, T + 3)

            act.wait_ge(s["best_made"], 2)
            F(wp[:], sm[:, 0:1], ACT.Exp, bias=gst[:, 1:2]).then_inc(s["wp_made"], 1)
            act.wait_ge(s["lg_made"], 1)
            F(gts[:], lg[:], ACT.Exp, bias=gst[:, 2:3]).then_inc(s["gexp_made"], 1)

            act.wait_ge(s["e_scales"], 1)
            F(w1s[:, 0], w1raw, ACT.Copy, scale=scale[:, W1_:W1_ + 1]).then_inc(s["w1_hi"], 1)
            F(w2s[:, 0], w2raw, ACT.Copy, scale=scale[:, W2_:W2_ + 1]).then_inc(s["w2_hi"], 1)
            act.wait_ge(s["b_loaded"], 64)

            def hidden(g, n):
                for b in range(2 * HC):
                    e, hc = b // HC, b % HC
                    after(act, s["z_made"], 2 * HC * g + b + 1)
                    after(act, s["h_lo"], 2 * HC * g - 2 * HC + b + 1)
                    F(g32[:, b, 0:n], bank[b][:, 0:n], ACT.Gelu, bias=b1t[:, e, hc:hc + 1], scale=mix[:, 3:4]
                      ).then_inc(s["g32_made"], 1)
                    after(act, s["g32_made"], 2 * HC * g + b + 1)
                    after(act, s["eo_made"], 2 * G4 * g - 2 * G4)
                    hh = hT[:, bass.ds(g % 2, 1)].rearrange("p b a e c n -> p (b a) e c n")
                    F(hh[:, 0, e, hc, 0:n], g32[:, b, 0:n], ACT.Copy, scale=scale[:, HB_:HB_ + 1]).then_inc(s["h_hi"], 1)

            def outs(g, tiles):
                for j in range(tiles):
                    for e in range(2):
                        m = 2 * (G4 * g + j) + e
                        after(act, s["pre_made"], m + 1)
                        after(act, s["y_half"], m - 3)
                        F(act2[:, j % 2, e], pre[:, j % 2, e], ACT.Gelu).then_inc(s["act_made"], 1)
            hidden(0, G4 * P)
            hidden(1, G4 * P)
            outs(0, G4)
            with act.Fori(2, NG) as g:
                hidden(g, G4 * P)
                outs(g - 1, G4)
            hidden(NG, P)
            outs(NG - 1, G4)
            outs(NG, 1)

        @block.vector
        def _(dve):
            V = nc.vector
            made = [0]

            def link(ins):
                made[0] += 1
                ins.then_inc(s["dve_chain"], 1)
                dve.wait_ge(s["dve_chain"], made[0])

            def powers(a, b, sw=SW):
                link(V.tensor_scalar(gmax[:, a:b], gmax[:, a:b], 1e-30, None, ALU.max))
                link(V.tensor_scalar(pow2[:, a:b].bitcast(I32), gmax[:, a:b].bitcast(I32), 0x7F800000, None,
                                     ALU.bitwise_and))
                link(V.reciprocal(scale[:, a:b], pow2[:, a:b]))
                link(V.tensor_scalar(scale[:, a:b], scale[:, a:b], sw, None, ALU.mult))
                link(V.tensor_scalar(undo[:, a:b], pow2[:, a:b], 1.0 / sw, None, ALU.mult))

            def largest(k, col):
                dve.wait_ge(w_loaded[k], 16)
                link(V.tensor_reduce(amax[:, col:col + 1], raw_w[k], AX.XY, ALU.max, apply_absolute_value=True))

            def lo_part(k, w, col):
                for c in range(C):
                    n = k * C + c
                    dve.wait_ge(s["w_hi_made"], n + 1)
                    V.scalar_tensor_tensor(out=w[:, 1, c, :], in0=bank[n % 4][:, :], scalar=scale[:, col:col + 1],
                                           in1=w[:, 0, c, :], op0=ALU.mult, op1=ALU.subtract).then_inc(s["w_lo_made"], 1)
            dve.wait_ge(s["ident_made"], 1)
            dve.wait_ge(s["consts"], 3)
            largest(0, K_)
            dve.sem_inc(s["amax_made"], 1)
            dve.wait_ge(s["biases_loaded"], 48)
            link(V.tensor_tensor(bias2[:, 0], bias2[:, 0], bias3[:, 0], ALU.add))
            link(V.tensor_tensor(biasb[:], biasb[:], bias2[:, 0], ALU.add))
            dve.wait_ge(s["gmax_made"], 1)
            powers(K_, K_ + 1)
            dve.sem_inc(s["scales_made"], 1)
            lo_part(0, wk, K_)
            dve.wait_ge(s["edges_loaded"], 144)
            V.tensor_tensor(below, raw_dst[:, :, P - 1:P].to_broadcast([P, CH, T + 1]),
                            tile_base[:, None, :].to_broadcast([P, CH, T + 1]), ALU.is_lt)
            V.tensor_tensor(steps[:, :, 0:1], raw_dst[:, :, 0:1], before[:, :, None], ALU.subtract)
            link(V.tensor_tensor(steps[:, :, 1:P], raw_dst[:, :, 1:P], raw_dst[:, :, 0:P - 1], ALU.subtract))
            link(V.tensor_reduce(least[:, 0:1], steps, AX.XY, ALU.min))
            link(V.tensor_scalar(back16[:], least[:, 0:1], 0.0, None, ALU.is_lt))
            dve.sem_inc(s["below_made"], 1)
            largest(1, Q_)
            dve.sem_inc(s["amax_made"], 1)
            largest(4, W_)
            dve.wait_ge(s["gmax_made"], 2)
            powers(Q_, Q_ + 1)
            dve.sem_inc(s["scales_made"], 1)
            largest(5, 7)
            link(V.tensor_tensor(amax[:, W_:W_ + 1], amax[:, W_:W_ + 1], amax[:, 7:8], ALU.max))
            dve.sem_inc(s["amax_made"], 1)
            lo_part(1, wq, Q_)
            dve.wait_ge(s["gmax_made"], 3)
            powers(W_, W_ + 1)
            dve.sem_inc(s["scales_made"], 1)
            link(V.tensor_scalar(rowmask[:], rowi[:], float(TAIL), None, ALU.is_lt))
            link(V.tensor_scalar(rowlow[:], rowmask[:], -LOW, LOW, ALU.mult, ALU.add))

            def keys(i):
                t = i + 1
                if real(t):
                    after(dve, s["t_made"], t + 1)
                    V.tensor_copy(xT[:, C:2 * C, cols(t)], ps_t[1]).then_inc(s["t_lo_taken"], 1)
                t = i + 3
                if real(t):
                    after(dve, s["std_made"], t + 1)
                    V.reciprocal(rs0[:], std[:]).then_inc(s["rs_made"], 1)
                    after(dve, s["rs_made"], t + 1)
                    m = rowmask[:] if isinstance(t, int) and t == T - 1 else ones[:, 0:1]
                    V.tensor_scalar(rstd[:], rs0[:], m, None, ALU.mult).then_inc(s["rstd_made"], 1)
                    after(dve, s["rstd_made"], t + 1)
                    after(dve, s["hi_made"], t - 1)
                    V.tensor_scalar(one(xn32, t % 2), one(xin, t % XI), mv[:, 0:1], rstd[:],
                                    ALU.subtract, ALU.mult).then_inc(s["xn_made"], 1)
                t = i + 2
                if real(t):
                    after(dve, s["hi_made"], t + 1)
                    V.tensor_tensor(one(xnhl, t % XN)[:, D:2 * D], one(xn32, t % 2), one(xnhl, t % XN)[:, 0:D],
                                    ALU.subtract).then_inc(s["lo_made"], 1)
                t = i + 4
                if real(t):
                    after(dve, s["x_loaded"], 16 * t + 16)
                    V.bn_stats(st6[:], one(xin, t % XI)).then_inc(s["stats_made"], 1)
                    after(dve, s["stats_made"], t + 1)
                    after(dve, s["xn_made"], t)
                    dve.sem_inc(s["turn"], 1)
                    V.bn_aggr(mv[:], st6[:]).then_inc(s["mv_made"], 1)
                t = i
                if real(t):
                    after(dve, s["k_made"], t + 1)
                    after(dve, s["kacc_made"], t)
                    V.tensor_scalar(k32, ps_k[:, :], SK, 0.0, ALU.mult, ALU.max).then_inc(s["k32_made"], 1)
            keys(-4)
            lo_part(4, wg1, W_)
            keys(-3)
            lo_part(5, wg2, W_)
            keys(-2)
            dve.wait_ge(s["consts"], NCONST)
            dve.wait_ge(s["below_summed"], 1)
            link(V.tensor_copy(firsts[:], bank[4][:, 0:T + 1]))
            link(V.tensor_scalar(firsts[:, 1:T + 1], firsts[:, 1:T + 1], 1.0, None, ALU.add))
            link(V.tensor_scalar(unsorted[:], bank[4][:, T + 1:T + 2], 0.0, None, ALU.is_gt))
            dve.sem_inc(s["counts_read"], 1)
            pipeline(dve, keys, -1, 2, T - 4, T)
            link(V.tensor_scalar(uns[:], uns[:], float(COLS * T - 1), None, ALU.min))
            link(V.tensor_tensor(uns[:], uns[:], firsts[:], ALU.subtract))
            link(V.scalar_tensor_tensor(out=first_i[:, 0:T + 1], in0=uns[:], scalar=unsorted[:], in1=firsts[:],
                                        op0=ALU.mult, op1=ALU.add))
            link(V.tensor_scalar(upper[:], first_i[:, 0:T + 1], U.bit_length() - 2, 1, ALU.arith_shift_right,
                                 ALU.bitwise_and))
            link(V.tensor_scalar(lower[:], upper[:], 1, None, ALU.bitwise_xor))
            link(V.tensor_scalar(first_i[:, 0:T + 1], first_i[:, 0:T + 1], U.bit_length() - 1, None,
                                 ALU.arith_shift_right))
            link(V.tensor_scalar(first_i[:, T + 1:T + 2], unsorted[:], float(T - 1), 1.0, ALU.mult, ALU.add))
            dve.sem_inc(s["firsts_made"], 1)


            dve.wait_ge(s["g_made"], T)
            for c in (2, 3):
                V.tensor_copy(gt32[:, c, :], bank[c][:, :]).then_inc(s["gt_lo_copied"], 1)
            dve.wait_ge(s["ksum_made"], 1)
            link(V.tensor_scalar(kinv[:], bank[6][:, 0:C], 1e-30, None, ALU.max))
            link(V.reciprocal(kinv[:], kinv[:]))
            link(V.tensor_scalar(kinv[:], kinv[:], 1.0 / SX, None, ALU.mult))
            link(V.tensor_tensor(mix[:, 0:1], undo[:, K_:K_ + 1], undo[:, Q_:Q_ + 1], ALU.mult))
            link(V.tensor_scalar(mix[:, 0:1], mix[:, 0:1], 1.0 / (SX * SX * SK), None, ALU.mult))
            link(V.tensor_scalar(ksb[:], bank[7][:, :], mix[:, 0:1], None, ALU.mult))
            link(V.tensor_scalar(mix[:, 1:2], undo[:, W_:W_ + 1], 1.0 / SX, None, ALU.mult))
            dve.wait_ge(s["vt_made"], 1)
            V.tensor_tensor(vtm, bank[4][:, :].rearrange("p (a f) -> p a f", a=C),
                            hmask[:, None, :].to_broadcast([P, C, P]), ALU.mult).then_inc(s["vtm_made"], 1)
            for j in range(C):
                dve.wait_ge(s["m_made"], j + 1)
                link(V.tensor_scalar(m32[:, j, :], bank[j][:, :], kinv[:, j:j + 1], None, ALU.mult))
            dve.sem_inc(s["banks_read"], 1)
            link(V.tensor_reduce(amax[:, M_:M_ + 1], m32, AX.XY, ALU.max, apply_absolute_value=True))
            dve.sem_inc(s["mmax_made"], 1)
            def layer(i):
                t = i
                if real(t):
                    a = dve.value_load(first_i[0:1, bass.ds(t, 1)], min_val=0, max_val=GROUPS * T)
                    b = dve.value_load(first_i[0:1, bass.ds(t + 1, 1)], min_val=0, max_val=GROUPS * T)
                    V.tensor_scalar(iota_t[:], iota16[:], tile_base[:, bass.ds(t, 1)], None, ALU.add
                                    ).then_inc(s["iota_made"], 1)
                    after(dve, s["iota_made"], t + 1)
                    dve.sem_inc(s["turn"], 1)
                    with dve.Fori(a, b + 1) as q:
                        dve.wait_ge(s["oh_used"], q + t + 1)
                        V.tensor_tensor(onehot[:, bass.ds((q + t) % OG * U, U), :],
                                        iota_t[:, None, :].to_broadcast([P, U, P]),
                                        dst_col[:, bass.ds(q % GROUPS * U, U), None].to_broadcast([P, U, P]),
                                        ALU.is_equal).then_inc(s["oh_made"], 1)
                t = i - 3
                if real(t):
                    after(dve, s["x2T_hi"], t + 1)
                    V.tensor_tensor(xT[:, C:2 * C, cols(t)], ps_tx[:, :].rearrange("p (c n) -> p c n", c=C),
                                    xT[:, 0:C, cols(t)], ALU.subtract).then_inc(s["x2T_lo"], 1)
                t = i - 2
                if real(t):
                    after(dve, s["lin_made"], t + 1)
                    after(dve, s["x2_stored"], 16 * t)
                    after(dve, s["xb_made"], t + 1)
                    V.scalar_tensor_tensor(out=x2, in0=ps_o[:, :], scalar=mix[:, 1:2], in1=xb,
                                           op0=ALU.mult, op1=ALU.add).then_inc(s["xa_made"], 1)
                    after(dve, s["xa_made"], t + 1)
                    V.scalar_tensor_tensor(out=x2, in0=ps_b[:, :], scalar=mix[:, 2:3], in1=x2,
                                           op0=ALU.mult, op1=ALU.add).then_inc(s["x2_made"], 1)
                    after(dve, s["x2_made"], t + 1)
                    V.bn_stats(st6[:], x2).then_inc(s["st2_made"], 1)
                    after(dve, s["st2_made"], t + 1)
                    dve.sem_inc(s["turn"], 1)
                    V.bn_aggr(mv[:], st6[:]).then_inc(s["mv2_made"], 1)
                t = i - 1
                if real(t):
                    after(dve, s["ahT_hi"], t + 1)
                    V.tensor_tensor(ahT[:, 1], ps_ta[:, :].rearrange("p (c n) -> p c n", c=C), ahT[:, 0],
                                    ALU.subtract).then_inc(s["ahT_lo"], 1)
                    after(dve, s["pT_hi"], t + 1)
                    V.scalar_tensor_tensor(out=pT[:, 1], in0=ps_tp[:, :].rearrange("p (c n) -> p c n", c=C),
                                           scalar=SP_, in1=pT[:, 0], op0=ALU.mult, op1=ALU.subtract
                                           ).then_inc(s["pT_lo"], 1)
                t = i - 2
                if real(t):
                    after(dve, s["std2_made"], t + 1)
                    V.reciprocal(rstd[:], std[:]).then_inc(s["rs2_made"], 1)
                    after(dve, s["rs2_made"], t + 1)
                    after(dve, s["turned_x2"], t)
                    V.tensor_scalar(xn2, x2, mv[:, 0:1], rstd[:], ALU.subtract, ALU.mult).then_inc(s["xn2_made"], 1)
                    after(dve, s["xn2_made"], t + 1)
                    V.scalar_tensor_tensor(out=accs, in0=xn2, scalar=1.0 / SX, in1=awb[:], op0=ALU.mult, op1=ALU.mult,
                                           accum_out=sraw[:]).then_inc(s["sraw_made"], 1)
                    after(dve, s["sraw_made"], t + 1)
                    after(dve, s["m_kept"], t)
                    V.tensor_scalar(sm[:, 1:2], sraw[:], abb[:], None, ALU.add).then_inc(s["sc_made"], 1)
                    if isinstance(t, int) and t == T - 1:
                        dve.wait_ge(s["sc_made"], t + 1)
                        link(V.tensor_tensor(sm[:, 1:2], sm[:, 1:2], rowmask[:], ALU.mult))
                        link(V.tensor_tensor(sm[:, 1:2], sm[:, 1:2], rowlow[:], ALU.add))
                    after(dve, s["sc_made"], t + 1)
                    V.tensor_reduce(negm[:], sm[:], AX.X, ALU.max, negate=True).then_inc(s["negm_made"], 1)
                t = i
                if real(t):
                    after(dve, s["q_made"], t + 1)
                    after(dve, s["turned_p"], t)
                    V.scalar_tensor_tensor(out=w32, in0=ps_q[:, :], scalar=0.0, in1=ksb[:], op0=ALU.max,
                                           op1=ALU.mult).then_inc(s["w_made"], 1)
                    after(dve, s["w_made"], t + 1)
                    V.tensor_reduce(den[:], w32.rearrange("p (h c) -> p h c", c=HEAD), AX.X, ALU.add
                                    ).then_inc(s["den_made"], 1)
                    after(dve, s["den_made"], t + 1)
                    V.tensor_scalar(den2[:], den[:], EPS_ATT, None, ALU.add).then_inc(s["den2_made"], 1)
                    after(dve, s["den2_made"], t + 1)
                    V.reciprocal(den[:], den2[:]).then_inc(s["rec_made"], 1)
                    after(dve, s["rec_made"], t + 1)
                    w3 = w32.rearrange("p (h c) -> p h c", c=HEAD)
                    V.tensor_tensor(w3, w3, den[:, :, None].to_broadcast([P, D // HEAD, HEAD]), ALU.mult
                                    ).then_inc(s["p_made"], 1)
                t = i - 2
                if real(t):
                    after(dve, s["accs_made"], t + 1)
                    V.tensor_scalar(sm[:, 0:1], negm[:], -1.0, None, ALU.mult).then_inc(s["m_kept"], 1)
                    after(dve, s["l_made"], t)
                    V.scalar_tensor_tensor(out=lsum[:], in0=lsum[:], scalar=e2[:, 0:1], in1=e2[:, 1:2],
                                           op0=ALU.mult, op1=ALU.add).then_inc(s["l_made"], 1)
                    V.scalar_tensor_tensor(out=acc, in0=xn2, scalar=e2[:, 1:2], in1=accs,
                                           op0=ALU.mult, op1=ALU.add).then_inc(s["acc_made"], 1)
                t = i - 1
                if real(t):
                    after(dve, s["x_loaded2"], 16 * t + 16)
                    V.tensor_tensor(xb, x_in, biasb[:], ALU.add).then_inc(s["xb_made"], 1)
                t = i
                if real(t):
                    after(dve, s["agg_made"], t + 1)
                    V.tensor_scalar(dg[:], ps_deg[:, 0:1], 1.0, None, ALU.max).then_inc(s["dg_made"], 1)
                    after(dve, s["dg_made"], t + 1)
                    V.reciprocal(rd[:], dg[:]).then_inc(s["rd_made"], 1)
            layer(0)
            dve.wait_ge(s["mgmax_made"], 1)
            powers(M_, M_ + 1)
            link(V.tensor_scalar(mix[:, 2:3], undo[:, M_:M_ + 1], 1.0 / SP_, None, ALU.mult))
            dve.sem_inc(s["mscale_made"], 1)
            dve.wait_ge(s["mhi_made"], 1)
            for c in range(C):
                r = V.scalar_tensor_tensor(out=wm[:, 1, c, :], in0=m32[:, c, :], scalar=scale[:, M_:M_ + 1],
                                           in1=wm[:, 0, c, :], op0=ALU.mult, op1=ALU.subtract)
            link(r)
            link(V.memset(acc, 0.0))
            dve.sem_inc(s["matrix_split"], 1)
            pipeline(dve, layer, 1, 4, T, T + 3)

            dve.wait_ge(s["best_made"], 1)
            link(V.tensor_scalar(gst[:, 1:2], gst[:, 0:1], -1.0, None, ALU.mult))
            dve.sem_inc(s["best_made"], 1)
            dve.wait_ge(s["wp_made"], 1)
            dve.wait_ge(s["l_made"], T)
            V.tensor_tensor(lw[:], lsum[:], wp[:], ALU.mult).then_inc(s["lw_made"], 1)
            dve.wait_ge(s["pooled_made"], 1)
            link(V.tensor_copy(pld[:, 0:C + 1], bank[0][:, 0:C + 1]))
            link(V.reciprocal(pld[:, 5:6], pld[:, C:C + 1]))
            link(V.tensor_scalar(pld[:, 5:6], pld[:, 5:6], 1.0 / SX, None, ALU.mult))
            link(V.tensor_scalar(pld[:, 0:C], pld[:, 0:C], pld[:, 5:6], None, ALU.mult))
            link(V.tensor_copy(plb, pld[:, 0:C, None].to_broadcast([P, C, P])))
            dve.wait_ge(s["small_loaded"], 64)
            dve.sem_inc(s["plb_made"], 1)
            dve.wait_ge(s["logits_made"], 1)
            link(V.tensor_tensor(lg[:], bank[1][:, 0:NE], gbb[:], ALU.add))
            link(V.tensor_reduce(gst[:, 2:3], lg[:], AX.X, ALU.max, negate=True))
            dve.sem_inc(s["lg_made"], 1)
            dve.wait_ge(s["gexp_made"], 1)
            link(V.tensor_reduce(gst[:, 3:4], gts[:], AX.X, ALU.add))
            link(V.reciprocal(gst[:, 4:5], gst[:, 3:4]))
            link(V.tensor_scalar(gts[:], gts[:], gst[:, 4:5], None, ALU.mult))
            link(V.max(top[:], gts[:]))
            link(V.max_index(topi[:], top[:], gts[:]))
            dve.sem_inc(s["chosen"], 1)
            link(V.tensor_tensor(gst[:, 5:6], top[:, 0:1], top[:, 1:2], ALU.add))
            link(V.tensor_scalar(gst[:, 5:6], gst[:, 5:6], EPS_GATE, None, ALU.add))
            link(V.reciprocal(gst[:, 6:7], gst[:, 5:6]))
            link(V.tensor_scalar(gexp[:], top[:, 0:2], gst[:, 6:7], None, ALU.mult))

            dve.wait_ge(s["x2_stored"], 16 * T)
            for k in range(4):
                dve.wait_ge(e_loaded[k], 16)
            dve.wait_ge(s["b_loaded"], 64)
            V.tensor_reduce(amax[:, W1_:W1_ + 1], w1raw.rearrange("p e c h -> p (e c h)"), AX.X, ALU.max, apply_absolute_value=True)
            V.tensor_reduce(amax[:, HB_:HB_ + 1], b1t[:], AX.XY, ALU.max, apply_absolute_value=True)
            link(V.tensor_reduce(amax[:, W2_:W2_ + 1], w2raw.rearrange("p e c o -> p (e c o)"), AX.X, ALU.max, apply_absolute_value=True))
            dve.sem_inc(s["e_amax_made"], 1)
            dve.wait_ge(s["e_gmax_made"], 1)
            link(V.scalar_tensor_tensor(out=gmax[:, HB_:HB_ + 1], in0=gmax[:, W1_:W1_ + 1], scalar=float(D),
                                        in1=gmax[:, HB_:HB_ + 1], op0=ALU.mult, op1=ALU.add))
            powers(4, 7)
            link(V.tensor_scalar(mix[:, 3:4], undo[:, W1_:W1_ + 1], 1.0 / SX, None, ALU.mult))
            link(V.tensor_tensor(mix[:, 4:5], undo[:, HB_:HB_ + 1], undo[:, W2_:W2_ + 1], ALU.mult))
            dve.sem_inc(s["e_scales"], 1)
            dve.wait_ge(s["w1_hi"], 1)
            flat1, flat2 = "p e c h -> p (e c h)", "p e c o -> p (e c o)"
            V.scalar_tensor_tensor(out=w1s[:, 1].rearrange(flat1), in0=w1raw.rearrange(flat1),
                                   scalar=scale[:, W1_:W1_ + 1], in1=w1s[:, 0].rearrange(flat1),
                                   op0=ALU.mult, op1=ALU.subtract).then_inc(s["w1_lo"], 1)
            dve.wait_ge(s["w2_hi"], 1)
            V.scalar_tensor_tensor(out=w2s[:, 1].rearrange(flat2), in0=w2raw.rearrange(flat2),
                                   scalar=scale[:, W2_:W2_ + 1], in1=w2s[:, 0].rearrange(flat2),
                                   op0=ALU.mult, op1=ALU.subtract).then_inc(s["w2_lo"], 1)

            def hidden(g, n):
                for b in range(2 * HC):
                    e, hc = b // HC, b % HC
                    after(dve, s["h_hi"], 2 * HC * g + b + 1)
                    hh = hT[:, bass.ds(g % 2, 1)].rearrange("p b a e c n -> p (b a) e c n")
                    V.scalar_tensor_tensor(out=hh[:, 1, e, hc, 0:n], in0=g32[:, b, 0:n], scalar=scale[:, HB_:HB_ + 1],
                                           in1=hh[:, 0, e, hc, 0:n], op0=ALU.mult, op1=ALU.subtract
                                           ).then_inc(s["h_lo"], 1)

            def outs(g, tiles):
                def add(j):
                    y = x2g[:, bass.ds(g % 2, 1), j, :].rearrange("p a f -> p (a f)")
                    if j == 0:
                        after(dve, s["x2g_loaded"], 16 * g + 16)
                    for e in range(2):
                        m = 2 * (G4 * g + j) + e
                        after(dve, s["act_made"], m + 1)
                        after(dve, s["y_half"], m)
                        r = V.scalar_tensor_tensor(out=y, in0=act2[:, j % 2, e], scalar=gexp[:, e:e + 1], in1=y,
                                                   op0=ALU.mult, op1=ALU.add)
                        r.then_inc(s["y_half"], 1)
                    after(dve, s["y_half"], m + 1)
                    dve.sem_inc(s["y_made"], 1)
                for j in range(tiles):
                    for e in range(2):
                        m = 2 * (G4 * g + j) + e
                        after(dve, s["eo_made"], m + 1)
                        after(dve, s["act_made"], m - 3)
                        V.scalar_tensor_tensor(out=pre[:, j % 2, e], in0=bank[4 + 2 * (j % 2) + e][:, :],
                                               scalar=mix[:, 4:5], in1=b2b[:, e], op0=ALU.mult, op1=ALU.add
                                               ).then_inc(s["pre_made"], 1)
                    if j:
                        add(j - 1)
                add(tiles - 1)
            hidden(0, G4 * P)
            hidden(1, G4 * P)
            outs(0, G4)
            with dve.Fori(2, NG) as g:
                hidden(g, G4 * P)
                outs(g - 1, G4)
            hidden(NG, P)
            outs(NG - 1, G4)
            outs(NG, 1)


_INS = ['x', 'src', 'dst', 'L0_gnn_W1', 'L0_gnn_b1', 'L0_gnn_W2', 'L0_gnn_b2', 'L0_mix_qkv_weight',
        'L0_mix_proj_weight', 'L0_mix_proj_bias', 'L0_ffn_attn_w', 'L0_ffn_attn_b', 'L0_ffn_gate_w',
        'L0_ffn_gate_b', 'L0_ffn_w1', 'L0_ffn_b1', 'L0_ffn_w2', 'L0_ffn_b2']


def kernel(**inputs):
    import concourse.bacc as _bacc
    from concourse.bass_utils import run_bass_kernel_spmd as _run

    nc = _bacc.Bacc("TRN2", target_bir_lowering=False, num_devices=1)
    arrays, args = {}, []
    for name in _INS:
        a = np.ascontiguousarray(inputs[name])
        arrays[f"in_{name}"] = a
        args.append(nc.dram_tensor(f"in_{name}", a.shape, mybir.dt.from_np(a.dtype), kind="ExternalInput").ap())
    args.append(nc.dram_tensor("out_x", (N, D), F32, kind="ExternalOutput").ap())
    program(nc, *args)
    r = _run(nc, [arrays], core_ids=[0])
    return r.results[0]["out_x"]
```

```python
from contextlib import ExitStack

import numpy as np

import concourse.bass as bass
from concourse import mybir

F32, F16, I32, U32 = mybir.dt.float32, mybir.dt.float16, mybir.dt.int32, mybir.dt.uint32
ALU = mybir.AluOpType
ACT = mybir.ActivationFunctionType
AX = mybir.AxisListType
RMAX = bass.bass_isa.ReduceOp.max

P = 128
N, D, E = 6250, 512, 100000
HEAD = 32
NE, H = 8, 256
C = D // P
HC = H // P
T = (N + P - 1) // P
TAIL = N - (T - 1) * P
ROWS = T * P
BLOCKS = (E + P - 1) // P
R = 16
U = 4
NULL = U // 2
COLS = (NULL + BLOCKS + (E % P == 0) + R - 1) // R * R
ROUNDS = COLS // R
RG = R // U
OG = 8
GROUPS = COLS // U
CH = (BLOCKS + P - 1) // P
FULL = BLOCKS // P
XN = 5
XI = 3
G4 = 4
NG = T // G4
EPS_LN = 1e-5
EPS_ATT = 1e-15
EPS_GATE = 1e-9
SX = 2.0 ** 10
SW = 2.0 ** 14
SK = 2.0 ** -19
SP_ = 2.0 ** 14
LOW = -1e30
FAR = 1 << 20

K_, Q_, W_, M_, W1_, HB_, W2_ = range(7)


def real(t):
    return not isinstance(t, int) or 0 <= t < T


def after(eng, sem, count):
    if not isinstance(count, int) or count > 0:
        eng.wait_ge(sem, count)


def pipeline(eng, body, first, lo, hi, last):
    for i in range(first, lo):
        body(i)
    with eng.Fori(lo, hi) as i:
        body(i)
    for i in range(hi, last):
        body(i)


def program(nc, x, src, dst, gw1, gb1, gw2, gb2, qkv_w, proj_w, proj_b, attn_w, attn_b, gate_w, gate_b,
            w1, b1, w2, b2, out):
    ctx = ExitStack()
    with ctx:
        def sb(name, shape, dt):
            return ctx.enter_context(nc.sbuf_tensor(name, shape, dt))

        table = nc.dram_tensor("table", (N, 2 * D), F16, kind="Internal").ap()
        x2_dram = nc.dram_tensor("x2_rows", (ROWS, D), F32, kind="Internal").ap()

        xT = sb("xT", [P, 2 * C, ROWS], F16)
        flat = xT[:, :, :].rearrange("p a n -> p (a n)").bitcast(F32)
        raw_w = [flat[:, k * C * D:(k + 1) * C * D].rearrange("p (a f) -> p a f", a=C) for k in range(6)]
        o = 6 * C * D
        raw_src = flat[:, o:o + CH * P].bitcast(I32).rearrange("p (a f) -> p a f", a=CH)
        o += CH * P
        raw_dst = flat[:, o:o + CH * P].bitcast(I32).rearrange("p (a f) -> p a f", a=CH)
        o += CH * P
        f_src = flat[:, o:o + CH * P].rearrange("p (a f) -> p a f", a=CH)
        o += CH * P
        f_dst = flat[:, o:o + CH * P].rearrange("p (a f) -> p a f", a=CH)
        o += CH * P
        steps = flat[:, o:o + CH * P].rearrange("p (a f) -> p a f", a=CH)
        o += CH * P
        below = flat[:, o:o + CH * (T + 1)].bitcast(F16)[:, 0:CH * (T + 1)].rearrange("p (a f) -> p a f", a=CH)

        wts = sb("wts", [P, 4, 2, C, D], F16)
        wk, wq, wg1, wg2 = (wts[:, k] for k in range(4))
        wm = wk
        w1raw = wts[:, 0].rearrange("p a c f -> p (a c f)").bitcast(F32).rearrange("p (e c h) -> p e c h", e=2, c=C)
        w2raw = wts[:, 1].rearrange("p a c f -> p (a c f)").bitcast(F32).rearrange("p (e c o) -> p e c o", e=2, c=HC)
        w1s = wts[:, 2].rearrange("p a c f -> p a (c f)").rearrange("p a (e c h) -> p a e c h", e=2, c=C)
        w2s = wts[:, 3].rearrange("p a c f -> p a (c f)").rearrange("p a (e c o) -> p a e c o", e=2, c=HC)

        ring = sb("ring", [P, R, 2 * D], F16)
        ring32 = ring[:, :, :].rearrange("p a f -> p (a f)").bitcast(F32).rearrange("p (a f) -> p a f", f=D)
        xnhl = ring[:, 0:XN, :]
        xin = ring32[:, XN:XN + XI, :]
        xn32 = ring32[:, XN + XI:XN + XI + 2, :]
        k32 = ring32[:, XN + XI + 2, :]
        khl = ring[:, XN + XI + 3:XN + XI + 5, :]
        x2g = ring32[:, 0:2 * G4, :].rearrange("p (b j) f -> p b j f", b=2)
        hT = ring[:, 2 * G4:4 * G4, :].rearrange("p a f -> p (a f)").rearrange(
            "p (b a e c n) -> p b a e c n", b=2, a=2, e=2, c=HC)

        onehot = sb("onehot", [P, OG * U, P], F16)
        oh32 = onehot[:, :, :].rearrange("p a f -> p (a f)").bitcast(F32)
        gt32 = oh32.rearrange("p (a f) -> p a f", a=C)
        g32 = gt32
        plb = oh32[:, 0:C * P].rearrange("p (a f) -> p a f", a=C)

        work = sb("work", [P, 10, D], F32)
        wvT, m32, pT32 = work[:, 0:4], work[:, 0:4], work[:, 4:8]
        vtm = work[:, 8].rearrange("p (a f) -> p a f", a=C)
        kacc = work[:, 9]
        x_in, xb, x2, xn2, acc, accs, w32, ah32 = (work[:, k] for k in range(8))
        ahT, pT = (work[:, k].bitcast(F16).rearrange("p (a c n) -> p a c n", a=2, c=C) for k in (8, 9))
        pre = work[:, 0:4].rearrange("p (b e) f -> p b e f", b=2)
        act2 = work[:, 4:8].rearrange("p (b e) f -> p b e f", b=2)
        b2b = work[:, 8:10]

        src_col = sb("src_col", [P, COLS], I32)
        dst_col = sb("dst_col", [P, COLS], F32)
        biasb = sb("biasb", [P, D], F32)
        awb = sb("awb", [P, D], F32)
        bias3 = ring32[:, 15:16, :]
        bias2 = ring32[:, 14:15, :]

        ident = sb("ident", [P, P], F32)
        ident16 = sb("ident16", [P, P], F16)
        ones = sb("ones", [P, P], F32)
        hmask = sb("hmask", [P, P], F32)
        iota_t = hmask
        zero16 = sb("zero16", [P, P], F16)
        ones16 = sb("ones16", [P, P], F16)
        iota16 = sb("iota16", [P, P], F16)
        tile_base = sb("tile_base", [P, T + 1], F32)
        firsts = sb("firsts", [P, T + 1], F32)
        uns = sb("uns", [P, T + 1], F32)
        first_i = sb("first_i", [P, T + 2], I32)
        first_block = sb("first_block", [P, T + 1], I32)
        before = sb("before", [P, CH], I32)
        least = sb("least", [P, 4], F32)
        back16 = sb("back16", [P, 1], F16)
        unsorted = sb("unsorted", [P, 1], F32)
        rowi = sb("rowi", [P, 1], F32)
        rowmask = sb("rowmask", [P, 1], F32)
        rowlow = sb("rowlow", [P, 1], F32)
        idx_slots = sb("idx_slots", [P, R], I32)
        epsc = sb("epsc", [P, 1], F32)
        amax = sb("amax", [P, 8], F32)
        gmax = sb("gmax", [P, 8], F32)
        pow2 = sb("pow2", [P, 8], F32)
        scale = sb("scale", [P, 8], F32)
        undo = sb("undo", [P, 8], F32)
        mix = sb("mix", [P, 8], F32)
        st6 = sb("st6", [P, 6], F32)
        mv = sb("mv", [P, 2], F32)
        std = sb("std", [P, 1], F32)
        rs0 = sb("rs0", [P, 1], F32)
        rstd = sb("rstd", [P, 1], F32)
        kinv = sb("kinv", [P, C], F32)
        ksb = sb("ksb", [P, D], F32)
        den = sb("den", [P, D // HEAD], F32)
        den2 = sb("den2", [P, D // HEAD], F32)
        dg = sb("dg", [P, 1], F32)
        rd = sb("rd", [P, 1], F32)
        sraw = sb("sraw", [P, 1], F32)
        sm = sb("sm", [P, 2], F32)
        negm = sb("negm", [P, 1], F32)
        e2 = sb("e2", [P, 2], F32)
        lsum = sb("lsum", [P, 1], F32)
        wp = sb("wp", [P, 1], F32)
        lw = sb("lw", [P, 1], F32)
        gst = sb("gst", [P, 8], F32)
        abb = sb("abb", [P, 1], F32)
        gwt = sb("gwt", [P, C, NE], F32)
        gbb = sb("gbb", [P, NE], F32)
        pld = sb("pld", [P, 8], F32)
        lg = sb("lg", [P, NE], F32)
        gts = sb("gts", [P, NE], F32)
        top = sb("top", [P, 8], F32)
        topi = sb("topi", [P, 8], U32)
        gexp = sb("gexp", [P, 2], F32)
        b1t = sb("b1t", [P, 2, HC], F32)

        bank = [ctx.enter_context(nc.psum_tensor(f"bank{k}", [P, D], F32)) for k in range(8)]
        ps_q, ps_o, ps_b, ps_agg, ps_deg, ps_ta, ps_tp, ps_tx = bank
        ps_t = [bank[b][:, :].bitcast(F16).rearrange("p (q n) -> p q n", q=2 * C)[:, 0:C, :] for b in (4, 6)]
        ps_k = bank[5]

        names = """consts pads_made ident_made dve_chain act_chain pool_chain
            edges_loaded biases_loaded biases_added small_loaded floats_made turned_edges below_made below_summed counts_read
            firsts_made cols_made
            amax_made gmax_made scales_made w_turned w_hi_made w_lo_made
            x_loaded stats_made mv_made std_made rs_made rstd_made xn_made hi_made lo_made table_stored
            t_made t_hi_taken t_lo_taken k_made k32_made khi_made klo_made kacc_made g_made
            ksum_made gt_hi_copied gt_lo_copied vt_made vtm_made m_made m32_made mmax_made mgmax_made banks_read mscale_made
            mhi_made matrix_split
            arrived released iota_made oh_made oh_used q_made w_made den_made den2_made rec_made p_made turned_ah turned_p
            turned_x2 agg_made dg_made rd_made ah_made ahT_hi ahT_lo pT_hi pT_lo lin_made xa_made x2_made x2_stored
            st2_made mv2_made std2_made rs2_made rstd2_made xn2_made sraw_made sc_made negm_made exp_made
            m_kept l_made accs_made acc_made x2T_hi x2T_lo xb_made x_loaded2
            best_made wp_made lw_made pooled_made plb_made logits_made lg_made gexp_made chosen
            e_amax_made e_gmax_made e_scales w1_hi w1_lo w2_hi w2_lo b1_loaded b2_loaded
            z_made g32_made h_hi h_lo eo_made pre_made act_made y_made y_half x2g_loaded out_stored turn pool_turn""".split()
        s = {n: ctx.enter_context(nc.semaphore(n)) for n in names}
        w_loaded = [ctx.enter_context(nc.semaphore(f"w_loaded{k}")) for k in range(6)]
        e_loaded = [ctx.enter_context(nc.semaphore(f"e_loaded{k}")) for k in range(4)]
        slot_loaded = [ctx.enter_context(nc.semaphore(f"slot_loaded{k}")) for k in range(R)]
        block = ctx.enter_context(nc.Block())

        NCONST = 14

        IS_SPLIT = (1, 0, 1, 0, 1, 1)

        def lo_before(k):
            return C * sum(IS_SPLIT[:k])

        def w_bank(k, c):
            return bank[C * (k % 2) + c]

        def cols(t, w=P):
            return bass.ds(t * P, w)

        def one(a, k):
            return a[:, bass.ds(k, 1), :].rearrange("p a f -> p (a f)")

        def bcast(v, n):
            return v.rearrange("(a n) -> a n", a=1).to_broadcast([P, n])

        @block.sync
        def _(sp):
            def weight(k, w):
                sp.dma_start(raw_w[k], w.rearrange("(a p) f -> p a f", p=P)).then_inc(w_loaded[k], 16)
            weight(0, qkv_w[D:2 * D])
            sp.wait_ge(s["pads_made"], 1)
            for raw, dr in ((raw_dst, dst), (raw_src, src)):
                sp.dma_start(raw[:, 0:FULL, :],
                             dr[0:FULL * P * P].rearrange("(k p e) -> p k e", p=P, e=P)).then_inc(s["edges_loaded"], 16)
                o, last = FULL * P * P, BLOCKS - FULL * P - 1
                sp.dma_start(raw[0:last, FULL, :],
                             dr[o:o + last * P].rearrange("(p e) -> p e", e=P)).then_inc(s["edges_loaded"], 16)
                o += last * P
                sp.dma_start(raw[last:last + 1, FULL, 0:E - o],
                             dr[o:E].rearrange("(p e) -> p e", p=1)).then_inc(s["edges_loaded"], 16)
            with nc.allow_non_contiguous_dma(reason="an edge in 128, 3 KB in all"):
                ends = dst[0:(BLOCKS - 1) * P].rearrange("(r e) -> r e", e=P)[:, P - 1:P]
                sp.dma_start(before[1:P, 0:1], ends[0:P - 1, :]).then_inc(s["edges_loaded"], 16)
                sp.dma_start(before[:, 1:FULL], ends[P - 1:FULL * P - 1, :].rearrange("(k p) e -> p (k e)", p=P)
                             ).then_inc(s["edges_loaded"], 16)
                sp.dma_start(before[0:BLOCKS - FULL * P, FULL:FULL + 1], ends[FULL * P - 1:BLOCKS - 1, :]
                             ).then_inc(s["edges_loaded"], 16)
            for k, w in ((2, qkv_w[0:D]), (1, qkv_w[2 * D:3 * D]), (4, gw1), (5, gw2), (3, proj_w)):
                weight(k, w)

            def rows(i):
                if real(i):
                    after(sp, s["xn_made"], i - XI + 1)
                    sp.sem_inc(s["turn"], 1)
                    after(sp, s["x_loaded"], 16 * i)
                    n = TAIL if isinstance(i, int) and i == T - 1 else P
                    sp.dma_start(xin[0:n, bass.ds(i % XI, 1), :].rearrange("p a f -> p (a f)"),
                                 x[bass.ds(i * P, n), :]).then_inc(s["x_loaded"], 16)
                t = i - 5
                if real(t):
                    n = TAIL if isinstance(t, int) and t == T - 1 else P
                    after(sp, s["hi_made"], t + 1)
                    after(sp, s["lo_made"], t + 1)
                    after(sp, s["table_stored"], 16 * t)
                    sp.dma_start(table[bass.ds(t * P, n), :],
                                 xnhl[0:n, bass.ds(t % XN, 1), :].rearrange("p a f -> p (a f)")
                                 ).then_inc(s["table_stored"], 16)
            for i in range(XI):
                rows(i)
            pipeline(sp, rows, XI, 6, T - 1, T + 5)

            sp.wait_ge(s["firsts_made"], 1)
            passes = sp.value_load(first_i[0:1, T + 1:T + 2], min_val=1, max_val=T)
            with sp.Fori(0, passes) as a:
                with sp.Fori(0, ROUNDS) as g:
                    for k in range(R):
                        sp.wait_ge(slot_loaded[k], (a * ROUNDS + g) * 16 + 16)
                        if k % U == U - 1:
                            sp.sem_inc(s["arrived"], 1)

            sp.wait_ge(s["chosen"], 1)
            chosen = []
            for e in range(2):
                v = sp.value_load(topi[0:1, e:e + 1], min_val=0, max_val=NE - 1)
                chosen.append(v)
                sp.dma_start(w1raw[:, e], w1[bass.ds(v, 1), :, :].rearrange("a (c p) h -> p (a c) h", p=P)
                             ).then_inc(e_loaded[e], 16)
            with nc.allow_non_contiguous_dma(reason="a bias per partition, 1 KB in all"):
                for e, v in enumerate(chosen):
                    sp.dma_start(b1t[:, e], b1[bass.ds(v, 1), :].rearrange("a (c p) -> p (a c)", p=P)
                                 ).then_inc(s["b1_loaded"], 16)
            for e, v in enumerate(chosen):
                sp.dma_start(w2raw[:, e], w2[bass.ds(v, 1), :, :].rearrange("a (c p) o -> p (a c) o", p=P)
                             ).then_inc(e_loaded[2 + e], 16)
            for e, v in enumerate(chosen):
                sp.dma_start(b2b[:, e], b2[bass.ds(v, 1), :].to_broadcast([P, D])).then_inc(s["b2_loaded"], 16)

            def group(g):
                whole = not isinstance(g, int) or g < NG
                j = G4 if whole else 1
                after(sp, s["out_stored"], 16 * (g - 1))
                sp.sem_inc(s["turn"], 1)
                after(sp, s["x2g_loaded"], 16 * g)
                sp.dma_start(x2g[:, bass.ds(g % 2, 1), 0:j, :].rearrange("p a j f -> p (a j) f"),
                             x2_dram[bass.ds(g * G4 * P, j * P), :].rearrange("(j p) f -> p j f", p=P)
                             ).then_inc(s["x2g_loaded"], 16)

            def store(g):
                after(sp, s["y_made"], G4 * g + G4)
                sp.dma_start(out[bass.ds(g * G4 * P, G4 * P), :].rearrange("(j p) f -> p j f", p=P),
                             x2g[:, bass.ds(g % 2, 1), :, :].rearrange("p a j f -> p (a j) f")
                             ).then_inc(s["out_stored"], 16)
            sp.wait_ge(s["x2_stored"], 16 * T)
            group(0)
            group(1)
            store(0)
            with sp.Fori(2, NG) as g:
                group(g)
                store(g - 1)
            group(NG)
            store(NG - 1)
            sp.wait_ge(s["y_made"], T)
            body = TAIL // 16 * 16
            sp.dma_start(out[(T - 1) * P:(T - 1) * P + body, :], x2g[0:body, NG % 2, 0, :]).then_inc(s["out_stored"], 16)
            sp.dma_start(out[(T - 1) * P + body:N, :], x2g[body:TAIL, NG % 2, 0, :]).then_inc(s["out_stored"], 16)
            sp.wait_ge(s["out_stored"], 16 * (NG + 2))

        @block.gpsimd
        def _(pool):
            made = [0]

            def link(ins):
                made[0] += 1
                ins.then_inc(s["pool_chain"], 1)
                pool.wait_ge(s["pool_chain"], made[0])

            imp = dict(allow_small_or_imprecise_dtypes=True)
            link(pool.memset(raw_dst[:, FULL, :], FAR))
            link(pool.memset(raw_src[:, FULL, :], 0))
            link(pool.memset(before[:], 0))
            pool.sem_inc(s["pads_made"], 1)
            link(pool.memset(ident[:], 0.0))
            link(pool.affine_select(out=ident[:], in_=ident[:], compare_op=ALU.not_equal, fill=1.0, base=0,
                                    pattern=[[-1, P]], channel_multiplier=1))
            pool.sem_inc(s["ident_made"], 1)
            pool.memset(amax[:], 0.0).then_inc(s["consts"], 1)
            pool.iota(tile_base[:], pattern=[[P, T + 1]], base=0, channel_multiplier=0, **imp).then_inc(s["consts"], 1)
            pool.iota(rowi[:], pattern=[[0, 1]], base=0, channel_multiplier=1, **imp).then_inc(s["consts"], 1)
            link(pool.tensor_copy(ident16[:], ident[:]))
            link(pool.memset(hmask[:], 1.0))
            hm = hmask[:, :].rearrange("p (a c) -> p a c", c=HEAD)
            link(pool.affine_select(out=hm, in_=hm, compare_op=ALU.is_ge, fill=0.0, base=0,
                                    pattern=[[-HEAD, P // HEAD], [0, HEAD]], channel_multiplier=1))
            link(pool.affine_select(out=hm, in_=hm, compare_op=ALU.is_ge, fill=0.0, base=HEAD - 1,
                                    pattern=[[HEAD, P // HEAD], [0, HEAD]], channel_multiplier=-1))
            pool.memset(ones[:], 1.0).then_inc(s["consts"], 1)
            pool.memset(zero16[:], 0.0).then_inc(s["consts"], 1)
            pool.memset(ones16[:], 1.0).then_inc(s["consts"], 1)
            pool.memset(epsc[:], EPS_LN / (SX * SX)).then_inc(s["consts"], 1)
            pool.memset(kacc, 0.0).then_inc(s["consts"], 1)
            pool.iota(iota16[:], pattern=[[1, P]], base=0, channel_multiplier=0, **imp).then_inc(s["consts"], 1)
            pool.iota(uns[:], pattern=[[COLS, T + 1]], base=0, channel_multiplier=0, **imp).then_inc(s["consts"], 1)
            pool.memset(src_col[:], 0).then_inc(s["consts"], 1)
            pool.memset(dst_col[:], -1.0).then_inc(s["consts"], 1)
            pool.memset(sm[:, :], LOW).then_inc(s["consts"], 1)
            pool.memset(lsum[:], 0.0).then_inc(s["consts"], 1)

            for k in range(3):
                pool.wait_ge(s["amax_made"], k + 1)
                pool.partition_all_reduce(gmax[:, k:k + 1], amax[:, k:k + 1], P, RMAX).then_inc(s["gmax_made"], 1)
                if k == 0:
                    pool.wait_ge(s["biases_loaded"], 48)
                    link(pool.tensor_tensor(out=bias2[:, 0], in0=bias2[:, 0], in1=bias3[:, 0], op=ALU.add))
                    link(pool.tensor_tensor(out=biasb[:], in0=biasb[:], in1=bias2[:, 0], op=ALU.add))
                    pool.sem_inc(s["biases_added"], 1)

            def keys(i):
                if real(i):
                    pool.wait_ge(s["khi_made"], i + 1)
                    pool.tensor_tensor(out=one(khl, i % 2)[:, D:2 * D], in0=k32, in1=one(khl, i % 2)[:, 0:D],
                                       op=ALU.subtract).then_inc(s["klo_made"], 1)
                    after(pool, s["kacc_made"], i)
                    pool.tensor_tensor(out=kacc, in0=kacc, in1=k32, op=ALU.add).then_inc(s["kacc_made"], 1)
            pipeline(pool, keys, 0, 1, T, T)

            pool.wait_ge(s["firsts_made"], 1)
            pool.wait_ge(s["cols_made"], 4)
            pool.wait_ge(s["table_stored"], 16 * T)
            pool.wait_ge(s["g_made"], T)
            passes = pool.value_load(first_i[0:1, T + 1:T + 2], min_val=1, max_val=T)

            def gather(it, g, k):
                pool.wait_ge(s["released"], it * RG + k // U + 1)
                pool.tensor_copy(idx_slots[:, k:k + U], src_col[:, bass.ds(g * R + k, U)]
                                 ).then_inc(s["pool_turn"], 1)
                pool.wait_ge(s["pool_turn"], it * RG + k // U + 1)
                pool.sem_inc(s["turn"], 1)
                for n in range(k, k + U):
                    pool.indirect_dma_start(
                        ring[:, n, :], None, table[:, :],
                        bass.IndirectOffsetOnAxis(ap=idx_slots[:, n:n + 1], axis=0)
                    ).then_inc(slot_loaded[n], 16)
            for k in range(0, R, U):
                gather(0, 0, k)
            pool.wait_ge(s["mmax_made"], 1)
            pool.partition_all_reduce(gmax[:, 3:4], amax[:, 3:4], P, RMAX).then_inc(s["mgmax_made"], 1)
            with pool.Fori(1, ROUNDS) as g:
                for k in range(0, R, U):
                    gather(g, g, k)
            with pool.If(passes > 1):
                with pool.Fori(1, passes) as a:
                    with pool.Fori(0, ROUNDS) as g:
                        for k in range(0, R, U):
                            gather(a * ROUNDS + g, g, k)

            pool.wait_ge(s["acc_made"], T)
            pool.wait_ge(s["m_kept"], T)
            pool.partition_all_reduce(gst[:, 0:1], sm[:, 0:1], P, RMAX).then_inc(s["best_made"], 1)
            for k, (a, b) in enumerate(((W1_, HB_ + 1), (W2_, W2_ + 1))):
                pool.wait_ge(s["e_amax_made"], k + 1)
                pool.partition_all_reduce(gmax[:, a:b], amax[:, a:b], P, RMAX).then_inc(s["e_gmax_made"], 1)

        @block.tensor
        def _(pe):
            mm = nc.tensor.matmul

            def three(out_, wh, wl, mh, ml, n, first=True, last=True):
                for c in range(n):
                    mm(out_, wh(c), mh(c), start=first and c == 0, stop=False)
                    mm(out_, wh(c), ml(c), start=False, stop=False)
                for c in range(n):
                    r = mm(out_, wl(c), mh(c), start=False, stop=last and c == n - 1)
                return r

            def turn_weight(k):
                pe.wait_ge(w_loaded[k], 16)
                for c in range(C):
                    if k >= 2:
                        pe.wait_ge(s["w_hi_made"], (k - 2) * C + c + 1)
                        if IS_SPLIT[k - 2]:
                            pe.wait_ge(s["w_lo_made"], lo_before(k - 2) + c + 1)
                    for a in range(C):
                        r = nc.tensor.transpose(w_bank(k, c)[:, a * P:(a + 1) * P],
                                                raw_w[k][:, a, c * P:(c + 1) * P], ident[:])
                    r.then_inc(s["w_turned"], 1)
            pe.wait_ge(s["ident_made"], 1)
            turn_weight(0)
            pe.wait_ge(s["floats_made"], 2)
            for j, f in enumerate((f_dst, f_src)):
                for k in range(CH):
                    r = nc.tensor.transpose(bank[4 + 2 * j + k // C][:, k % C * P:(k % C + 1) * P], f[:, k, :], ident[:])
                    if k == C - 1 or k == CH - 1:
                        r.then_inc(s["turned_edges"], 1)
            pe.wait_ge(s["consts"], NCONST)
            pe.wait_ge(s["below_made"], 1)
            pe.wait_ge(s["w_hi_made"], 1)
            pe.wait_ge(s["w_lo_made"], 1)
            for k in range(CH):
                mm(bank[0][:, 0:T + 1], ones16[:], below[:, k, :], start=(k == 0), stop=(k == CH - 1))
            mm(bank[0][:, T + 1:T + 2], ones16[:], back16[:], start=True, stop=True).then_inc(s["below_summed"], 1)
            pe.wait_ge(s["cols_made"], 4)
            turn_weight(1)
            pe.wait_ge(s["counts_read"], 1)
            for k in range(2, 6):
                turn_weight(k)
            pe.wait_ge(s["w_hi_made"], 6 * C)
            pe.wait_ge(s["w_lo_made"], lo_before(6))

            def keys(i):
                t = i + 1
                if real(t):
                    after(pe, s["lo_made"], t + 1)
                    after(pe, s["t_hi_taken"], t)
                    after(pe, s["t_lo_taken"], t)
                    for q in range(2 * C):
                        r = nc.tensor.transpose(ps_t[q // C][:, q % C, :], one(xnhl, t % XN)[:, q * P:(q + 1) * P], ident16[:])
                    r.then_inc(s["t_made"], 1)
                t = i
                if real(t):
                    after(pe, s["t_hi_taken"], t + 1)
                    after(pe, s["t_lo_taken"], t + 1)
                    after(pe, s["k32_made"], t)
                    three(ps_k[:, :], lambda c: xT[:, c, cols(t)], lambda c: xT[:, C + c, cols(t)],
                          lambda c: wk[:, 0, c, :], lambda c: wk[:, 1, c, :], C).then_inc(s["k_made"], 1)
                t = i - 1
                if real(t):
                    pe.wait_ge(s["klo_made"], t + 1)
                    kh, kl, xs = one(khl, t % 2)[:, 0:D], one(khl, t % 2)[:, D:2 * D], one(xnhl, t % XN)
                    st, en = (isinstance(t, int) and t == 0), (isinstance(t, int) and t == T - 1)
                    for c in range(C):
                        mm(bank[c][:, :], xs[:, c * P:(c + 1) * P], kh, start=st, stop=False)
                        mm(bank[c][:, :], xs[:, c * P:(c + 1) * P], kl, start=False, stop=False)
                        r = mm(bank[c][:, :], xs[:, D + c * P:D + (c + 1) * P], kh, start=False, stop=en)
                    r.then_inc(s["g_made"], 1)
            pipeline(pe, keys, -1, 2, T - 4, T + 1)

            pe.sem_inc(s["released"], RG)
            pe.sem_inc(s["oh_used"], OG)

            pe.wait_ge(s["kacc_made"], T)
            for c in range(C):
                mm(bank[6][:, c:c + 1], kacc[:, c * P:(c + 1) * P], ones[:, 0:1], start=True, stop=True)
            mm(bank[7][:, :], ones[:], kacc, start=True, stop=True).then_inc(s["ksum_made"], 1)
            pe.wait_ge(s["gt_hi_copied"], 2)
            pe.wait_ge(s["gt_lo_copied"], 2)
            for j in range(C):
                for c in range(C):
                    r = mm(bank[4][:, j * P:(j + 1) * P], wvT[:, c, j * P:(j + 1) * P], gt32[:, c, j * P:(j + 1) * P],
                           start=(c == 0), stop=(c == C - 1))
            r.then_inc(s["vt_made"], 1)
            pe.wait_ge(s["vtm_made"], 1)
            for j in range(C):
                mm(bank[j][:, :], vtm[:, j, :], pT32[:, j, :], start=True, stop=True).then_inc(s["m_made"], 1)

            agg3 = ps_agg[:, :].rearrange("p (c n) -> p c n", c=C)

            def consume(q, t, first=None, last=None):
                pe.wait_ge(s["arrived"], q + 1)
                pe.wait_ge(s["oh_made"], q + t + 1)
                w = onehot[:, bass.ds((q + t) % OG * U, U), :]
                rows = ring[:, bass.ds(q % RG * U, U), :]

                def add(k, start=False, stop=False):
                    mm(ps_agg[:, :], w[:, k, :], rows[:, k, 0:D], start=start, stop=False, skip_group_check=True)
                    r = mm(ps_agg[:, :], w[:, k, :], rows[:, k, D:2 * D], start=False, stop=stop,
                           skip_group_check=True)
                    d = mm(ps_deg[:, 0:1], w[:, k, :], ones16[:, 0:1], start=start, stop=False, skip_group_check=True)
                    return r, d

                def when(cond, k):
                    with pe.If(cond):
                        add(k)
                if last is not None:
                    with pe.If(last >= 2):
                        when(last >= 3, 3)
                        add(2)
                    when(last >= 1, 1)
                    add(0, stop=True)[1].then_inc(s["oh_used"], 1)
                    return
                if first is None:
                    for k in range(U):
                        r, d = add(k)
                else:
                    add(3, start=True)
                    with pe.If(first < 2):
                        when(first < 1, 0)
                        add(1)
                    when(first < 3, 2)
                    r, d = (mm(ps_deg[:, 0:1], zero16[:], ones16[:, 0:1], start=False, stop=False,
                               skip_group_check=True) for _ in range(2))
                r.then_inc(s["released"], 1)
                d.then_inc(s["oh_used"], 1)

            def layer(i):
                t = i
                if real(t):
                    if isinstance(t, int) and t == 0:
                        pe.wait_ge(s["banks_read"], 1)
                    fa = pe.value_load(first_block[0:1, bass.ds(t, 1)], min_val=0, max_val=COLS * T - 1)
                    after(pe, s["w_made"], t)
                    three(ps_q[:, :], lambda c: xT[:, c, cols(t)], lambda c: xT[:, C + c, cols(t)],
                          lambda c: wq[:, 0, c, :], lambda c: wq[:, 1, c, :], C).then_inc(s["q_made"], 1)
                    fb = pe.value_load(first_block[0:1, bass.ds(t + 1, 1)], min_val=0, max_val=COLS * T - 1)
                    a, b = fa // U, fb // U
                t = i - 1
                if real(t):
                    after(pe, s["ah_made"], t + 1)
                    after(pe, s["ahT_lo"], t)
                    for c in range(C):
                        r = nc.tensor.transpose(ps_ta[:, c * P:(c + 1) * P], ah32[:, c * P:(c + 1) * P], ident[:])
                    r.then_inc(s["turned_ah"], 1)
                    after(pe, s["p_made"], t + 1)
                    after(pe, s["pT_lo"], t)
                    for c in range(C):
                        r = nc.tensor.transpose(ps_tp[:, c * P:(c + 1) * P], w32[:, c * P:(c + 1) * P], ident[:])
                    r.then_inc(s["turned_p"], 1)
                t = i
                if real(t):
                    after(pe, s["ah_made"], t)
                    after(pe, s["dg_made"], t)
                    with pe.If(a < b):
                        consume(a, t, first=fa % U)
                        with pe.If(a + 2 < b):
                            with pe.Fori(a + 1, b - 1) as q:
                                consume(q, t)
                    with pe.If(a >= b):
                        mm(agg3, zero16[:], zero16[:, None, :].to_broadcast([P, C, P]), start=True, stop=False, skip_group_check=True)
                        mm(ps_deg[:, 0:1], zero16[:], ones16[:, 0:1], start=True, stop=False, skip_group_check=True)
                t = i - 1
                if real(t):
                    after(pe, s["x2_made"], t)
                    three(ps_o[:, :], lambda c: xT[:, c, cols(t)], lambda c: xT[:, C + c, cols(t)],
                          lambda c: wg1[:, 0, c, :], lambda c: wg1[:, 1, c, :], C, last=False)
                t = i
                if real(t):
                    with pe.If(a + 1 < b):
                        consume(b - 1, t)
                t = i - 1
                if real(t):
                    after(pe, s["ahT_lo"], t + 1)
                    three(ps_o[:, :], lambda c: ahT[:, 0, c, :], lambda c: ahT[:, 1, c, :],
                          lambda c: wg2[:, 0, c, :], lambda c: wg2[:, 1, c, :], C, first=False)
                t = i
                if real(t):
                    consume(b, t, last=fb % U)
                    mm(ps_deg[:, 0:1], zero16[:], ones16[:, 0:1], start=False, stop=True, skip_group_check=True
                       ).then_inc(s["agg_made"], 1)
                t = i - 1
                if real(t):
                    after(pe, s["pT_lo"], t + 1)
                    if isinstance(t, int) and t == 0:
                        pe.wait_ge(s["matrix_split"], 1)
                    three(ps_b[:, :], lambda c: pT[:, 0, c, :], lambda c: pT[:, 1, c, :],
                          lambda c: wm[:, 0, c, :], lambda c: wm[:, 1, c, :], C).then_inc(s["lin_made"], 1)
                t = i - 2
                if real(t):
                    after(pe, s["xn2_made"], t + 1)
                    after(pe, s["x2T_lo"], t)
                    for c in range(C):
                        r = nc.tensor.transpose(ps_tx[:, c * P:(c + 1) * P], xn2[:, c * P:(c + 1) * P], ident[:])
                    r.then_inc(s["turned_x2"], 1)
            pipeline(pe, layer, 0, 3, T, T + 2)

            pe.wait_ge(s["wp_made"], 1)
            pe.wait_ge(s["lw_made"], 1)
            for c in range(C):
                mm(bank[0][:, c:c + 1], acc[:, c * P:(c + 1) * P], wp[:], start=True, stop=True)
            mm(bank[0][:, C:C + 1], ones[:], lw[:], start=True, stop=True).then_inc(s["pooled_made"], 1)
            pe.wait_ge(s["plb_made"], 1)
            for c in range(C):
                r = mm(bank[1][:, 0:NE], plb[:, c, :], gwt[:, c, :], start=(c == 0), stop=(c == C - 1))
            r.then_inc(s["logits_made"], 1)

            pe.wait_ge(s["x2T_lo"], T)

            def hidden(g, n):
                for b in range(2 * HC):
                    e, hc = b // HC, b % HC
                    if isinstance(g, int) and g == 0:
                        pe.wait_ge(s["w1_lo"], e + 1)
                    after(pe, s["g32_made"], 2 * HC * g - 2 * HC + b + 1)
                    three(bank[b][:, 0:n], lambda c: w1s[:, 0, e, c, hc * P:(hc + 1) * P],
                          lambda c: w1s[:, 1, e, c, hc * P:(hc + 1) * P],
                          lambda c: xT[:, c, bass.ds(g * G4 * P, n)],
                          lambda c: xT[:, C + c, bass.ds(g * G4 * P, n)], C).then_inc(s["z_made"], 1)

            def outs(g, tiles):
                if isinstance(g, int) and g == 0:
                    pe.wait_ge(s["w2_lo"], 2)
                after(pe, s["h_lo"], 2 * HC * g + 2 * HC)
                for j in range(tiles):
                    for e in range(2):
                        after(pe, s["pre_made"], 2 * (G4 * g + j) - 4 + e + 1)
                        hh = hT[:, bass.ds(g % 2, 1)].rearrange("p b a e c n -> p (b a) e c n")
                        three(bank[4 + 2 * (j % 2) + e][:, :],
                              lambda c: hh[:, 0, e, c, j * P:(j + 1) * P], lambda c: hh[:, 1, e, c, j * P:(j + 1) * P],
                              lambda c: w2s[:, 0, e, c, :], lambda c: w2s[:, 1, e, c, :], HC).then_inc(s["eo_made"], 1)
            hidden(0, G4 * P)
            hidden(1, G4 * P)
            outs(0, G4)
            with pe.Fori(2, NG) as g:
                hidden(g, G4 * P)
                outs(g - 1, G4)
            hidden(NG, P)
            outs(NG - 1, G4)
            outs(NG, 1)

        @block.scalar
        def _(act):
            F = nc.scalar.activation
            made = [0]

            def link(ins):
                made[0] += 1
                ins.then_inc(s["act_chain"], 1)
                act.wait_ge(s["act_chain"], made[0])

            act.dma_start(biasb[:], bcast(gb1, D)).then_inc(s["biases_loaded"], 16)
            act.dma_start(bias2[:, 0], bcast(gb2, D)).then_inc(s["biases_loaded"], 16)
            act.dma_start(bias3[:, 0], bcast(proj_b, D)).then_inc(s["biases_loaded"], 16)
            act.dma_start(awb[:], attn_w.rearrange("(a n) b -> a (n b)", a=1).to_broadcast([P, D])
                          ).then_inc(s["small_loaded"], 16)
            act.dma_start(abb[:], bcast(attn_b, 1)).then_inc(s["small_loaded"], 16)
            act.dma_start(gbb[:], bcast(gate_b, NE)).then_inc(s["small_loaded"], 16)
            act.dma_start(gwt[:], gate_w.rearrange("(c p) e -> p c e", p=P)).then_inc(s["small_loaded"], 16)

            def split_weight(k, out_, scales, col):
                after(act, s["scales_made"], scales)
                for c in range(C):
                    n = k * C + c
                    act.wait_ge(s["w_turned"], n + 1)
                    if col is None:
                        F(out_[:, c, :], w_bank(k, c)[:, :], ACT.Copy).then_inc(s["w_hi_made"], 1)
                    else:
                        F(out_[:, 0, c, :], w_bank(k, c)[:, :], ACT.Copy, scale=scale[:, col:col + 1]
                          ).then_inc(s["w_hi_made"], 1)
            split_weight(0, wk, 1, K_)
            act.wait_ge(s["edges_loaded"], 144)
            F(f_dst, raw_dst, ACT.Copy).then_inc(s["floats_made"], 1)
            F(f_src, raw_src, ACT.Copy).then_inc(s["floats_made"], 1)
            act.wait_ge(s["consts"], NCONST)
            for j, col in enumerate((dst_col, src_col)):
                for h in range(2):
                    w = min(C * P, BLOCKS - h * C * P)
                    act.wait_ge(s["turned_edges"], 2 * j + h + 1)
                    F(col[:, NULL + h * C * P:NULL + h * C * P + w], bank[4 + 2 * j + h][:, 0:w], ACT.Copy
                      ).then_inc(s["cols_made"], 1)
            split_weight(1, wvT, 0, None)
            split_weight(2, wq, 2, Q_)
            split_weight(3, pT32, 0, None)
            def keys(i):
                t = i + 1
                if real(t):
                    after(act, s["t_made"], t + 1)
                    F(xT[:, 0:C, cols(t)], ps_t[0], ACT.Copy).then_inc(s["t_hi_taken"], 1)
                t = i + 3
                if real(t):
                    after(act, s["xn_made"], t + 1)
                    after(act, s["g_made"], t - XN + 1)
                    after(act, s["table_stored"], 16 * (t - XN + 1))
                    F(one(xnhl, t % XN)[:, 0:D], one(xn32, t % 2), ACT.Copy).then_inc(s["hi_made"], 1)
                t = i + 4
                if real(t):
                    after(act, s["mv_made"], t + 1)
                    after(act, s["rs_made"], t)
                    F(std[:], mv[:, 1:2], ACT.Sqrt, bias=epsc[:], scale=1.0 / (SX * SX)).then_inc(s["std_made"], 1)
                t = i
                if real(t):
                    after(act, s["k32_made"], t + 1)
                    after(act, s["g_made"], t - 1)
                    F(one(khl, t % 2)[:, 0:D], k32, ACT.Copy).then_inc(s["khi_made"], 1)
            keys(-4)
            split_weight(4, wg1, 3, W_)
            split_weight(5, wg2, 3, W_)
            keys(-3)
            keys(-2)
            pipeline(act, keys, -1, 2, T - 4, T)

            act.wait_ge(s["g_made"], T)
            for c in range(2):
                F(gt32[:, c, :], bank[c][:, :], ACT.Copy).then_inc(s["gt_hi_copied"], 1)
            def layer(i):
                t = i - 3
                if real(t):
                    after(act, s["turned_x2"], t + 1)
                    F(xT[:, 0:C, cols(t)], ps_tx[:, :].rearrange("p (c n) -> p c n", c=C), ACT.Copy).then_inc(s["x2T_hi"], 1)
                t = i - 2
                if real(t):
                    after(act, s["mv2_made"], t + 1)
                    after(act, s["rs2_made"], t)
                    F(std[:], mv[:, 1:2], ACT.Sqrt, bias=epsc[:], scale=1.0 / (SX * SX)).then_inc(s["std2_made"], 1)
                t = i - 1
                if real(t):
                    after(act, s["turned_ah"], t + 1)
                    F(ahT[:, 0], ps_ta[:, :].rearrange("p (c n) -> p c n", c=C), ACT.Copy).then_inc(s["ahT_hi"], 1)
                    after(act, s["turned_p"], t + 1)
                    F(pT[:, 0], ps_tp[:, :].rearrange("p (c n) -> p c n", c=C), ACT.Copy, scale=SP_).then_inc(s["pT_hi"], 1)
                t = i - 2
                if real(t):
                    after(act, s["negm_made"], t + 1)
                    F(e2[:], sm[:], ACT.Exp, bias=negm[:]).then_inc(s["exp_made"], 1)
                    after(act, s["exp_made"], t + 1)
                    after(act, s["acc_made"], t)
                    F(accs, acc, ACT.Copy, scale=e2[:, 0:1]).then_inc(s["accs_made"], 1)
                    after(act, s["x2_stored"], 16 * t)
                    after(act, s["x2_made"], t + 1)
                    act.dma_start(x2_dram[bass.ds(t * P, P), :], x2).then_inc(s["x2_stored"], 16)
                t = i
                if real(t):
                    n = TAIL if isinstance(t, int) and t == T - 1 else P
                    if not isinstance(t, int) or t > 0:
                        after(act, s["xb_made"], t)
                        after(act, s["x_loaded2"], 16 * t)
                        act.dma_start(x_in[0:n, :], x[bass.ds(t * P, n), :]).then_inc(s["x_loaded2"], 16)
                    after(act, s["rd_made"], t + 1)
                    F(ah32, ps_agg[:, :], ACT.Copy, scale=rd[:]).then_inc(s["ah_made"], 1)
            act.wait_ge(s["mscale_made"], 1)
            for c in range(C):
                r = F(wm[:, 0, c, :], m32[:, c, :], ACT.Copy, scale=scale[:, M_:M_ + 1])
            r.then_inc(s["mhi_made"], 1)
            act.wait_ge(s["matrix_split"], 1)
            act.dma_start(x_in, x[0:P, :]).then_inc(s["x_loaded2"], 16)
            pipeline(act, layer, 0, 4, T - 1, T + 3)

            act.wait_ge(s["best_made"], 2)
            F(wp[:], sm[:, 0:1], ACT.Exp, bias=gst[:, 1:2]).then_inc(s["wp_made"], 1)
            act.wait_ge(s["lg_made"], 1)
            F(gts[:], lg[:], ACT.Exp, bias=gst[:, 2:3]).then_inc(s["gexp_made"], 1)

            act.wait_ge(s["e_scales"], 1)
            for e in range(2):
                F(w1s[:, 0, e], w1raw[:, e], ACT.Copy, scale=scale[:, W1_:W1_ + 1]).then_inc(s["w1_hi"], 1)

            def hidden(g, n):
                for b in range(2 * HC):
                    e, hc = b // HC, b % HC
                    after(act, s["z_made"], 2 * HC * g + b + 1)
                    after(act, s["h_lo"], 2 * HC * g - 2 * HC + b + 1)
                    F(g32[:, b, 0:n], bank[b][:, 0:n], ACT.Gelu, bias=b1t[:, e, hc:hc + 1], scale=mix[:, 3:4]
                      ).then_inc(s["g32_made"], 1)
                    after(act, s["g32_made"], 2 * HC * g + b + 1)
                    after(act, s["eo_made"], 2 * G4 * g - 2 * G4)
                    hh = hT[:, bass.ds(g % 2, 1)].rearrange("p b a e c n -> p (b a) e c n")
                    F(hh[:, 0, e, hc, 0:n], g32[:, b, 0:n], ACT.Copy, scale=scale[:, HB_:HB_ + 1]).then_inc(s["h_hi"], 1)

            def outs(g, tiles):
                for j in range(tiles):
                    for e in range(2):
                        m = 2 * (G4 * g + j) + e
                        after(act, s["pre_made"], m + 1)
                        after(act, s["y_half"], m - 3)
                        F(act2[:, j % 2, e], pre[:, j % 2, e], ACT.Gelu).then_inc(s["act_made"], 1)
            hidden(0, G4 * P)
            act.wait_ge(s["e_scales"], 2)
            for e in range(2):
                F(w2s[:, 0, e], w2raw[:, e], ACT.Copy, scale=scale[:, W2_:W2_ + 1]).then_inc(s["w2_hi"], 1)
            hidden(1, G4 * P)
            outs(0, G4)
            with act.Fori(2, NG) as g:
                hidden(g, G4 * P)
                outs(g - 1, G4)
            hidden(NG, P)
            outs(NG - 1, G4)
            outs(NG, 1)

        @block.vector
        def _(dve):
            V = nc.vector
            made = [0]

            def link(ins):
                made[0] += 1
                ins.then_inc(s["dve_chain"], 1)
                dve.wait_ge(s["dve_chain"], made[0])

            def powers(a, b, sw=SW):
                link(V.tensor_scalar(gmax[:, a:b], gmax[:, a:b], 1e-30, None, ALU.max))
                link(V.tensor_scalar(pow2[:, a:b].bitcast(I32), gmax[:, a:b].bitcast(I32), 0x7F800000, None,
                                     ALU.bitwise_and))
                link(V.reciprocal(scale[:, a:b], pow2[:, a:b]))
                link(V.tensor_scalar(scale[:, a:b], scale[:, a:b], sw, None, ALU.mult))
                link(V.tensor_scalar(undo[:, a:b], pow2[:, a:b], 1.0 / sw, None, ALU.mult))

            def largest(k, col):
                dve.wait_ge(w_loaded[k], 16)
                link(V.tensor_reduce(amax[:, col:col + 1], raw_w[k], AX.XY, ALU.max, apply_absolute_value=True))

            def lo_part(k, w, col):
                for c in range(C):
                    n = k * C + c
                    dve.wait_ge(s["w_hi_made"], n + 1)
                    V.scalar_tensor_tensor(out=w[:, 1, c, :], in0=w_bank(k, c)[:, :], scalar=scale[:, col:col + 1],
                                           in1=w[:, 0, c, :], op0=ALU.mult, op1=ALU.subtract).then_inc(s["w_lo_made"], 1)
            dve.wait_ge(s["ident_made"], 1)
            dve.wait_ge(s["consts"], 3)
            largest(0, K_)
            dve.sem_inc(s["amax_made"], 1)
            dve.wait_ge(s["gmax_made"], 1)
            powers(K_, K_ + 1)
            dve.sem_inc(s["scales_made"], 1)
            lo_part(0, wk, K_)
            dve.wait_ge(s["edges_loaded"], 144)
            V.tensor_tensor(below, raw_dst[:, :, P - 1:P].to_broadcast([P, CH, T + 1]),
                            tile_base[:, None, :].to_broadcast([P, CH, T + 1]), ALU.is_lt)
            V.tensor_tensor(steps[:, :, 0:1], raw_dst[:, :, 0:1], before[:, :, None], ALU.subtract)
            link(V.tensor_tensor(steps[:, :, 1:P], raw_dst[:, :, 1:P], raw_dst[:, :, 0:P - 1], ALU.subtract))
            link(V.tensor_reduce(least[:, 0:1], steps, AX.XY, ALU.min))
            link(V.tensor_scalar(back16[:], least[:, 0:1], 0.0, None, ALU.is_lt))
            dve.sem_inc(s["below_made"], 1)
            dve.wait_ge(s["consts"], NCONST)
            dve.wait_ge(s["below_summed"], 1)
            link(V.tensor_copy(firsts[:], bank[0][:, 0:T + 1]))
            link(V.tensor_scalar(firsts[:], firsts[:], float(NULL), None, ALU.add))
            link(V.tensor_scalar(unsorted[:], bank[0][:, T + 1:T + 2], 0.0, None, ALU.is_gt))
            dve.sem_inc(s["counts_read"], 1)
            largest(2, Q_)
            dve.sem_inc(s["amax_made"], 1)
            largest(4, W_)
            dve.wait_ge(s["gmax_made"], 2)
            powers(Q_, Q_ + 1)
            dve.sem_inc(s["scales_made"], 1)
            largest(5, 7)
            link(V.tensor_tensor(amax[:, W_:W_ + 1], amax[:, W_:W_ + 1], amax[:, 7:8], ALU.max))
            dve.sem_inc(s["amax_made"], 1)
            lo_part(2, wq, Q_)
            dve.wait_ge(s["gmax_made"], 3)
            powers(W_, W_ + 1)
            dve.sem_inc(s["scales_made"], 1)
            link(V.tensor_scalar(rowmask[:], rowi[:], float(TAIL), None, ALU.is_lt))
            link(V.tensor_scalar(rowlow[:], rowmask[:], -LOW, LOW, ALU.mult, ALU.add))

            def keys(i):
                t = i + 1
                if real(t):
                    after(dve, s["t_made"], t + 1)
                    V.tensor_copy(xT[:, C:2 * C, cols(t)], ps_t[1]).then_inc(s["t_lo_taken"], 1)
                t = i + 3
                if real(t):
                    after(dve, s["std_made"], t + 1)
                    V.reciprocal(rs0[:], std[:]).then_inc(s["rs_made"], 1)
                    after(dve, s["rs_made"], t + 1)
                    m = rowmask[:] if isinstance(t, int) and t == T - 1 else ones[:, 0:1]
                    V.tensor_scalar(rstd[:], rs0[:], m, None, ALU.mult).then_inc(s["rstd_made"], 1)
                    after(dve, s["rstd_made"], t + 1)
                    after(dve, s["hi_made"], t - 1)
                    V.tensor_scalar(one(xn32, t % 2), one(xin, t % XI), mv[:, 0:1], rstd[:],
                                    ALU.subtract, ALU.mult).then_inc(s["xn_made"], 1)
                t = i + 2
                if real(t):
                    after(dve, s["hi_made"], t + 1)
                    V.tensor_tensor(one(xnhl, t % XN)[:, D:2 * D], one(xn32, t % 2), one(xnhl, t % XN)[:, 0:D],
                                    ALU.subtract).then_inc(s["lo_made"], 1)
                t = i + 4
                if real(t):
                    after(dve, s["x_loaded"], 16 * t + 16)
                    V.bn_stats(st6[:], one(xin, t % XI)).then_inc(s["stats_made"], 1)
                    after(dve, s["stats_made"], t + 1)
                    after(dve, s["xn_made"], t)
                    dve.sem_inc(s["turn"], 1)
                    V.bn_aggr(mv[:], st6[:]).then_inc(s["mv_made"], 1)
                t = i
                if real(t):
                    after(dve, s["k_made"], t + 1)
                    after(dve, s["kacc_made"], t)
                    V.tensor_scalar(k32, ps_k[:, :], SK, 0.0, ALU.mult, ALU.max).then_inc(s["k32_made"], 1)
            keys(-4)
            lo_part(4, wg1, W_)
            keys(-3)
            lo_part(5, wg2, W_)
            keys(-2)
            pipeline(dve, keys, -1, 2, T - 4, T)
            link(V.tensor_scalar(uns[:], uns[:], float(COLS * T - 1), None, ALU.min))
            link(V.tensor_tensor(uns[:], uns[:], firsts[:], ALU.subtract))
            link(V.scalar_tensor_tensor(out=first_block[:], in0=uns[:], scalar=unsorted[:], in1=firsts[:],
                                        op0=ALU.mult, op1=ALU.add))
            link(V.tensor_scalar(first_i[:, 0:T + 1], first_block[:], U.bit_length() - 1, None,
                                 ALU.arith_shift_right))
            link(V.tensor_scalar(first_i[:, T + 1:T + 2], unsorted[:], float(T - 1), 1.0, ALU.mult, ALU.add))
            dve.sem_inc(s["firsts_made"], 1)


            dve.wait_ge(s["g_made"], T)
            for c in (2, 3):
                V.tensor_copy(gt32[:, c, :], bank[c][:, :]).then_inc(s["gt_lo_copied"], 1)
            dve.wait_ge(s["ksum_made"], 1)
            link(V.tensor_scalar(kinv[:], bank[6][:, 0:C], 1e-30, None, ALU.max))
            link(V.reciprocal(kinv[:], kinv[:]))
            link(V.tensor_scalar(kinv[:], kinv[:], 1.0 / SX, None, ALU.mult))
            link(V.tensor_tensor(mix[:, 0:1], undo[:, K_:K_ + 1], undo[:, Q_:Q_ + 1], ALU.mult))
            link(V.tensor_scalar(mix[:, 0:1], mix[:, 0:1], 1.0 / (SX * SX * SK), None, ALU.mult))
            link(V.tensor_scalar(ksb[:], bank[7][:, :], mix[:, 0:1], None, ALU.mult))
            link(V.tensor_scalar(mix[:, 1:2], undo[:, W_:W_ + 1], 1.0 / SX, None, ALU.mult))
            dve.wait_ge(s["vt_made"], 1)
            V.tensor_tensor(vtm, bank[4][:, :].rearrange("p (a f) -> p a f", a=C),
                            hmask[:, None, :].to_broadcast([P, C, P]), ALU.mult).then_inc(s["vtm_made"], 1)
            for j in range(C):
                dve.wait_ge(s["m_made"], j + 1)
                link(V.tensor_scalar(m32[:, j, :], bank[j][:, :], kinv[:, j:j + 1], None, ALU.mult))
            dve.sem_inc(s["banks_read"], 1)
            link(V.tensor_reduce(amax[:, M_:M_ + 1], m32, AX.XY, ALU.max, apply_absolute_value=True))
            dve.sem_inc(s["mmax_made"], 1)
            def split_matrix():
                dve.wait_ge(s["mgmax_made"], 1)
                powers(M_, M_ + 1)
                link(V.tensor_scalar(mix[:, 2:3], undo[:, M_:M_ + 1], 1.0 / SP_, None, ALU.mult))
                dve.sem_inc(s["mscale_made"], 1)
                dve.wait_ge(s["mhi_made"], 1)
                for c in range(C):
                    r = V.scalar_tensor_tensor(out=wm[:, 1, c, :], in0=m32[:, c, :], scalar=scale[:, M_:M_ + 1],
                                               in1=wm[:, 0, c, :], op0=ALU.mult, op1=ALU.subtract)
                link(r)
                link(V.memset(acc, 0.0))
                dve.sem_inc(s["matrix_split"], 1)

            dve.wait_ge(s["biases_added"], 1)

            def layer(i):
                t = i
                if real(t):
                    a = dve.value_load(first_i[0:1, bass.ds(t, 1)], min_val=0, max_val=GROUPS * T)
                    b = dve.value_load(first_i[0:1, bass.ds(t + 1, 1)], min_val=0, max_val=GROUPS * T)
                    V.tensor_scalar(iota_t[:], iota16[:], tile_base[:, bass.ds(t, 1)], None, ALU.add
                                    ).then_inc(s["iota_made"], 1)
                    after(dve, s["iota_made"], t + 1)
                    dve.sem_inc(s["turn"], 1)
                    with dve.Fori(a, b + 1) as q:
                        dve.wait_ge(s["oh_used"], q + t + 1)
                        V.tensor_tensor(onehot[:, bass.ds((q + t) % OG * U, U), :],
                                        iota_t[:, None, :].to_broadcast([P, U, P]),
                                        dst_col[:, bass.ds(q % GROUPS * U, U), None].to_broadcast([P, U, P]),
                                        ALU.is_equal).then_inc(s["oh_made"], 1)
                t = i - 3
                if real(t):
                    after(dve, s["x2T_hi"], t + 1)
                    V.tensor_tensor(xT[:, C:2 * C, cols(t)], ps_tx[:, :].rearrange("p (c n) -> p c n", c=C),
                                    xT[:, 0:C, cols(t)], ALU.subtract).then_inc(s["x2T_lo"], 1)
                t = i - 2
                if real(t):
                    after(dve, s["lin_made"], t + 1)
                    after(dve, s["x2_stored"], 16 * t)
                    after(dve, s["xb_made"], t + 1)
                    V.scalar_tensor_tensor(out=x2, in0=ps_o[:, :], scalar=mix[:, 1:2], in1=xb,
                                           op0=ALU.mult, op1=ALU.add).then_inc(s["xa_made"], 1)
                    after(dve, s["xa_made"], t + 1)
                    V.scalar_tensor_tensor(out=x2, in0=ps_b[:, :], scalar=mix[:, 2:3], in1=x2,
                                           op0=ALU.mult, op1=ALU.add).then_inc(s["x2_made"], 1)
                    after(dve, s["x2_made"], t + 1)
                    V.bn_stats(st6[:], x2).then_inc(s["st2_made"], 1)
                    after(dve, s["st2_made"], t + 1)
                    dve.sem_inc(s["turn"], 1)
                    V.bn_aggr(mv[:], st6[:]).then_inc(s["mv2_made"], 1)
                t = i - 1
                if real(t):
                    after(dve, s["ahT_hi"], t + 1)
                    V.tensor_tensor(ahT[:, 1], ps_ta[:, :].rearrange("p (c n) -> p c n", c=C), ahT[:, 0],
                                    ALU.subtract).then_inc(s["ahT_lo"], 1)
                    after(dve, s["pT_hi"], t + 1)
                    V.scalar_tensor_tensor(out=pT[:, 1], in0=ps_tp[:, :].rearrange("p (c n) -> p c n", c=C),
                                           scalar=SP_, in1=pT[:, 0], op0=ALU.mult, op1=ALU.subtract
                                           ).then_inc(s["pT_lo"], 1)
                t = i - 2
                if real(t):
                    after(dve, s["std2_made"], t + 1)
                    V.reciprocal(rstd[:], std[:]).then_inc(s["rs2_made"], 1)
                    after(dve, s["rs2_made"], t + 1)
                    after(dve, s["turned_x2"], t)
                    V.tensor_scalar(xn2, x2, mv[:, 0:1], rstd[:], ALU.subtract, ALU.mult).then_inc(s["xn2_made"], 1)
                    after(dve, s["xn2_made"], t + 1)
                    V.scalar_tensor_tensor(out=accs, in0=xn2, scalar=1.0 / SX, in1=awb[:], op0=ALU.mult, op1=ALU.mult,
                                           accum_out=sraw[:]).then_inc(s["sraw_made"], 1)
                    after(dve, s["sraw_made"], t + 1)
                    after(dve, s["m_kept"], t)
                    V.tensor_scalar(sm[:, 1:2], sraw[:], abb[:], None, ALU.add).then_inc(s["sc_made"], 1)
                    if isinstance(t, int) and t == T - 1:
                        dve.wait_ge(s["sc_made"], t + 1)
                        link(V.tensor_tensor(sm[:, 1:2], sm[:, 1:2], rowmask[:], ALU.mult))
                        link(V.tensor_tensor(sm[:, 1:2], sm[:, 1:2], rowlow[:], ALU.add))
                    after(dve, s["sc_made"], t + 1)
                    V.tensor_reduce(negm[:], sm[:], AX.X, ALU.max, negate=True).then_inc(s["negm_made"], 1)
                t = i
                if real(t):
                    after(dve, s["q_made"], t + 1)
                    after(dve, s["turned_p"], t)
                    V.scalar_tensor_tensor(out=w32, in0=ps_q[:, :], scalar=0.0, in1=ksb[:], op0=ALU.max,
                                           op1=ALU.mult).then_inc(s["w_made"], 1)
                    after(dve, s["w_made"], t + 1)
                    V.tensor_reduce(den[:], w32.rearrange("p (h c) -> p h c", c=HEAD), AX.X, ALU.add
                                    ).then_inc(s["den_made"], 1)
                    after(dve, s["den_made"], t + 1)
                    V.tensor_scalar(den2[:], den[:], EPS_ATT, None, ALU.add).then_inc(s["den2_made"], 1)
                    after(dve, s["den2_made"], t + 1)
                    V.reciprocal(den[:], den2[:]).then_inc(s["rec_made"], 1)
                    after(dve, s["rec_made"], t + 1)
                    w3 = w32.rearrange("p (h c) -> p h c", c=HEAD)
                    V.tensor_tensor(w3, w3, den[:, :, None].to_broadcast([P, D // HEAD, HEAD]), ALU.mult
                                    ).then_inc(s["p_made"], 1)
                t = i - 2
                if real(t):
                    after(dve, s["accs_made"], t + 1)
                    V.tensor_scalar(sm[:, 0:1], negm[:], -1.0, None, ALU.mult).then_inc(s["m_kept"], 1)
                    after(dve, s["l_made"], t)
                    V.scalar_tensor_tensor(out=lsum[:], in0=lsum[:], scalar=e2[:, 0:1], in1=e2[:, 1:2],
                                           op0=ALU.mult, op1=ALU.add).then_inc(s["l_made"], 1)
                    V.scalar_tensor_tensor(out=acc, in0=xn2, scalar=e2[:, 1:2], in1=accs,
                                           op0=ALU.mult, op1=ALU.add).then_inc(s["acc_made"], 1)
                t = i - 1
                if real(t):
                    after(dve, s["x_loaded2"], 16 * t + 16)
                    V.tensor_tensor(xb, x_in, biasb[:], ALU.add).then_inc(s["xb_made"], 1)
                if isinstance(i, int) and i == 0:
                    split_matrix()
                t = i
                if real(t):
                    after(dve, s["agg_made"], t + 1)
                    V.tensor_scalar(dg[:], ps_deg[:, 0:1], 1.0, None, ALU.max).then_inc(s["dg_made"], 1)
                    after(dve, s["dg_made"], t + 1)
                    V.reciprocal(rd[:], dg[:]).then_inc(s["rd_made"], 1)
            pipeline(dve, layer, 0, 4, T, T + 3)

            dve.wait_ge(s["best_made"], 1)
            link(V.tensor_scalar(gst[:, 1:2], gst[:, 0:1], -1.0, None, ALU.mult))
            dve.sem_inc(s["best_made"], 1)
            dve.wait_ge(s["wp_made"], 1)
            dve.wait_ge(s["l_made"], T)
            V.tensor_tensor(lw[:], lsum[:], wp[:], ALU.mult).then_inc(s["lw_made"], 1)
            dve.wait_ge(s["pooled_made"], 1)
            link(V.tensor_copy(plb, bank[0][:, 0:C, None].to_broadcast([P, C, P])))
            dve.wait_ge(s["small_loaded"], 64)
            dve.sem_inc(s["plb_made"], 1)
            link(V.reciprocal(pld[:, 0:1], bank[0][:, C:C + 1]))
            link(V.tensor_scalar(pld[:, 1:2], pld[:, 0:1], 1.0 / SX, None, ALU.mult))
            dve.wait_ge(s["logits_made"], 1)
            link(V.scalar_tensor_tensor(out=lg[:], in0=bank[1][:, 0:NE], scalar=pld[:, 1:2], in1=gbb[:],
                                        op0=ALU.mult, op1=ALU.add))
            link(V.tensor_reduce(gst[:, 2:3], lg[:], AX.X, ALU.max, negate=True))
            dve.sem_inc(s["lg_made"], 1)
            dve.wait_ge(s["gexp_made"], 1)
            link(V.tensor_reduce(gst[:, 3:4], gts[:], AX.X, ALU.add))
            link(V.reciprocal(gst[:, 4:5], gst[:, 3:4]))
            link(V.tensor_scalar(gts[:], gts[:], gst[:, 4:5], None, ALU.mult))
            link(V.max(top[:], gts[:]))
            link(V.max_index(topi[:], top[:], gts[:]))
            dve.sem_inc(s["chosen"], 1)
            link(V.tensor_tensor(gst[:, 5:6], top[:, 0:1], top[:, 1:2], ALU.add))
            link(V.tensor_scalar(gst[:, 5:6], gst[:, 5:6], EPS_GATE, None, ALU.add))
            link(V.reciprocal(gst[:, 6:7], gst[:, 5:6]))
            link(V.tensor_scalar(gexp[:], top[:, 0:2], gst[:, 6:7], None, ALU.mult))

            dve.wait_ge(s["x2_stored"], 16 * T)
            def largest_of(raw, first, rearrange, col):
                for e in range(2):
                    dve.wait_ge(e_loaded[first + e], 16)
                    link(V.tensor_reduce(pld[:, 2 + e:3 + e], raw[:, e].rearrange(rearrange), AX.X, ALU.max,
                                         apply_absolute_value=True))
                if col == W1_:
                    dve.wait_ge(s["b1_loaded"], 32)
                    link(V.tensor_reduce(amax[:, HB_:HB_ + 1], b1t[:], AX.XY, ALU.max, apply_absolute_value=True))
                link(V.tensor_tensor(amax[:, col:col + 1], pld[:, 2:3], pld[:, 3:4], ALU.max))
                dve.sem_inc(s["e_amax_made"], 1)
            flat1, flat2 = "p c h -> p (c h)", "p c o -> p (c o)"
            largest_of(w1raw, 0, flat1, W1_)
            dve.wait_ge(s["e_gmax_made"], 1)
            link(V.scalar_tensor_tensor(out=gmax[:, HB_:HB_ + 1], in0=gmax[:, W1_:W1_ + 1], scalar=float(D),
                                        in1=gmax[:, HB_:HB_ + 1], op0=ALU.mult, op1=ALU.add))
            powers(W1_, HB_ + 1)
            link(V.tensor_scalar(mix[:, 3:4], undo[:, W1_:W1_ + 1], 1.0 / SX, None, ALU.mult))
            dve.sem_inc(s["e_scales"], 1)
            for e in range(2):
                dve.wait_ge(s["w1_hi"], e + 1)
                V.scalar_tensor_tensor(out=w1s[:, 1, e].rearrange(flat1), in0=w1raw[:, e].rearrange(flat1),
                                       scalar=scale[:, W1_:W1_ + 1], in1=w1s[:, 0, e].rearrange(flat1),
                                       op0=ALU.mult, op1=ALU.subtract).then_inc(s["w1_lo"], 1)
            largest_of(w2raw, 2, flat2, W2_)
            dve.wait_ge(s["e_gmax_made"], 2)
            powers(W2_, W2_ + 1)
            link(V.tensor_tensor(mix[:, 4:5], undo[:, HB_:HB_ + 1], undo[:, W2_:W2_ + 1], ALU.mult))
            dve.sem_inc(s["e_scales"], 1)

            def hidden(g, n):
                for b in range(2 * HC):
                    e, hc = b // HC, b % HC
                    after(dve, s["h_hi"], 2 * HC * g + b + 1)
                    hh = hT[:, bass.ds(g % 2, 1)].rearrange("p b a e c n -> p (b a) e c n")
                    V.scalar_tensor_tensor(out=hh[:, 1, e, hc, 0:n], in0=g32[:, b, 0:n], scalar=scale[:, HB_:HB_ + 1],
                                           in1=hh[:, 0, e, hc, 0:n], op0=ALU.mult, op1=ALU.subtract
                                           ).then_inc(s["h_lo"], 1)

            def outs(g, tiles, hold=False, held=None):
                def add(j):
                    y = x2g[:, bass.ds(g % 2, 1), j, :].rearrange("p a f -> p (a f)")
                    if j == 0:
                        after(dve, s["x2g_loaded"], 16 * g + 16)
                    for e in range(2):
                        m = 2 * (G4 * g + j) + e
                        after(dve, s["act_made"], m + 1)
                        after(dve, s["y_half"], m)
                        r = V.scalar_tensor_tensor(out=y, in0=act2[:, j % 2, e], scalar=gexp[:, e:e + 1], in1=y,
                                                   op0=ALU.mult, op1=ALU.add)
                        r.then_inc(s["y_half"], 1)
                    after(dve, s["y_half"], m + 1)
                    dve.sem_inc(s["y_made"], 1)
                for j in range(tiles):
                    for e in range(2):
                        m = 2 * (G4 * g + j) + e
                        after(dve, s["eo_made"], m + 1)
                        after(dve, s["act_made"], m - 3)
                        V.scalar_tensor_tensor(out=pre[:, j % 2, e], in0=bank[4 + 2 * (j % 2) + e][:, :],
                                               scalar=mix[:, 4:5], in1=b2b[:, e], op0=ALU.mult, op1=ALU.add
                                               ).then_inc(s["pre_made"], 1)
                    if held and j == 0:
                        held()
                    if j:
                        add(j - 1)
                if hold:
                    return lambda: add(tiles - 1)
                add(tiles - 1)
            hidden(0, G4 * P)
            for e in range(2):
                dve.wait_ge(s["w2_hi"], e + 1)
                V.scalar_tensor_tensor(out=w2s[:, 1, e].rearrange(flat2), in0=w2raw[:, e].rearrange(flat2),
                                       scalar=scale[:, W2_:W2_ + 1], in1=w2s[:, 0, e].rearrange(flat2),
                                       op0=ALU.mult, op1=ALU.subtract).then_inc(s["w2_lo"], 1)
            dve.wait_ge(s["b2_loaded"], 32)
            hidden(1, G4 * P)
            outs(0, G4)
            with dve.Fori(2, NG) as g:
                hidden(g, G4 * P)
                outs(g - 1, G4)
            hidden(NG, P)
            last = outs(NG - 1, G4, hold=True)
            outs(NG, 1, held=last)


_INS = ['x', 'src', 'dst', 'L0_gnn_W1', 'L0_gnn_b1', 'L0_gnn_W2', 'L0_gnn_b2', 'L0_mix_qkv_weight',
        'L0_mix_proj_weight', 'L0_mix_proj_bias', 'L0_ffn_attn_w', 'L0_ffn_attn_b', 'L0_ffn_gate_w',
        'L0_ffn_gate_b', 'L0_ffn_w1', 'L0_ffn_b1', 'L0_ffn_w2', 'L0_ffn_b2']


def kernel(**inputs):
    import concourse.bacc as _bacc
    from concourse.bass_utils import run_bass_kernel_spmd as _run

    nc = _bacc.Bacc("TRN2", target_bir_lowering=False, num_devices=1)
    arrays, args = {}, []
    for name in _INS:
        a = np.ascontiguousarray(inputs[name])
        arrays[f"in_{name}"] = a
        args.append(nc.dram_tensor(f"in_{name}", a.shape, mybir.dt.from_np(a.dtype), kind="ExternalInput").ap())
    args.append(nc.dram_tensor("out_x", (N, D), F32, kind="ExternalOutput").ap())
    program(nc, *args)
    r = _run(nc, [arrays], core_ids=[0])
    return r.results[0]["out_x"]
```
